# Optimizing a Trainium2 kernel written in Bass

```python
import numpy as np
import jax
import jax.numpy as jnp

def _softmax(x, axis=-1):
    return jax.nn.softmax(x, axis=axis)

def _gelu(x):
    return jax.nn.gelu(x, approximate=True)

def _silu(x):
    return jax.nn.silu(x)

def _sigmoid(x):
    return jax.nn.sigmoid(x)

def _layernorm(x, axis=-1, eps=1e-05):
    m = jnp.mean(x, axis=axis, keepdims=True)
    v = jnp.var(x, axis=axis, keepdims=True)
    return (x - m) / jnp.sqrt(v + eps)

def _scatter_add(tgt, idx, src, axis=0):
    return tgt.at[idx].add(src)

def _segment_sum(src, seg, n):
    return jax.ops.segment_sum(src, seg, n)
kernel_name = 'mk_decoder_preln_d1_seqx_r8_fce97c'

def setup_inputs(seed: int=0):
    np.random.seed(seed)
    _w = jnp.asarray

    def _rec_inputs():
        import jax
        import jax.numpy as jnp
        _rk = jax.random.key(seed)
        x = -0.0003929 + 0.9999 * jax.random.normal(jax.random.fold_in(_rk, 1), (16, 256, 128), jnp.float32)
        _lenS = 256 - jax.random.randint(jax.random.fold_in(_rk, 7), (16,), 0, max(1, 256 // 4) + 1, jnp.int32)
        _lenS2 = 64 - jax.random.randint(jax.random.fold_in(_rk, 8), (16,), 0, max(1, 64 // 4) + 1, jnp.int32)
        _ctx_768P = jax.random.normal(jax.random.fold_in(_rk, 11), (16, 16, 96), jnp.float32)
        _ctx_768c = jax.random.dirichlet(jax.random.fold_in(_rk, 511), 0.3 * jnp.ones((16,), jnp.float32), (16, 64))
        _ctx_768t = jnp.einsum('bsk,bkd->bsd', _ctx_768c, _ctx_768P)
        _ctx_768t = _ctx_768t * jax.lax.rsqrt(jnp.mean(jnp.square(_ctx_768t)) + 1e-12) * 0.953939
        ctx_768 = -0.00055796 + 0.999787 * (_ctx_768t + 0.3 * jax.random.normal(jax.random.fold_in(_rk, 611), (16, 64, 96), jnp.float32))
        return (x, ctx_768)
    x, ctx_768 = _rec_inputs()

    def _L0_attn_setup():
        import jax, jax.numpy as jnp
        import numpy as np
        import math
        EMBED_DIM = 128
        NUM_HEADS = 16
        HEAD_DIM = EMBED_DIM // NUM_HEADS
        BLOCK_SIZE = 64
        N_GLOBAL = 8

        def _sparse_mask(seq_len: int) -> jnp.ndarray:
            idx = jnp.arange(seq_len)
            block_id = idx // BLOCK_SIZE
            local = block_id[:, None] == block_id[None, :]
            gp = np.linspace(0, seq_len - 1, min(N_GLOBAL, seq_len)).astype(np.int64)
            is_global = jnp.zeros((seq_len,), dtype=bool).at[jnp.asarray(gp)].set(True)
            return local | is_global[:, None] | is_global[None, :]
        key = jax.random.key(seed)
        ks = jax.random.split(key, 9)
        E = EMBED_DIM
        s = 0.02
        return {'x': jax.random.normal(ks[0], (1, 512, E), dtype=jnp.float32), 'Wq': jax.random.normal(ks[1], (E, E), dtype=jnp.float32) * s, 'bq': jnp.zeros((E,), dtype=jnp.float32), 'Wk': jax.random.normal(ks[2], (E, E), dtype=jnp.float32) * s, 'bk': jnp.zeros((E,), dtype=jnp.float32), 'Wv': jax.random.normal(ks[3], (E, E), dtype=jnp.float32) * s, 'bv': jnp.zeros((E,), dtype=jnp.float32), 'Wo': jax.random.normal(ks[4], (E, E), dtype=jnp.float32) * s, 'bo': jnp.zeros((E,), dtype=jnp.float32)}
    _L0_attn_all = _L0_attn_setup()
    _L0_attn_in = {k: v for k, v in _L0_attn_all.items() if k in ('Wq', 'bq', 'Wk', 'bk', 'Wv', 'bv', 'Wo', 'bo')}
    del _L0_attn_all

    def _L0_xattn_setup():
        import jax, jax.numpy as jnp
        import numpy as np
        IMAGE_DIM = 128
        TEXT_DIM = 96
        NUM_HEADS = 16
        HEAD_DIM = IMAGE_DIM // NUM_HEADS
        key = jax.random.key(seed)
        ks = jax.random.split(key, 14)
        B, N, M = (4, 512, 64)
        s_img = 1.0 / np.sqrt(IMAGE_DIM)
        s_txt = 1.0 / np.sqrt(TEXT_DIM)
        s_ff = 1.0 / np.sqrt(2 * IMAGE_DIM)
        return {'x': jax.random.normal(ks[0], (B, N, IMAGE_DIM), jnp.float32), 'y': jax.random.normal(ks[1], (B, M, TEXT_DIM), jnp.float32), 'Wq': jax.random.normal(ks[2], (IMAGE_DIM, IMAGE_DIM), jnp.float32) * s_img, 'bq': jax.random.normal(ks[3], (IMAGE_DIM,), jnp.float32) * s_img, 'Wk': jax.random.normal(ks[4], (TEXT_DIM, IMAGE_DIM), jnp.float32) * s_txt, 'bk': jax.random.normal(ks[5], (IMAGE_DIM,), jnp.float32) * s_txt, 'Wv': jax.random.normal(ks[6], (TEXT_DIM, IMAGE_DIM), jnp.float32) * s_txt, 'bv': jax.random.normal(ks[7], (IMAGE_DIM,), jnp.float32) * s_txt, 'W1': jax.random.normal(ks[8], (IMAGE_DIM, 2 * IMAGE_DIM), jnp.float32) * s_img, 'b1': jax.random.normal(ks[9], (2 * IMAGE_DIM,), jnp.float32) * s_img, 'W2': jax.random.normal(ks[10], (2 * IMAGE_DIM, IMAGE_DIM), jnp.float32) * s_ff, 'b2': jax.random.normal(ks[11], (IMAGE_DIM,), jnp.float32) * s_ff}
    _L0_xattn_all = _L0_xattn_setup()
    _L0_xattn_in = {k: v for k, v in _L0_xattn_all.items() if k in ('Wq', 'bq', 'Wk', 'bk', 'Wv', 'bv', 'W1', 'b1', 'W2', 'b2')}
    del _L0_xattn_all

    def _L0_ffn_setup():
        import jax, jax.numpy as jnp
        import numpy as np
        D_MODEL = 128
        N_EXPERTS = 16
        TOP_K = 2
        EXPERT_DIM = 128
        SHARED_DIM = 256
        B, T = (2, 128)
        key = jax.random.key(seed)
        ks = jax.random.split(key, 7)
        std = 0.02
        return {'x': jax.random.normal(ks[0], (B, T, D_MODEL), dtype=jnp.float32), 'router_w': jax.random.normal(ks[1], (N_EXPERTS, D_MODEL), dtype=jnp.float32) * std, 'gate_up_w': jax.random.normal(ks[2], (N_EXPERTS, D_MODEL, 2 * EXPERT_DIM), dtype=jnp.float32) * std, 'down_w': jax.random.normal(ks[3], (N_EXPERTS, EXPERT_DIM, D_MODEL), dtype=jnp.float32) * std, 'shared_gate_w': jax.random.normal(ks[4], (SHARED_DIM, D_MODEL), dtype=jnp.float32) * std, 'shared_up_w': jax.random.normal(ks[5], (SHARED_DIM, D_MODEL), dtype=jnp.float32) * std, 'shared_down_w': jax.random.normal(ks[6], (D_MODEL, SHARED_DIM), dtype=jnp.float32) * std}
    _L0_ffn_all = _L0_ffn_setup()
    _L0_ffn_in = {k: v for k, v in _L0_ffn_all.items() if k in ('router_w', 'gate_up_w', 'down_w', 'shared_gate_w', 'shared_up_w', 'shared_down_w')}
    del _L0_ffn_all
    return {'x': x, 'ctx_768': ctx_768, 'L0_attn_Wq': _L0_attn_in['Wq'], 'L0_attn_bq': _L0_attn_in['bq'], 'L0_attn_Wk': _L0_attn_in['Wk'], 'L0_attn_bk': _L0_attn_in['bk'], 'L0_attn_Wv': _L0_attn_in['Wv'], 'L0_attn_bv': _L0_attn_in['bv'], 'L0_attn_Wo': _L0_attn_in['Wo'], 'L0_attn_bo': _L0_attn_in['bo'], 'L0_xattn_Wq': _L0_xattn_in['Wq'], 'L0_xattn_bq': _L0_xattn_in['bq'], 'L0_xattn_Wk': _L0_xattn_in['Wk'], 'L0_xattn_bk': _L0_xattn_in['bk'], 'L0_xattn_Wv': _L0_xattn_in['Wv'], 'L0_xattn_bv': _L0_xattn_in['bv'], 'L0_xattn_W1': _L0_xattn_in['W1'], 'L0_xattn_b1': _L0_xattn_in['b1'], 'L0_xattn_W2': _L0_xattn_in['W2'], 'L0_xattn_b2': _L0_xattn_in['b2'], 'L0_ffn_router_w': _L0_ffn_in['router_w'], 'L0_ffn_gate_up_w': _L0_ffn_in['gate_up_w'], 'L0_ffn_down_w': _L0_ffn_in['down_w'], 'L0_ffn_shared_gate_w': _L0_ffn_in['shared_gate_w'], 'L0_ffn_shared_up_w': _L0_ffn_in['shared_up_w'], 'L0_ffn_shared_down_w': _L0_ffn_in['shared_down_w']}

def reference(x, ctx_768, L0_attn_Wq, L0_attn_bq, L0_attn_Wk, L0_attn_bk, L0_attn_Wv, L0_attn_bv, L0_attn_Wo, L0_attn_bo, L0_xattn_Wq, L0_xattn_bq, L0_xattn_Wk, L0_xattn_bk, L0_xattn_Wv, L0_xattn_bv, L0_xattn_W1, L0_xattn_b1, L0_xattn_W2, L0_xattn_b2, L0_ffn_router_w, L0_ffn_gate_up_w, L0_ffn_down_w, L0_ffn_shared_gate_w, L0_ffn_shared_up_w, L0_ffn_shared_down_w):
    import jax
    import jax.numpy as jnp

    def _L0_attn_ref(x, Wq, bq, Wk, bk, Wv, bv, Wo, bo):
        import jax, jax.numpy as jnp
        import numpy as np
        import math
        EMBED_DIM = 128
        NUM_HEADS = 16
        HEAD_DIM = EMBED_DIM // NUM_HEADS
        BLOCK_SIZE = 64
        N_GLOBAL = 8

        def _sparse_mask(seq_len: int) -> jnp.ndarray:
            idx = jnp.arange(seq_len)
            block_id = idx // BLOCK_SIZE
            local = block_id[:, None] == block_id[None, :]
            gp = np.linspace(0, seq_len - 1, min(N_GLOBAL, seq_len)).astype(np.int64)
            is_global = jnp.zeros((seq_len,), dtype=bool).at[jnp.asarray(gp)].set(True)
            return local | is_global[:, None] | is_global[None, :]
        B, S, E = x.shape
        H, D = (NUM_HEADS, HEAD_DIM)
        mask = _sparse_mask(S)

        def split_heads(y):
            return y.reshape(B, S, H, D).transpose(0, 2, 1, 3)
        q = split_heads(x @ Wq + bq)
        k = split_heads(x @ Wk + bk)
        v = split_heads(x @ Wv + bv)
        scale = math.sqrt(D)
        scores = jnp.einsum('bhqd,bhkd->bhqk', q, k) / scale
        scores = jnp.where(mask[None, None], scores, -jnp.inf)
        attn = jax.nn.softmax(scores, axis=-1)
        out = jnp.einsum('bhqk,bhkd->bhqd', attn, v)
        out = out.transpose(0, 2, 1, 3).reshape(B, S, E)
        return out @ Wo + bo

    def _L0_xattn_ref(x, y, Wq, bq, Wk, bk, Wv, bv, W1, b1, W2, b2):
        import jax, jax.numpy as jnp
        import numpy as np
        IMAGE_DIM = 128
        TEXT_DIM = 96
        NUM_HEADS = 16
        HEAD_DIM = IMAGE_DIM // NUM_HEADS
        B, N, _ = x.shape
        M = y.shape[1]
        q = (x @ Wq + bq).reshape(B, N, NUM_HEADS, HEAD_DIM)
        k = (y @ Wk + bk).reshape(B, M, NUM_HEADS, HEAD_DIM)
        v = (y @ Wv + bv).reshape(B, M, NUM_HEADS, HEAD_DIM)
        scale = 1.0 / np.sqrt(HEAD_DIM)
        scores = jnp.einsum('bnhd,bmhd->bhnm', q, k) * scale
        attn = jax.nn.softmax(scores, axis=-1)
        out = jnp.einsum('bhnm,bmhd->bnhd', attn, v).reshape(B, N, IMAGE_DIM)
        h = jax.nn.relu(out @ W1 + b1)
        return h @ W2 + b2

    def _L0_ffn_ref(x, router_w, gate_up_w, down_w, shared_gate_w, shared_up_w, shared_down_w):
        import jax, jax.numpy as jnp
        import numpy as np
        D_MODEL = 128
        N_EXPERTS = 16
        TOP_K = 2
        EXPERT_DIM = 128
        SHARED_DIM = 256
        B, T = (2, 128)
        Bb, Tt, C = x.shape
        N = Bb * Tt
        E = gate_up_w.shape[0]
        logits = jnp.einsum('btc,ec->bte', x, router_w)
        top_vals, top_idx = jax.lax.top_k(logits, TOP_K)
        gates = jax.nn.sigmoid(top_vals)
        xf = x.reshape(N, C)
        sel = top_idx.reshape(N, TOP_K)
        gw = gates.reshape(N, TOP_K)
        w_full = jnp.zeros((N, E), dtype=x.dtype).at[jnp.arange(N)[:, None], sel].add(gw)
        gu = jnp.einsum('nc,ech->neh', xf, gate_up_w)
        gate, up = jnp.split(gu, 2, axis=-1)
        h = jax.nn.silu(gate) * up
        out_all = jnp.einsum('neh,ehc->nec', h, down_w)
        moe = jnp.einsum('ne,nec->nc', w_full, out_all).reshape(Bb, Tt, C)
        sg = jnp.einsum('btc,sc->bts', x, shared_gate_w)
        su = jnp.einsum('btc,sc->bts', x, shared_up_w)
        shared = jnp.einsum('bts,cs->btc', jax.nn.silu(sg) * su, shared_down_w)
        return moe + shared
    x = x + _L0_attn_ref(_layernorm(x, axis=-1), L0_attn_Wq, L0_attn_bq, L0_attn_Wk, L0_attn_bk, L0_attn_Wv, L0_attn_bv, L0_attn_Wo, L0_attn_bo)
    x = x + _L0_xattn_ref(_layernorm(x, axis=-1), ctx_768, L0_xattn_Wq, L0_xattn_bq, L0_xattn_Wk, L0_xattn_bk, L0_xattn_Wv, L0_xattn_bv, L0_xattn_W1, L0_xattn_b1, L0_xattn_W2, L0_xattn_b2)
    x = x + _L0_ffn_ref(_layernorm(x, axis=-1), L0_ffn_router_w, L0_ffn_gate_up_w, L0_ffn_down_w, L0_ffn_shared_gate_w, L0_ffn_shared_up_w, L0_ffn_shared_down_w)
    return x

_drawn_inputs = setup_inputs


def setup_inputs(seed=0):
    import zlib

    import numpy as np

    out = dict(_drawn_inputs(seed))
    spreads = {'L0_attn_bq': (0.0, 0.8),
     'L0_attn_bk': (0.0, 0.8),
     'L0_attn_bv': (0.0, 0.404),
     'L0_attn_bo': (0.0, 0.1)}
    factors = {'L0_attn_Wq': 8.0,
     'L0_attn_Wk': 8.0,
     'L0_attn_Wv': 8.0,
     'L0_attn_Wo': 3.001,
     'L0_xattn_bq': 3.824,
     'L0_xattn_bk': 8.0,
     'L0_ffn_router_w': 8.0,
     'L0_ffn_gate_up_w': 8.0,
     'L0_ffn_down_w': 8.0,
     'L0_ffn_shared_gate_w': 7.387,
     'L0_ffn_shared_up_w': 7.381,
     'L0_ffn_shared_down_w': 7.344}
    for name, (base, spread) in spreads.items():
        noise = np.random.default_rng([zlib.crc32(name.encode()), seed]).standard_normal(out[name].shape)
        drawn = base * np.exp(spread * noise) if base else spread * noise
        out[name] = jnp.asarray(drawn.astype(out[name].dtype))
    for name, factor in factors.items():
        out[name] = (out[name] * factor).astype(out[name].dtype)
    return out
```

```python
import numpy as np
import concourse.bass as bass
from concourse import mybir
from contextlib import ExitStack

F32 = mybir.dt.float32
BF16 = mybir.dt.bfloat16
I32 = mybir.dt.int32
U32 = mybir.dt.uint32
ACT = mybir.ActivationFunctionType
ALU = mybir.AluOpType
AX = mybir.AxisListType

B, S, E = 16, 256, 128
M, EC = 64, 96
H, D = 16, 8
BLOCK, NGLOB = 64, 8
NB = S // BLOCK
PAIRS = H // 2
NT = B * S // 128
NE, TOPK, ED, SD = 16, 2, 128, 256
CAP = B * S + 128
TILES = B * S * TOPK // 128 + NE
EPS = 1e-5
SCALE = 1.0 / float(np.sqrt(D))
GLOBALS = [int(g) for g in np.linspace(0, S - 1, NGLOB)]
RUNS = [(GLOBALS[0], 1, 1, 0), (GLOBALS[1], GLOBALS[3] - GLOBALS[1], 4, 1), (GLOBALS[2], GLOBALS[4] - GLOBALS[2], 3, 5)]
G_ORDER = [a + s * i for a, s, c, _ in RUNS for i in range(c)]
assert sorted(G_ORDER) == GLOBALS
Q_PART = (0, 0, 0, 1, 1, 2)
K_PART = (0, 1, 2, 0, 1, 0)
NP = len(Q_PART)
KROWS = 2 * NP * D
SHIFT = KROWS


def shape_constants():
    p = np.arange(128)
    c = {}
    c["ident"] = np.eye(128, dtype=np.float32)
    c["same_head"] = (p[:, None] // D == p[None, :] // D).astype(np.float32)
    c["outside"] = (np.array(G_ORDER)[p % NGLOB][:, None] // BLOCK != np.arange(NB)[None, :]).astype(np.float32)
    c["head_of_pair"] = ((p // D % 2)[:, None] == np.arange(2)[None, :]).astype(np.float32)
    r = np.arange(32) % H
    c["shift_pair"] = (r[:, None] == np.arange(H)[None, :]).astype(np.float32)
    c["shift_glob"] = (r[:, None] == p[None, :] // D).astype(np.float32)
    e = np.arange(NE, dtype=np.float32)
    c["experts"] = np.concatenate([np.tile(e, (128, 1)), np.tile(e * CAP, (128, 1)), p[:, None].astype(np.float32)], axis=1)
    c["ahead"] = np.concatenate([(p[:, None] < p[None, :]), np.ones((128, 128))], axis=1).astype(np.float32)
    o = np.zeros((128, 2, 2, 2, D), np.float32)
    for jj in range(2):
        for a in range(2):
            o[a * 64:(a + 1) * 64, jj, jj, a] = 1.0
    c["key_ones"] = o.reshape(128, 64)
    return c


def at_least(eng, sem, value):
    if not isinstance(value, int) or value > 0:
        eng.wait_ge(sem, value)


def decoder(nc, t, out, phases="ABC"):
    ctx = ExitStack()
    with ctx:
        def sb(name, shape, dt=F32):
            return ctx.enter_context(nc.sbuf_tensor(name, shape, dt))

        class Sems:
            def __init__(self, prefix):
                self.prefix, self.made = prefix, {}

            def __call__(self, name):
                if name not in self.made:
                    self.made[name] = ctx.enter_context(nc.semaphore(self.prefix + name))
                return self.made[name]

        w_ = Sems("w_")
        s_ = Sems("self_")
        c_ = Sems("cross_")
        r_ = Sems("route_")
        e_ = Sems("expert_")
        h_ = Sems("shared_")
        g_ = Sems("gather_")

        X = sb("x_rows", [128, NT, E])
        ident = sb("ident", [128, 128])
        identb = sb("identb", [128, 128], BF16)
        same_head = sb("same_head", [128, 128])
        outside = sb("outside", [128, NB])
        sel_f = sb("sel_f", [128, H + 128])
        shift_glob = sb("shift_glob", [128, 128], BF16)
        key_ones = sb("key_ones", [128, 2, 32])
        of_pair = sb("of_pair", [128, 2])
        kbias = sb("kbias", [128, 2, 2])
        minus_half = sb("minus_half", [128, 2])
        wq, wk, wv, wo = (sb(n, [E, E]) for n in ("wq", "wk", "wv", "wo"))
        cwq = sb("cwq", [E, E])
        cwk, cwv = sb("cwk", [EC, E]), sb("cwv", [EC, E])
        cw1, cw2 = sb("cw1", [E, 2 * E]), sb("cw2", [128, 2, E])
        cols = sb("cols", [128, 8])
        rows = sb("rows", [128, 2, E])
        cb1_ = sb("cb1_", [128, 2])
        bo_ = sb("bo_", [128, E])
        ctx_rows = sb("ctx_rows", [128, B * M // 128, EC])
        ctxT = sb("ctxT", [EC, B * M])
        x3T = sb("x3T", [128, B * S])
        wgu = sb("wgu", [E, NE, 2 * ED])
        ck32 = x3T[:, 0:2 * B * M].rearrange("p (b a k) -> p b a k", a=2, k=M)
        ckres = x3T[:, 2 * B * M:4 * B * M].rearrange("p (b a k) -> p b a k", a=2, k=M)
        ckpart = wgu[:, 0:12, :].rearrange("p e h -> p (e h)").bitcast(BF16).rearrange("p (i b a k) -> p i b a k", i=3, a=2, k=M)
        cvbd_all = sb("cvbd_all", [128, B, PAIRS, 32])

        st = sb("st", [128, 2, 6])
        mv = sb("mv", [128, 2, 2])
        veps = sb("veps", [128, 2])
        rstd = sb("rstd", [128, 2])
        xn = sb("xn", [128, 2, E])
        xnT = sb("xnT", [128, S])
        xg = sb("xg", [128, H, NGLOB])
        qkz = [sb(f"qkz{i}", [128, 3 * S]) for i in range(2)]
        k32 = [sb(f"k32_{i}", [128, S]) for i in range(2)]
        res = sb("res", [128, 3 * S])
        part = sb("part", [128, 3, 3 * S], BF16)
        qs = [sb(f"qs{i}", [128, PAIRS, S], BF16) for i in range(2)]
        kbd = [sb(f"kbd{i}", [128, PAIRS, NB, 2, BLOCK], BF16) for i in range(2)]
        vbd = [sb(f"vbd{i}", [128, NB, PAIRS, 32]) for i in range(2)]
        vtok = [sb(f"vtok{i}", [128, 2, E]) for i in range(2)]
        vg = [sb(f"vg{i}", [128, E]) for i in range(2)]
        kg = [sb(f"kg{i}", [128, H, NGLOB]) for i in range(2)]
        qg = [sb(f"qg{i}", [128, H, NGLOB]) for i in range(2)]
        nmax = sb("nmax", [128, 2, H])
        nmaxg = sb("nmaxg", [128, 2, H])
        mparts = sb("mparts", [128, 2, 2, H], BF16)
        probs = sb("probs", [128, PAIRS, S])
        probs_g = sb("probs_g", [128, S])
        pgq = sb("pgq", [128, S])
        pgqT = sb("pgqT", [128, 2, 128])
        gstat = sb("gstat", [128, 4])
        gtmp = sb("gtmp", [128, H, NGLOB])
        rden = sb("rden", [128, S])
        attT = sb("attT", [128, S])
        ckbd = [sb(f"ckbd{i}", [128, PAIRS, 2, M], BF16) for i in range(2)]
        cvbd = [sb(f"cvbd{i}", [128, PAIRS, 32]) for i in range(2)]
        hT = sb("hT", [128, 2, S])

        experts = sb("experts", [128, 2 * NE + 1])
        ahead = sb("ahead", [128, 256])
        aheadb = sb("aheadb", [128, 256], BF16)
        rw_rows = sb("rw_rows", [NE, E])
        rwT = sb("rwT", [E, NE])
        sh_rows = sb("sh_rows", [128, 6, 128])
        shT = sb("shT", [128, 6, 128])
        wd = kbd[0][:, :, :, :, :].rearrange("p j n a k -> p (j n a k)").bitcast(F32).rearrange("p (e c) -> p e c", c=E)
        zero_rows = sb("zero_rows", [128, E])
        xn3 = [sb(f"xn3_{i}", [128, 2, E]) for i in range(2)]
        x3s = sb("x3s", [128, S])
        logits = sb("logits", [128, 2, NE])
        top8 = sb("top8", [128, 2, 8])
        topi = sb("topi", [128, 2, 8], U32)
        topf = sb("topf", [128, 2, TOPK])
        onehot = sb("onehot", [128, NT, TOPK, NE])
        topv = sb("topv", [128, NT, TOPK])
        both = sb("both", [128, 2, NE], BF16)
        rowpos = sb("rowpos", [128, 2, NE])
        picked = sb("picked", [128, 2, TOPK, NE])
        slotf = sb("slotf", [128, NT, TOPK])
        sloti = [sb(f"sloti{i}", [128, 2 * TOPK], I32) for i in range(2)]
        used = [sb(f"used{i}", [128, NE]) for i in range(2)]
        plan = sb("plan", [128, 8, NE])
        plani = sb("plani", [128, 2, NE], I32)
        tile_of = sb("tile_of", [128, 4])
        tails = sb("tails", [1, NE], I32)
        tile_row = sb("tile_row", [1, 2, 128], I32)
        back = sb("back", [128, NT * TOPK])
        backi = sb("backi", [128, NT * TOPK], I32)
        picked_all = sb("picked_all", [128, NT * TOPK, NE])
        gate = sb("gate", [128, NT * TOPK])
        xt = [sb(f"xt{i}", [128, E]) for i in range(2)]
        xtT = [sb(f"xtT{i}", [E, 128]) for i in range(2)]
        sg = [sb(f"sg{i}", [128, ED]) for i in range(2)]
        eh = [sb(f"eh{i}", [128, ED]) for i in range(2)]
        ehT = [sb(f"ehT{i}", [ED, 128]) for i in range(2)]
        ey = [sb(f"ey{i}", [128, E]) for i in range(2)]
        sgs = probs[:, 0:4, :].rearrange("p (c i) n -> p c (i n)", c=2)
        shs = probs[:, 4:8, :].rearrange("p (c i) n -> p c (i n)", c=2)
        idx = [sb(f"idx{i}", [128, 4], I32) for i in range(2)]
        yrow = [sb(f"yrow{i}", [128, 4, E]) for i in range(2)]

        PS = [ctx.enter_context(nc.psum_tensor(f"ps{i}", [128, 512], F32)) for i in range(8)]
        A0, A1, MISC = PS[0], PS[1], PS[7]
        P1, P2, OD = PS[2:4], PS[4:6], PS[6]

        q_scr = nc.dram_tensor("q_scr", (2, B, NP, 2 * D, PAIRS, S), BF16, kind="Internal").ap()
        k_scr = nc.dram_tensor("k_scr", (B, NP, 2 * D, PAIRS, 2 * S), BF16, kind="Internal").ap()
        ck_scr = nc.dram_tensor("ck_scr", (NP, 2 * D, PAIRS, 2 * B * M), BF16, kind="Internal").ap()

        xs = nc.dram_tensor("expert_in", (NE * CAP + 128, E), F32, kind="Internal").ap()
        ys = nc.dram_tensor("expert_out", (TILES * 128, E), F32, kind="Internal").ap()

        def loop2(eng, body, n):
            for k in (0, 1):
                body(k, 0, k)
            with eng.Fori(1, n // 2 - 1) as i:
                for k in (0, 1):
                    body(2 * i + k, i, k)
            for k in (0, 1):
                body(n - 2 + k, n // 2 - 1, k)

        def skewed(eng, stages, n):
            most = max(lag for _, lag in stages)
            lead = 2 * ((most + 3) // 2)

            def at(k, i, q, from_, to):
                for f, lag in stages:
                    if from_ is None or from_ <= k - lag < to:
                        f(k - lag, i - (lag + 1 - q) // 2 if lag else i, (q - lag) % 2)

            for k in range(lead):
                at(k, k // 2, k % 2, 0, n)
            with eng.Fori(lead // 2, n // 2) as i:
                for q in (0, 1):
                    at(2 * i + q, i, q, None, None)
            for k in range(n, n + most):
                at(k, k // 2, k % 2, 0, n)

        def loop(eng, body):
            body(0, 0, True)
            body(1, 1, True)
            with eng.Fori(1, B // 2 - 1) as i:
                body(2 * i, 0, True)
                body(2 * i + 1, 1, True)
            body(B - 2, 0, True)
            body(B - 1, 1, False)

        def wait_apart(eng, *waits):
            held = [(sem, v if isinstance(v, int) else eng.to_reg(v)) for sem, v in waits]
            eng.wait_ge(w_("set"), 1)
            for sem, v in held:
                at_least(eng, sem, v)

        block = ctx.enter_context(nc.Block())

        @block.sync
        def _(sp):
            def load(dst, src, sem="weights"):
                sp.dma_start(dst, src).then_inc(w_(sem), 16)

            xv = t["x"].rearrange("b (u p) c -> p (b u) c", p=128)
            load(X[:, 0:2, :], xv[:, 0:2, :], "x_first")
            load(ident[:, :], t["ident"])
            load(same_head[:, :], t["same_head"])
            load(outside[:, :], t["outside"])
            load(of_pair[:, :], t["head_of_pair"])
            load(sel_f[SHIFT:128, 0:H], t["shift_pair"])
            load(sel_f[SHIFT:128, H:H + 128], t["shift_glob"])
            load(key_ones[:, :, :], t["key_ones"].rearrange("p (j c) -> p j c", j=2))
            for dst, name in ((wq, "L0_attn_Wq"), (wk, "L0_attn_Wk"), (wv, "L0_attn_Wv"), (wo, "L0_attn_Wo"),
                              (cwq, "L0_xattn_Wq"), (cwk, "L0_xattn_Wk"), (cwv, "L0_xattn_Wv"), (cw1, "L0_xattn_W1")):
                load(dst[:, :], t[name])
            load(cw2[:, :, :], t["L0_xattn_W2"].rearrange("(c p) n -> p c n", p=128))
            for i, name in enumerate(("L0_attn_bq", "L0_attn_bk", "L0_attn_bv", "L0_xattn_bq", "L0_xattn_bk", "L0_xattn_bv")):
                load(cols[:, i:i + 1], t[name].rearrange("(p o) -> p o", o=1))
            for i in range(2):
                load(cols[:, 6 + i:7 + i], t["L0_xattn_b1"][i * 128:(i + 1) * 128].rearrange("(p o) -> p o", o=1))
            load(rows[:, 0, :], t["L0_attn_bo"].rearrange("(o n) -> o n", o=1).to_broadcast([128, E]))
            load(rows[:, 1, :], t["L0_xattn_b2"].rearrange("(o n) -> o n", o=1).to_broadcast([128, E]))
            load(experts[:, :], t["experts"])
            load(ahead[:, :], t["ahead"])
            load(rw_rows[:, :], t["L0_ffn_router_w"])
            for i, name in enumerate(("gate", "up")):
                load(sh_rows[:, 2 * i:2 * i + 2, :], t[f"L0_ffn_shared_{name}_w"].rearrange("(k p) c -> p k c", p=128))
            load(sh_rows[:, 4:6, :], t["L0_ffn_shared_down_w"].rearrange("p (k s) -> p k s", k=2))
            load(ctx_rows[:, :, :], t["ctx_768"].rearrange("b m c -> (b m) c").rearrange("(u p) c -> p u c", p=128))
            load(X[:, 2:NT, :], xv[:, 2:NT, :], "x_rest")

            sp.wait_ge(w_("ckpart"), 3)
            for i, k in enumerate(K_PART):
                sp.dma_start(ck_scr[i].rearrange("r j n -> j r n"), ckpart[:, k].rearrange("p b a k -> p (b a k)")).then_inc(w_("ck_put"), 16)
            sp.wait_ge(w_("ck_put"), 16 * NP)
            load(wgu[:, :, :], t["L0_ffn_gate_up_w"].rearrange("e c h -> c e h"), "experts")

            def regroup(s, layer, b, p, keys):
                sp.wait_ge(s("part"), 3 * b + 3)
                for i in range(NP):
                    sp.dma_start(q_scr[layer, bass.ds(b, 1), i].rearrange("o r j n -> (o j) r n"),
                                 part[:, Q_PART[i], 0:S]).then_inc(s("put"), 16)
                    if keys:
                        sp.dma_start(k_scr[bass.ds(b, 1), i].rearrange("o r j n -> (o j) r n"),
                                     part[:, K_PART[i], S:3 * S]).then_inc(s("put"), 16)
                n_put = 16 * NP * (2 if keys else 1)
                sp.wait_ge(s("put"), n_put * b + n_put)
                sp.dma_start(qs[p][0:KROWS, :, :].rearrange("r j n -> r (j n)"),
                             q_scr[layer, bass.ds(b, 1)].rearrange("o i r j n -> (o i r) (j n)")).then_inc(s("got"), 16)
                if keys:
                    sp.dma_start(kbd[p][0:KROWS].rearrange("r j n a k -> r (j n a k)"),
                                 k_scr[bass.ds(b, 1)].rearrange("o i r j n -> (o i r) (j n)")).then_inc(s("got"), 16)
                else:
                    sp.dma_start(ckbd[p][0:KROWS, :, :, :].rearrange("r j a k -> r j (a k)"),
                                 ck_scr[:, :, :, bass.ds(2 * M * b, 2 * M)].rearrange("i r j n -> (i r) j n")).then_inc(s("got"), 16)
                    sp.dma_start(cvbd[p][:, :, :], cvbd_all[:, bass.ds(b, 1), :, :].squeeze(1)).then_inc(s("got"), 16)
                n_got = 16 * (2 if keys else 3)
                wait_apart(sp, (s("got"), n_got * b + n_got))

            regroup(s_, 0, 0, 0, True)
            loop(sp, lambda b, p, more: more and regroup(s_, 0, b + 1, 1 - p, True))
            if "B" in phases:
                sp.wait_ge(s_("x_new"), B)
                sp.wait_ge(w_("cv"), 8)
                load(wd, t["L0_ffn_down_w"].rearrange("e c h -> c e h"), "experts")
                regroup(c_, 1, 0, 0, False)
                loop(sp, lambda b, p, more: more and regroup(c_, 1, b + 1, 1 - p, False))
            ov = out.rearrange("b (u p) c -> p (b u) c", p=128)
            if "C" not in phases:
                sp.wait_ge((c_ if "B" in phases else s_)("x_new"), B)
                sp.dma_start(ov, X[:, :, :]).then_inc(w_("stored"), 16)
                sp.wait_ge(w_("stored"), 16)
                return

            sp.wait_ge(r_("tails"), 1)
            sp.wait_ge(r_("sent"), 64 * B)
            sp.dma_start(xs[NE * CAP:NE * CAP + 128, :], zero_rows[:, :]).then_inc(e_("zeros"), 16)
            with sp.Fori(0, NE) as i:
                end = sp.value_load(tails[0:1, bass.ds(i, 1)], min_val=0, max_val=NE * CAP - 128)
                sp.dma_start(xs[bass.ds(end, 128), :], zero_rows[:, :]).then_inc(e_("zeros"), 16)
            sp.wait_ge(e_("zeros"), 16 * (NE + 1))
            sp.wait_ge(e_("tile_row"), 1)

            def tile_in(k, i, p):
                at_least(sp, e_("xT_ps"), k - 1)
                first = sp.value_load(tile_row[0:1, 0, bass.ds(k, 1)], min_val=0, max_val=NE * CAP)
                sp.dma_start(xt[p][:, :], xs[bass.ds(first, 128), :]).then_inc(e_(f"in{p}"), 16)

            loop2(sp, tile_in, TILES)

            def store(b, i, p):
                sp.wait_ge(g_("x_out"), b + 1)
                sp.dma_start(ov[:, bass.ds(2 * b, 2), :], X[:, bass.ds(2 * b, 2), :]).then_inc(w_("stored"), 16)

            loop2(sp, store, B)
            sp.wait_ge(w_("stored"), 16 * B)

        @block.gpsimd
        def _(pool):
            g = nc.gpsimd
            g.memset(minus_half[:, :], -0.5)
            for p in range(2):
                g.memset(vbd[p][:, :, :, :], 0.0)
            g.memset(cvbd_all[:, :, :, :], 0.0).then_inc(w_("zeroed"), 1)
            pool.wait_ge(w_("zeroed"), 1)
            pool.wait_ge(w_("weights"), 16 * W_LOADS)
            for i in range(2):
                g.tensor_scalar(kbias[:, i, :], of_pair[:, :], cols[:, 1 + 3 * i:2 + 3 * i], None, ALU.mult).then_inc(w_("kbias"), 1)
            g.tensor_copy(identb[:, :], ident[:, :]).then_inc(w_("kbias"), 1)
            pool.wait_ge(w_("kbias"), 3)
            sel = sel_f[SHIFT:128, 0:H].rearrange("p (j a) -> p j a", a=2).unsqueeze(3)
            for p in range(2):
                for n in range(NB):
                    g.tensor_copy(kbd[p][SHIFT:128, :, n, :, :], sel.to_broadcast([32, PAIRS, 2, BLOCK]))
                g.tensor_copy(ckbd[p][SHIFT:128, :, :, :], sel.to_broadcast([32, PAIRS, 2, M]))
            g.tensor_copy(shift_glob[SHIFT:128, :], sel_f[SHIFT:128, H:H + 128]).then_inc(w_("set"), 1)
            pool.wait_ge(w_("set"), 1)

            g.tensor_copy(aheadb[:, :], ahead[:, :]).then_inc(w_("set"), 1)
            g.memset(zero_rows[:, :], 0.0).then_inc(w_("set"), 1)
            g.tensor_copy(used[0][:, :], experts[:, NE:2 * NE]).then_inc(w_("set"), 1)

            def rstd_of(s, b):
                wait_apart(pool, (s("aggr"), 2 * b + 2), (s("norm"), 2 * b))
                g.tensor_scalar(veps[:, :], mv[:, :, 1], EPS, None, ALU.add).then_inc(s("veps"), 1)
                pool.wait_ge(s("veps"), b + 1)
                g.tensor_tensor(rstd[:, :], veps[:, :], minus_half[:, :], ALU.pow).then_inc(s("rstd"), 1)

            def add_bias(s, b, bias, ready):
                pool.wait_ge(s("norm"), 2 * b + 2)
                g.tensor_tensor(X[:, bass.ds(2 * b, 2), :], X[:, bass.ds(2 * b, 2), :],
                                bias.unsqueeze(1).to_broadcast([128, 2, E]), ALU.add).then_inc(s("x_biased"), 1)

            def self_start(b, p):
                rstd_of(s_, b)
                wait_apart(pool, (s_("xnT"), b + 1), (s_("vtok_ps"), b))
                for first, step, n, to in RUNS:
                    last = g.tensor_copy(xg[:, :, to:to + n],
                                         xnT[:, first:first + step * (n - 1) + 1:step].unsqueeze(1).to_broadcast([128, H, n]))
                last.then_inc(s_("xg"), 1)
                add_bias(s_, b, bo_[:, :], None)
                pool.wait_ge(s_("qk32"), 4 * b + 4)
                for dst, of in ((kg, k32), (qg, qkz)):
                    for first, step, n, to in RUNS:
                        src = of[p][:, first:first + step * (n - 1) + 1:step]
                        last = g.tensor_tensor(dst[p][:, :, to:to + n], src.unsqueeze(1).to_broadcast([128, H, n]),
                                               same_head[:, ::D].unsqueeze(2).to_broadcast([128, H, n]), ALU.mult)
                    last.then_inc(s_("kgqg"), 1)

            def self_attend(b, p):
                pool.wait_ge(s_("gexp"), b + 1)
                v = probs_g[:, :].rearrange("p (n q) -> p n q", n=NB)
                g.tensor_tensor(v, v, outside[:, :].unsqueeze(2).to_broadcast([128, NB, BLOCK]), ALU.mult).then_inc(s_("gmasked"), 1)
                wait_apart(pool, (s_("gq_rcp"), b + 1))
                g.tensor_scalar(pgq[:, :], pgq[:, :], gstat[:, 3:4], None, ALU.mult).then_inc(s_("gq_norm"), 1)

            pool.wait_ge(w_("bo_"), 1)
            self_start(0, 0)
            def body(b, p, more):
                if more:
                    self_start(b + 1, 1 - p)
                self_attend(b, p)
            loop(pool, body)

            if "B" in phases:
                def cross_start(b, p):
                    rstd_of(c_, b)
                    add_bias(c_, b, rows[:, 1, :], None)

                cross_start(0, 0)
                loop(pool, lambda b, p, more: more and cross_start(b + 1, 1 - p))

            if "C" in phases:
                def route(b, i, p):
                    rstd_of(r_, b)
                    wait_apart(pool, (r_("slot"), b + 1), (r_("sent"), 64 * b))
                    for u in range(2):
                        for k in range(TOPK):
                            pool.indirect_dma_start(xs, bass.IndirectOffsetOnAxis(sloti[p][:, 2 * u + k:2 * u + k + 1], 0),
                                                    xn3[p][:, u, :], None).then_inc(r_("sent"), 16)

                loop2(pool, route, B)

                pool.wait_ge(g_("backi"), 1)
                for q in range(2):
                    pool.wait_ge(e_(f"out{q}"), 16 * (TILES // 2))

                def gather(b, i, p):
                    wait_apart(pool, (g_("x_out"), b - 1))
                    g.tensor_copy(idx[p][:, :], backi[:, bass.ds(4 * b, 4)]).then_inc(g_("idx"), 1)
                    wait_apart(pool, (g_("idx"), b + 1))
                    for k in range(4):
                        pool.indirect_dma_start(yrow[p][:, k, :], None, ys,
                                                bass.IndirectOffsetOnAxis(idx[p][:, k:k + 1], 0)).then_inc(g_(f"got{p}"), 16)

                loop2(pool, gather, B)

        @block.vector
        def _(dve):
            v = nc.vector
            dve.wait_ge(w_("bias_ps"), 1)
            v.tensor_tensor(bo_[:, :], MISC[:, 0:E], rows[:, 0, :], ALU.add).then_inc(w_("bo_"), 1)
            v.tensor_tensor(cb1_[:, :], MISC[:, E:E + 2], cols[:, 6:8], ALU.add).then_inc(w_("bo_"), 1)
            dve.wait_ge(w_("ck32"), 4)
            v.tensor_copy(ckpart[:, 0], ck32).then_inc(w_("ckpart"), 1)
            dve.wait_ge(w_("ckpart"), 1)
            v.tensor_tensor(ckres, ck32, ckpart[:, 0], ALU.subtract).then_inc(w_("ckres"), 1)
            dve.wait_ge(w_("ckres"), 1)
            v.tensor_copy(ckpart[:, 1], ckres).then_inc(w_("ckpart"), 1)
            dve.wait_ge(w_("ckpart"), 2)
            v.tensor_tensor(ckpart[:, 2], ckres, ckpart[:, 1], ALU.subtract).then_inc(w_("ckpart"), 1)

            def stats(s, b, arrived):
                arrived(b)
                for u in range(2):
                    v.bn_stats(st[:, u, :], X[:, bass.ds(2 * b + u, 1), :].squeeze(1)).then_inc(s("stats"), 1)
                for u in range(2):
                    wait_apart(dve, (s("stats"), 2 * b + u + 1), (s("veps"), b))
                    v.bn_aggr(mv[:, u, :], st[:, u, :]).then_inc(s("aggr"), 1)

            def normalise(s, b):
                dve.wait_ge(s("rstd"), b + 1)
                at_least(dve, s("xT_ps"), b)
                for u in range(2):
                    v.tensor_scalar(xn[:, u, :], X[:, bass.ds(2 * b + u, 1), :].squeeze(1), mv[:, u, 0:1], rstd[:, u:u + 1],
                                    ALU.subtract, ALU.mult).then_inc(s("norm"), 1)

            def split(s, b, p, n, per, n_put):
                dve.wait_ge(s("qk32"), per * b + per)
                at_least(dve, s("put"), n_put * b)
                src, r = qkz[p][:, 0:n], res[:, 0:n]
                v.tensor_copy(part[:, 0, 0:n], src).then_inc(s("part"), 1)
                dve.wait_ge(s("part"), 3 * b + 1)
                v.tensor_tensor(r, src, part[:, 0, 0:n], ALU.subtract).then_inc(s("res"), 1)
                dve.wait_ge(s("res"), b + 1)
                v.tensor_copy(part[:, 1, 0:n], r).then_inc(s("part"), 1)
                dve.wait_ge(s("part"), 3 * b + 2)
                v.tensor_tensor(part[:, 2, 0:n], r, part[:, 1, 0:n], ALU.subtract).then_inc(s("part"), 1)

            def row_max(s, b, u, half):
                use = 4 * b + 2 * u + half
                dve.wait_ge(s("scores"), use + 1)
                bank = P1[half]
                v.tensor_reduce(nmax[:, u, 8 * half:8 * half + 8], bank[:, :].rearrange("p (h k) -> p h k", k=64),
                                AX.X, ALU.max, negate=True).then_inc(s("nmax"), 1)

            def shift_rows(s, b, p, n_max):
                at_least(dve, s("mT_ps"), b)
                v.tensor_copy(mparts[:, :, 0, :], nmax[:, :, :]).then_inc(s("mpart"), 1)
                dve.wait_ge(s("mpart"), 2 * b + 1)
                v.tensor_tensor(mparts[:, :, 1, :], nmax[:, :, :], mparts[:, :, 0, :], ALU.subtract).then_inc(s("mpart"), 1)

            def shift_spread(s, b, p):
                dve.wait_ge(s("mT_ps"), b + 1)
                v.tensor_copy(qs[p][SHIFT:128, 0, :], A1[:, :].bitcast(BF16)[SHIFT:128, 0:S]).then_inc(s("mT"), 1)
                dve.wait_ge(s("mT"), 2 * b + 1)
                v.tensor_copy(qs[p][SHIFT:128, 1:PAIRS, :], qs[p][SHIFT:128, 0:1, :].to_broadcast([32, PAIRS - 1, S])).then_inc(s("mT"), 1)

            def attended(s, b):
                dve.wait_ge(s("od"), b + 1)
                v.reciprocal(rden[:, :], OD[:, S:2 * S]).then_inc(s("rden"), 1)
                dve.wait_ge(s("rden"), b + 1)
                v.tensor_tensor(attT[:, :], OD[:, 0:S], rden[:, :], ALU.mult).then_inc(s("attT"), 1)

            def self_arrived(b):
                if isinstance(b, int) and b == 0:
                    dve.wait_ge(w_("x_first"), 16)
                elif isinstance(b, int) and b == 1:
                    dve.wait_ge(w_("x_rest"), 16)

            def self_finish_start(b, p):
                split(s_, b, p, 3 * S, 4, 32 * NP)
                dve.wait_ge(s_("vtok_ps"), b + 1)
                v.tensor_tensor(vg[p][:, :], A1[:, 2 * E:3 * E], same_head[:, :], ALU.mult).then_inc(s_("vg"), 1)

            def self_body(b, p, more):
                if more:
                    stats(s_, b + 1, self_arrived)
                row_max(s_, b, 0, 0)
                row_max(s_, b, 0, 1)
                if more:
                    normalise(s_, b + 1)
                row_max(s_, b, 1, 0)
                row_max(s_, b, 1, 1)
                dve.wait_ge(s_("scores_g"), b + 1)
                v.tensor_reduce(nmaxg[:, :, :], P1[0][:, 0:2 * 128].rearrange("p (h k) -> p h k", k=NGLOB),
                                AX.X, ALU.max, negate=True).then_inc(s_("nmaxg"), 1)
                dve.wait_ge(s_("nmaxg"), b + 1)
                dve.wait_ge(s_("nmax"), 4 * b + 4)
                v.tensor_tensor(nmax[:, :, :], nmax[:, :, :], nmaxg[:, :, :], ALU.min).then_inc(s_("nmaxall"), 1)
                dve.wait_ge(s_("nmaxall"), b + 1)
                shift_rows(s_, b, p, 4)
                dve.wait_ge(s_("gq_ps"), b + 1)
                v.tensor_reduce(gstat[:, 0:1], MISC[:, 0:S], AX.X, ALU.max, negate=True).then_inc(s_("gq_max"), 1)
                dve.wait_ge(s_("gq_max"), b + 1)
                v.tensor_scalar(gstat[:, 1:2], gstat[:, 0:1], SCALE, None, ALU.mult).then_inc(s_("gq_bias"), 1)
                shift_spread(s_, b, p)
                dve.wait_ge(s_("gq_exp"), b + 1)
                v.reciprocal(gstat[:, 3:4], gstat[:, 2:3]).then_inc(s_("gq_rcp"), 1)
                if more:
                    self_finish_start(b + 1, 1 - p)
                attended(s_, b)
                dve.wait_ge(s_("gq_o"), b + 1)
                v.tensor_tensor(gtmp[:, :, :], MISC[:, 0:128].rearrange("p (h g) -> p h g", g=NGLOB),
                                same_head[:, ::D].unsqueeze(2).to_broadcast([128, H, NGLOB]), ALU.mult).then_inc(s_("gtmp"), 1)
                dve.wait_ge(s_("gtmp"), b + 1)
                dve.wait_ge(s_("attT"), b + 1)
                for first, step, n, to in RUNS:
                    last = v.tensor_reduce(attT[:, first:first + step * (n - 1) + 1:step],
                                           gtmp[:, :, to:to + n].rearrange("p h g -> p g h"), AX.X, ALU.add)
                last.then_inc(s_("att_all"), 1)
                dve.wait_ge(s_("wo_ps"), b + 1)
                dve.wait_ge(s_("x_biased"), b + 1)
                xb = X[:, bass.ds(2 * b, 2), :]
                v.tensor_tensor(xb, MISC[:, 0:2 * E].rearrange("p (u c) -> p u c", u=2), xb, ALU.add).then_inc(s_("x_new"), 1)

            stats(s_, 0, self_arrived)
            normalise(s_, 0)
            self_finish_start(0, 0)
            loop(dve, self_body)

            if "B" in phases:
                def cross_arrived(b):
                    dve.wait_ge(s_("x_new"), b + 1)

                def cross_body(b, p, more):
                    if more:
                        stats(c_, b + 1, cross_arrived)
                    row_max(c_, b, 0, 0)
                    row_max(c_, b, 0, 1)
                    if more:
                        normalise(c_, b + 1)
                    row_max(c_, b, 1, 0)
                    row_max(c_, b, 1, 1)
                    dve.wait_ge(c_("nmax"), 4 * b + 4)
                    shift_rows(c_, b, p, 4)
                    shift_spread(c_, b, p)
                    if more:
                        split(c_, b + 1, 1 - p, S, 1, 16 * NP)
                    attended(c_, b)
                    dve.wait_ge(c_("y_ps"), b + 1)
                    dve.wait_ge(c_("x_biased"), b + 1)
                    xb = X[:, bass.ds(2 * b, 2), :]
                    v.tensor_tensor(xb, A1[:, 0:2 * E].rearrange("p (u c) -> p u c", u=2), xb, ALU.add).then_inc(c_("x_new"), 1)

                stats(c_, 0, cross_arrived)
                normalise(c_, 0)
                split(c_, 0, 0, S, 1, 16 * NP)
                loop(dve, cross_body)

            if "C" in phases:
                number = experts[:, 0:NE]

                def route(b, i, p):
                    stats(r_, b, lambda b: dve.wait_ge(c_("x_new"), b + 1))
                    dve.wait_ge(r_("rstd"), b + 1)
                    at_least(dve, r_("sent"), 64 * (b - 1))
                    for u in range(2):
                        v.tensor_scalar(xn3[p][:, u, :], X[:, bass.ds(2 * b + u, 1), :].squeeze(1), mv[:, u, 0:1],
                                        rstd[:, u:u + 1], ALU.subtract, ALU.mult).then_inc(r_("norm"), 1)
                    dve.wait_ge(r_("logit_ps"), b + 1)
                    v.tensor_copy(logits[:, :, :], A0[:, 0:2 * NE].rearrange("p (u e) -> p u e", e=NE)).then_inc(r_("logits"), 1)
                    wait_apart(dve, (r_("logits"), b + 1))
                    for u in range(2):
                        v.max(top8[:, u, :], logits[:, u, :]).then_inc(r_("top"), 1)
                    for u in range(2):
                        wait_apart(dve, (r_("top"), 2 * b + u + 1))
                        v.max_index(topi[:, u, :], top8[:, u, :], logits[:, u, :]).then_inc(r_("topi"), 1)
                    v.tensor_copy(topv[:, bass.ds(2 * b, 2), :], top8[:, :, 0:TOPK]).then_inc(r_("topv"), 1)
                    dve.wait_ge(r_("topi"), 2 * b + 2)
                    v.tensor_copy(topf[:, :, :], topi[:, :, 0:TOPK]).then_inc(r_("topf"), 1)
                    dve.wait_ge(r_("topf"), b + 1)
                    for u in range(2):
                        v.tensor_tensor(onehot[:, bass.ds(2 * b + u, 1), :, :].squeeze(1), number.unsqueeze(1).to_broadcast([128, TOPK, NE]),
                                        topf[:, u, :].unsqueeze(2).to_broadcast([128, TOPK, NE]), ALU.is_equal).then_inc(r_("onehot"), 1)
                    dve.wait_ge(r_("onehot"), 2 * b + 2)
                    oh = onehot[:, bass.ds(2 * b, 2), :, :]
                    v.tensor_tensor(both[:, :, :], oh[:, :, 0, :], oh[:, :, 1, :], ALU.add).then_inc(r_("both"), 1)
                    dve.wait_ge(r_("count_ps"), b + 1)
                    v.tensor_tensor(rowpos[:, :, :], A0[:, 0:2 * NE].rearrange("p (u e) -> p u e", e=NE),
                                    used[p][:, :].unsqueeze(1).to_broadcast([128, 2, NE]), ALU.add).then_inc(r_("rowpos"), 1)
                    v.tensor_tensor(used[1 - p][:, :], A0[:, 2 * NE:3 * NE], used[p][:, :], ALU.add).then_inc(r_("used"), 1)
                    dve.wait_ge(r_("rowpos"), b + 1)
                    for u in range(2):
                        v.tensor_tensor(picked[:, u, :, :], onehot[:, bass.ds(2 * b + u, 1), :, :].squeeze(1),
                                        rowpos[:, u, :].unsqueeze(1).to_broadcast([128, TOPK, NE]), ALU.mult).then_inc(r_("picked"), 1)
                    dve.wait_ge(r_("picked"), 2 * b + 2)
                    sl = slotf[:, bass.ds(2 * b, 2), :]
                    v.tensor_reduce(sl, picked[:, :, :, :], AX.X, ALU.add).then_inc(r_("slotf"), 1)
                    wait_apart(dve, (r_("slotf"), b + 1))
                    v.tensor_copy(sloti[p][:, :].rearrange("p (u k) -> p u k", k=TOPK), sl).then_inc(r_("slot"), 1)
                    dve.wait_ge(r_("used"), b + 1)

                dve.wait_ge(w_("set"), 4)
                loop2(dve, route, B)

                COUNT, TL, CUM, MET, NUM, AHEAD, ADJ, ONE = range(8)
                step = [0]

                def then(ins):
                    step[0] += 1
                    ins.then_inc(r_("plan"), 1)
                    dve.wait_ge(r_("plan"), step[0])

                end = used[0]
                v.tensor_copy(tails[0:1, :], end[0:1, :]).then_inc(r_("tails"), 1)
                then(v.tensor_tensor(plan[:, COUNT, :], end[:, :], experts[:, NE:2 * NE], ALU.subtract))
                then(v.tensor_scalar(plani[:, 0, :], plan[:, COUNT, :], 127.0, None, ALU.add))
                then(v.tensor_scalar(plani[:, 1, :], plani[:, 0, :], 7, None, ALU.arith_shift_right))
                then(v.tensor_copy(plan[:, TL, :], plani[:, 1, :]))
                then(v.memset(plan[:, ONE, :], 1.0))
                then(v.tensor_tensor_scan(plan[:, CUM, :], plan[:, ONE, :], plan[:, TL, :], 0.0, ALU.mult, ALU.add))
                then(v.tensor_scalar(plan[:, MET, :], plan[:, CUM, :], experts[:, 2 * NE:2 * NE + 1], None, ALU.is_le))
                then(v.tensor_tensor(plan[:, AHEAD, :], plan[:, MET, :], plan[:, TL, :], ALU.mult))
                then(v.tensor_reduce(tile_of[:, 0:1], plan[:, MET, :], AX.X, ALU.add))
                then(v.tensor_reduce(tile_of[:, 1:2], plan[:, AHEAD, :], AX.X, ALU.add))
                then(v.tensor_tensor(tile_of[:, 2:3], experts[:, 2 * NE:2 * NE + 1], tile_of[:, 1:2], ALU.subtract))
                then(v.tensor_scalar(tile_of[:, 2:3], tile_of[:, 2:3], 128.0, None, ALU.mult))
                then(v.scalar_tensor_tensor(tile_of[:, 2:3], tile_of[:, 0:1], float(CAP), tile_of[:, 2:3], ALU.mult, ALU.add))
                then(v.tensor_scalar(tile_of[:, 2:3], tile_of[:, 2:3], float(NE * CAP), None, ALU.min))
                v.tensor_scalar(tile_of[:, 3:4], tile_of[:, 0:1], float(NE - 1), None, ALU.min).then_inc(e_("tile_of"), 1)
                then(v.tensor_tensor(plan[:, ADJ, :], plan[:, CUM, :], plan[:, TL, :], ALU.subtract))
                then(v.tensor_scalar(plan[:, ADJ, :], plan[:, ADJ, :], 128.0, None, ALU.mult))
                then(v.tensor_tensor(plan[:, ADJ, :], plan[:, ADJ, :], experts[:, NE:2 * NE], ALU.subtract))
                then(v.tensor_tensor(picked_all[:, :, :], onehot[:, :, :, :].rearrange("p t k e -> p (t k) e"),
                                     plan[:, ADJ, :].unsqueeze(1).to_broadcast([128, NT * TOPK, NE]), ALU.mult))
                then(v.tensor_reduce(back[:, :], picked_all[:, :, :], AX.X, ALU.add))
                then(v.tensor_tensor(back[:, :], back[:, :], slotf[:, :, :].rearrange("p t k -> p (t k)"), ALU.add))
                v.tensor_copy(backi[:, :], back[:, :]).then_inc(g_("backi"), 1)
                dve.wait_ge(g_("gate_exp"), 1)
                then(v.tensor_scalar(gate[:, :], gate[:, :], 1.0, None, ALU.add))
                then(v.reciprocal(gate[:, :], gate[:, :]))
                dve.wait_ge(e_("map_ps"), 1)
                v.tensor_copy(tile_row[0:1, :, :], MISC[0:1, 0:256].rearrange("p (i k) -> p i k", i=2)).then_inc(e_("tile_row"), 1)

                def tile(k, i, p):
                    dve.wait_ge(e_("silu"), k + 1)
                    at_least(dve, e_("hT_ps"), k - 1)
                    v.tensor_tensor(eh[p][:, :], PS[2 + p][:, ED:2 * ED], sg[p][:, :], ALU.mult).then_inc(e_("h"), 1)

                def tile_end(k, i, p):
                    dve.wait_ge(e_("y_ps"), k + 1)
                    at_least(dve, e_(f"out{p}"), 16 * i)
                    v.tensor_copy(ey[p][:, :], PS[6 + p][:, 0:E]).then_inc(e_("y"), 1)

                skewed(dve, [(tile, 0), (tile_end, 2)], TILES)

                def shared(u, i, p):
                    for c in range(2):
                        dve.wait_ge(h_("silu"), 2 * u + c + 1)
                        at_least(dve, h_("y_ps"), u)
                        v.tensor_tensor(shs[:, c, :], PS[2 * c + 1][:, :], sgs[:, c, :], ALU.mult).then_inc(h_("h"), 1)
                    dve.wait_ge(h_("y_ps"), u + 1)
                    xu = X[:, bass.ds(4 * u, 4), :]
                    v.tensor_tensor(xu, PS[4 + p][:, :].rearrange("p (t c) -> p t c", t=4), xu, ALU.add).then_inc(h_("x"), 1)

                loop2(dve, shared, B // 2)

                def combine(b, i, p):
                    dve.wait_ge(h_("x"), B // 2)
                    dve.wait_ge(g_(f"got{p}"), 64 * (i + 1))
                    for u in range(2):
                        xu = X[:, bass.ds(2 * b + u, 1), :].squeeze(1)
                        for k in range(TOPK):
                            if k:
                                dve.wait_ge(g_("first"), 2 * b + u + 1)
                            last = v.scalar_tensor_tensor(xu, yrow[p][:, 2 * u + k, :], gate[:, bass.ds(4 * b + 2 * u + k, 1)], xu,
                                                          ALU.mult, ALU.add)
                            if k == 0:
                                last.then_inc(g_("first"), 1)
                    last.then_inc(g_("x_out"), 1)

                loop2(dve, combine, B)

        @block.scalar
        def _(act):
            a_ = nc.scalar
            act.wait_ge(w_("turned_ps"), 1)
            a_.copy(rwT[:, :], PS[4][:, 0:NE]).then_inc(w_("turned"), 1)
            for i in range(2):
                a_.copy(shT[:, 3 * i:3 * i + 3, :], PS[5 + i][:, 0:384].rearrange("p (i c) -> p i c", i=3)).then_inc(w_("turned"), 1)
            act.wait_ge(w_("ctxT_ps"), 1)
            for i in range(2):
                a_.copy(ctxT[:, 512 * i:512 * i + 512], PS[i][0:EC, :]).then_inc(w_("ctxT"), 1)
            act.wait_ge(w_("kbias"), 2)
            for i in range(2):
                act.wait_ge(w_("ck_ps"), i + 1)
                for a in range(2):
                    a_.activation(ck32[:, 8 * i:8 * i + 8, a, :], PS[2 + i][:, :].rearrange("p (b k) -> p b k", k=M), ACT.Identity,
                                  bias=kbias[:, 1, a:a + 1], scale=of_pair[:, a:a + 1]).then_inc(w_("ck32"), 1)
            act.wait_ge(w_("zeroed"), 1)
            for i in range(4):
                act.wait_ge(w_("cv_ps"), i + 1)
                value_cells(a_, cvbd_all[:, 4 * i:4 * i + 4, :, :], PS[i], w_("cv"))

            def self_start(b, p):
                act.wait_ge(s_("xT_ps"), b + 1)
                at_least(act, s_("vtok_ps"), b)
                a_.copy(xnT[:, :], A0[:, 0:S]).then_inc(s_("xnT"), 1)

            def self_start2(b, p):
                act.wait_ge(s_("qk_ps"), 2 * b + 2)
                a_.activation(qkz[p][:, 0:S], A0[:, 0:S], ACT.Identity, bias=cols[:, 0:1]).then_inc(s_("qk32"), 1)
                kz = qkz[p][:, S:3 * S].rearrange("p (n a k) -> p n a k", a=2, k=BLOCK)
                for a in range(2):
                    a_.activation(kz[:, :, a, :], A0[:, S:2 * S].rearrange("p (n k) -> p n k", k=BLOCK), ACT.Identity,
                                  bias=kbias[:, 0, a:a + 1], scale=of_pair[:, a:a + 1]).then_inc(s_("qk32"), 1)
                a_.activation(k32[p][:, :], A0[:, S:2 * S], ACT.Identity, bias=cols[:, 1:2]).then_inc(s_("qk32"), 1)
                act.wait_ge(s_("vdup_ps"), b + 1)
                value_cells(a_, vbd[p][:, :, :, :], A1, s_("vbd"))

            def self_start3(b, p):
                act.wait_ge(s_("vtok_ps"), b + 1)
                dve_done = s_("vg")
                act.wait_ge(dve_done, b + 1)
                a_.copy(vtok[p][:, :, :], A1[:, 0:2 * E].rearrange("p (u c) -> p u c", u=2)).then_inc(s_("vtok"), 1)

            def exps(s, b, used):
                for i in range(4):
                    act.wait_ge(s("pair"), 4 * b + i + 1)
                    if i == 0:
                        at_least(act, s("od"), b)
                    a_.activation(probs[:, 2 * i:2 * i + 2, :], P2[i % 2][:, :].rearrange("p (j q) -> p j q", j=2),
                                  ACT.Exp, scale=SCALE).then_inc(s("probs"), 1)

            def self_body(b, p, more):
                if more:
                    self_start(b + 1, 1 - p)
                act.wait_ge(s_("gq_bias"), b + 1)
                at_least(act, s_("gq_T"), b)
                a_.activation(pgq[:, :], MISC[:, 0:S], ACT.Exp, bias=gstat[:, 1:2], scale=SCALE,
                              accum_out=gstat[:, 2:3]).then_inc(s_("gq_exp"), 1)
                if more:
                    self_start2(b + 1, 1 - p)
                exps(s_, b, None)
                act.wait_ge(s_("gk_ps"), b + 1)
                a_.activation(probs_g[:, :], P2[0][:, 0:S], ACT.Exp, scale=SCALE).then_inc(s_("gexp"), 1)
                if more:
                    self_start3(b + 1, 1 - p)
                act.wait_ge(s_("gq_T"), b + 1)
                a_.copy(pgqT[:, :, :], MISC[:, 0:256].rearrange("p (u c) -> p u c", u=2)).then_inc(s_("pgqT"), 1)

            self_start(0, 0)
            self_start2(0, 0)
            self_start3(0, 0)
            loop(act, self_body)

            if "B" in phases:
                def cross_start(b, p):
                    act.wait_ge(c_("xT_ps"), b + 1)
                    a_.copy(xnT[:, :], A0[:, 0:S]).then_inc(c_("xnT"), 1)

                def cross_start2(b, p):
                    act.wait_ge(c_("q_ps"), b + 1)
                    a_.activation(qkz[p][:, 0:S], A0[:, 0:S], ACT.Identity, bias=cols[:, 3:4]).then_inc(c_("qk32"), 1)

                def cross_body(b, p, more):
                    if more:
                        cross_start(b + 1, 1 - p)
                        cross_start2(b + 1, 1 - p)
                    exps(c_, b, None)
                    act.wait_ge(c_("h_ps"), b + 1)
                    for i in range(2):
                        a_.activation(hT[:, i, :], MISC[:, i * S:(i + 1) * S], ACT.Relu, bias=cb1_[:, i:i + 1]).then_inc(c_("h"), 1)

                act.wait_ge(w_("bo_"), 2)
                cross_start(0, 0)
                cross_start2(0, 0)
                loop(act, cross_body)

            if "C" in phases:
                def route(b, i, p):
                    act.wait_ge(r_("xT_ps"), b + 1)
                    at_least(act, r_("logit_ps"), b)
                    a_.copy(x3s[:, :], A0[:, 0:S]).then_inc(r_("xnT"), 1)
                    a_.copy(x3T[:, bass.ds(S * b, S)], A0[:, 0:S]).then_inc(r_("xnT"), 1)

                loop2(act, route, B)
                act.wait_ge(r_("topv"), B)
                a_.activation(gate[:, :], topv[:, :, :].rearrange("p t k -> p (t k)"), ACT.Exp, scale=-1.0).then_inc(g_("gate_exp"), 1)

                def turn(k, i, p):
                    act.wait_ge(e_("xT_ps"), k + 1)
                    at_least(act, e_("gu_ps"), k - 1)
                    a_.copy(xtT[p][:, :], PS[p][:, 0:128]).then_inc(e_("xtT"), 1)

                def silu(k, i, p):
                    act.wait_ge(e_("gu_ps"), k + 1)
                    at_least(act, e_("h"), k - 1)
                    a_.activation(sg[p][:, :], PS[2 + p][:, 0:ED], ACT.Silu).then_inc(e_("silu"), 1)

                def turn_h(k, i, p):
                    act.wait_ge(e_("hT_ps"), k + 1)
                    at_least(act, e_("y_ps"), k - 1)
                    a_.copy(ehT[p][:, :], PS[4 + p][:, 0:128]).then_inc(e_("ehT"), 1)

                def out_rows(k, i, p):
                    act.wait_ge(e_("y"), k + 1)
                    act.dma_start(ys[bass.ds(128 * k, 128), :], ey[p][:, :]).then_inc(e_(f"out{p}"), 16)

                skewed(act, [(turn, 0), (silu, 1), (turn_h, 2), (out_rows, 4)], TILES)

                def shared(u, i, p):
                    for c in range(2):
                        act.wait_ge(h_("gu_ps"), 2 * u + c + 1)
                        at_least(act, h_("h"), 2 * u)
                        a_.activation(sgs[:, c, :], PS[2 * c][:, :], ACT.Silu).then_inc(h_("silu"), 1)

                loop2(act, shared, B // 2)

        @block.tensor
        def _(pe):
            mm, tr = nc.tensor.matmul, nc.tensor.transpose

            pe.wait_ge(w_("weights"), 16 * W_LOADS)
            tr(PS[4][:, 0:NE], rw_rows[:, :], ident[0:NE, 0:NE])
            for i in range(6):
                last = tr(PS[5 + i // 3][:, (i % 3) * 128:(i % 3) * 128 + 128], sh_rows[:, i, :], ident[:, :])
            last.then_inc(w_("turned_ps"), 1)
            for i in range(B * M // 128):
                last = tr(PS[i // 4][0:EC, (i % 4) * 128:(i % 4) * 128 + 128], ctx_rows[:, i, :], ident[:, :])
            last.then_inc(w_("ctxT_ps"), 1)
            mm(MISC[:, 0:E], cols[:, 2:3].to_broadcast([128, 128]), wo[:, :], start=True, stop=True)
            for i in range(2):
                last = mm(MISC[:, E + i:E + i + 1], cw1[:, i * 128:(i + 1) * 128], cols[:, 5:6], start=True, stop=True)
            last.then_inc(w_("bias_ps"), 1)
            pe.wait_ge(w_("ctxT"), 2)
            for i in range(2):
                mm(PS[2 + i][:, :], cwk[:, :], ctxT[:, 512 * i:512 * i + 512], start=True, stop=True).then_inc(w_("ck_ps"), 1)
            for i in range(4):
                if i >= 2:
                    pe.wait_ge(w_("ck32"), 2 * (i - 1))
                for j in range(4):
                    bb = 4 * i + j
                    for a in range(2):
                        last = mm(PS[i][64 * a:64 * a + 64, j * 128:(j + 1) * 128], ctxT[:, bb * M:(bb + 1) * M], cwv[:, :], start=True, stop=True)
                last.then_inc(w_("cv_ps"), 1)
            pe.wait_ge(w_("turned"), 3)
            pe.wait_ge(w_("cv"), 8)
            pe.wait_ge(w_("set"), 4)
            pe.wait_ge(w_("bo_"), 2)

            def columns(s, b, free):
                pe.wait_ge(s("norm"), 2 * b + 2)
                at_least(pe, s("qk32"), free * b)
                for u in range(2):
                    last = tr(A0[:, u * 128:(u + 1) * 128], xn[:, u, :], ident[:, :])
                last.then_inc(s("xT_ps"), 1)

            def self_project(b, p):
                pe.wait_ge(s_("xnT"), b + 1)
                for i, w in enumerate((wq, wk)):
                    mm(A0[:, i * S:(i + 1) * S], w[:, :], xnT[:, :], start=True, stop=True).then_inc(s_("qk_ps"), 1)
                if isinstance(b, int) and b == 0:
                    pass
                else:
                    pe.wait_ge(s_("mT"), 2 * b - 1)
                for n in range(NB):
                    for a in range(2):
                        last = mm(A1[64 * a:64 * a + 64, n * E:(n + 1) * E], xnT[:, n * BLOCK:(n + 1) * BLOCK], wv[:, :], start=True, stop=True)
                last.then_inc(s_("vdup_ps"), 1)

            def self_project2(b, p):
                pe.wait_ge(s_("vbd"), 2 * b + 2)
                pe.wait_ge(s_("xg"), b + 1)
                for u in range(2):
                    mm(A1[:, u * E:(u + 1) * E], xnT[:, u * 128:(u + 1) * 128], wv[:, :], start=True, stop=True)
                mm(A1[:, 2 * E:3 * E], xg[:, :, :].rearrange("p h g -> p (h g)"), wv[:, :],
                   start=True, stop=True).then_inc(s_("vtok_ps"), 1)

            def turn_shift(s, b):
                pe.wait_ge(s("mpart"), 2 * b + 2)
                for u in range(2):
                    last = tr(A1[:, :].bitcast(BF16)[SHIFT:128, u * 128:(u + 1) * 128],
                              mparts[:, u, :, :].rearrange("p i h -> p (i h)"), identb[:, :])
                last.then_inc(s("mT_ps"), 1)

            def self_body(b, p, more):
                pe.wait_ge(s_("got"), 32 * b + 32)
                for u in range(2):
                    for half in range(2):
                        if u == 0 and half == 0:
                            at_least(pe, s_("nmaxg"), b)
                        elif u == 0:
                            at_least(pe, s_("nmax"), 4 * b)
                        else:
                            pe.wait_ge(s_("nmax"), 4 * b + half + 1)
                        for j in range(4):
                            for i in range(2):
                                n = 2 * u + i
                                last = mm(P1[half][64 * i:64 * i + 64, j * 128:(j + 1) * 128],
                                          qs[p][0:KROWS, 4 * half + j, n * BLOCK:(n + 1) * BLOCK],
                                          kbd[p][0:KROWS, 4 * half + j, n, :, :].rearrange("r a k -> r (a k)"), start=True, stop=True)
                        last.then_inc(s_("scores"), 1)
                if more:
                    columns(s_, b + 1, 4)
                pe.wait_ge(s_("kgqg"), 2 * b + 2)
                at_least(pe, s_("x_new"), b)
                mm(MISC[:, 0:S], qg[p][:, :, :].rearrange("p h g -> p (h g)"), k32[p][:, :], start=True, stop=True).then_inc(s_("gq_ps"), 1)
                pe.wait_ge(s_("nmax"), 4 * b + 3)
                for u in range(2):
                    last = mm(P1[0][:, u * 128:(u + 1) * 128], qkz[p][:, u * 128:(u + 1) * 128],
                              kg[p][:, :, :].rearrange("p h g -> p (h g)"), start=True, stop=True)
                last.then_inc(s_("scores_g"), 1)
                pe.wait_ge(s_("vtok"), b + 1)
                turn_shift(s_, b)
                if more:
                    self_project(b + 1, 1 - p)
                pe.wait_ge(s_("mT"), 2 * b + 2)
                for i in range(4):
                    if i < 2:
                        at_least(pe, s_("gexp") if i == 0 else s_("probs"), b if i == 0 else 4 * b)
                    else:
                        pe.wait_ge(s_("probs"), 4 * b + i - 1)
                    for jj in range(2):
                        j = 2 * i + jj
                        for n in range(NB):
                            last = mm(P2[i % 2][:, jj * S + n * BLOCK:jj * S + (n + 1) * BLOCK],
                                      kbd[p][:, j, n, :, :].rearrange("r a k -> r (a k)"), qs[p][:, j, n * BLOCK:(n + 1) * BLOCK],
                                      start=True, stop=True)
                    last.then_inc(s_("pair"), 1)
                pe.wait_ge(s_("probs"), 4 * b + 3)
                mm(P2[0][:, 0:S], kg[p][:, :, :].rearrange("p h g -> p (h g)"), qkz[p][:, 0:S], start=True, stop=False)
                mm(P2[0][:, 0:S], shift_glob[SHIFT:128, :], qs[p][SHIFT:128, 0, :], start=False, stop=True).then_inc(s_("gk_ps"), 1)
                if more:
                    self_project2(b + 1, 1 - p)
                at_least(pe, s_("attT"), b)
                for i in range(4):
                    pe.wait_ge(s_("probs"), 4 * b + i + 1)
                    for jj in range(2):
                        j = 2 * i + jj
                        for n in range(NB):
                            mm(OD[32 * i:32 * i + 32, n * BLOCK:(n + 1) * BLOCK], vbd[p][:, n, j, :],
                               probs[:, j, n * BLOCK:(n + 1) * BLOCK], start=(jj == 0 and n == 0), stop=False, skip_group_check=True)
                        mm(OD[32 * i:32 * i + 32, S:2 * S], key_ones[:, jj, :], probs[:, j, :], start=False, stop=False, skip_group_check=True)
                pe.wait_ge(s_("gmasked"), b + 1)
                mm(OD[:, 0:S], vg[p][:, :], probs_g[:, :], start=False, stop=True, skip_group_check=True)
                mm(OD[:, S:2 * S], same_head[:, :], probs_g[:, :], start=False, stop=True, skip_group_check=True).then_inc(s_("od"), 1)
                pe.wait_ge(s_("gq_norm"), b + 1)
                for u in range(2):
                    last = tr(MISC[:, u * 128:(u + 1) * 128], pgq[:, u * 128:(u + 1) * 128], ident[:, :])
                last.then_inc(s_("gq_T"), 1)
                pe.wait_ge(s_("pgqT"), b + 1)
                for u in range(2):
                    last = mm(MISC[:, 0:128], vtok[p][:, u, :], pgqT[:, u, :], start=(u == 0), stop=(u == 1))
                last.then_inc(s_("gq_o"), 1)
                pe.wait_ge(s_("att_all"), b + 1)
                for u in range(2):
                    last = mm(MISC[:, u * E:(u + 1) * E], attT[:, u * 128:(u + 1) * 128], wo[:, :], start=True, stop=True)
                last.then_inc(s_("wo_ps"), 1)

            columns(s_, 0, 4)
            self_project(0, 0)
            self_project2(0, 0)
            loop(pe, self_body)

            if "B" in phases:
                def cross_project(b, p):
                    pe.wait_ge(c_("xnT"), b + 1)
                    mm(A0[:, 0:S], cwq[:, :], xnT[:, :], start=True, stop=True).then_inc(c_("q_ps"), 1)

                def cross_body(b, p, more):
                    pe.wait_ge(c_("got"), 48 * b + 48)
                    for u in range(2):
                        for half in range(2):
                            if u == 0:
                                at_least(pe, c_("nmax"), 4 * b - 1 + half if not isinstance(b, int) or b > 0 else 0)
                            else:
                                pe.wait_ge(c_("nmax"), 4 * b + half + 1)
                            for j in range(4):
                                last = mm(P1[half][:, j * 128:(j + 1) * 128], qs[p][0:KROWS, 4 * half + j, u * 128:(u + 1) * 128],
                                          ckbd[p][0:KROWS, 4 * half + j, :, :].rearrange("r a k -> r (a k)"), start=True, stop=True)
                            last.then_inc(c_("scores"), 1)
                    if more:
                        columns(c_, b + 1, 1)
                    at_least(pe, c_("x_new"), b)
                    turn_shift(c_, b)
                    if more:
                        cross_project(b + 1, 1 - p)
                    pe.wait_ge(c_("mT"), 2 * b + 2)
                    for i in range(4):
                        at_least(pe, c_("probs"), 4 * b + i - 1 if not isinstance(b, int) or b + i > 1 else 0)
                        for jj in range(2):
                            j = 2 * i + jj
                            last = mm(P2[i % 2][:, jj * S:(jj + 1) * S], ckbd[p][:, j, :, :].rearrange("p a k -> p (a k)"), qs[p][:, j, :],
                                      start=True, stop=True)
                        last.then_inc(c_("pair"), 1)
                    at_least(pe, c_("attT"), b)
                    for i in range(4):
                        pe.wait_ge(c_("probs"), 4 * b + i + 1)
                        for jj in range(2):
                            j = 2 * i + jj
                            mm(OD[32 * i:32 * i + 32, 0:S], cvbd[p][:, j, :], probs[:, j, :], start=(jj == 0), stop=(jj == 1), skip_group_check=True)
                            last = mm(OD[32 * i:32 * i + 32, S:2 * S], key_ones[:, jj, :], probs[:, j, :], start=False, stop=(jj == 1), skip_group_check=True)
                    last.then_inc(c_("od"), 1)
                    pe.wait_ge(c_("attT"), b + 1)
                    at_least(pe, c_("h"), 2 * b)
                    for i in range(2):
                        last = mm(MISC[:, i * S:(i + 1) * S], cw1[:, i * 128:(i + 1) * 128], attT[:, :], start=True, stop=True)
                    last.then_inc(c_("h_ps"), 1)
                    pe.wait_ge(c_("h"), 2 * b + 2)
                    for u in range(2):
                        for i in range(2):
                            last = mm(A1[:, u * E:(u + 1) * E], hT[:, i, u * 128:(u + 1) * 128], cw2[:, i, :], start=(i == 0), stop=(i == 1))
                    last.then_inc(c_("y_ps"), 1)

                pe.wait_ge(s_("x_new"), B)
                columns(c_, 0, 1)
                cross_project(0, 0)
                loop(pe, cross_body)

            if "C" in phases:
                def route(b, i, p):
                    pe.wait_ge(r_("norm"), 2 * b + 2)
                    at_least(pe, r_("used"), b)
                    for u in range(2):
                        last = tr(A0[:, u * 128:(u + 1) * 128], xn3[p][:, u, :], ident[:, :])
                    last.then_inc(r_("xT_ps"), 1)
                    pe.wait_ge(r_("xnT"), 2 * b + 2)
                    for u in range(2):
                        last = mm(A0[:, u * NE:(u + 1) * NE], x3s[:, u * 128:(u + 1) * 128], rwT[:, :], start=True, stop=True)
                    last.then_inc(r_("logit_ps"), 1)
                    pe.wait_ge(r_("both"), b + 1)
                    mm(A0[:, 0:NE], aheadb[:, 0:128], both[:, 0, :], start=True, stop=True)
                    mm(A0[:, NE:2 * NE], aheadb[:, 0:128], both[:, 1, :], start=True, stop=False)
                    mm(A0[:, NE:2 * NE], aheadb[:, 128:256], both[:, 0, :], start=False, stop=True)
                    mm(A0[:, 2 * NE:3 * NE], aheadb[:, 128:256], both[:, 0, :], start=True, stop=False)
                    mm(A0[:, 2 * NE:3 * NE], aheadb[:, 128:256], both[:, 1, :], start=False, stop=True).then_inc(r_("count_ps"), 1)

                loop2(pe, route, B)

                pe.wait_ge(e_("tile_of"), 1)
                pe.wait_ge(c_("h"), 2 * B)
                for i in range(2):
                    last = tr(MISC[0:1, i * 128:(i + 1) * 128], tile_of[:, 2 + i:3 + i], ident[:, :])
                last.then_inc(e_("map_ps"), 1)
                pe.wait_ge(e_("tile_row"), 1)
                pe.wait_ge(w_("experts"), 32)
                pe.wait_ge(c_("y_ps"), B)
                pe.wait_ge(c_("x_new"), B)
                pe.wait_ge(c_("attT"), B)

                def turn(k, i, p):
                    pe.wait_ge(e_(f"in{p}"), 16 * (i + 1))
                    at_least(pe, e_("xtT"), k - 1)
                    tr(PS[p][:, 0:128], xt[p][:, :], ident[:, :]).then_inc(e_("xT_ps"), 1)

                def gate_up(k, i, p):
                    which = pe.value_load(tile_row[0:1, 1, bass.ds(k, 1)], min_val=0, max_val=NE - 1)
                    pe.wait_ge(e_("xtT"), k + 1)
                    at_least(pe, e_("h"), k - 1)
                    mm(PS[2 + p][:, 0:2 * ED], xtT[p][:, :], wgu[:, bass.ds(which, 1), :].squeeze(1), start=True, stop=True).then_inc(e_("gu_ps"), 1)

                def turn_h(k, i, p):
                    pe.wait_ge(e_("h"), k + 1)
                    at_least(pe, e_("ehT"), k - 1)
                    tr(PS[4 + p][:, 0:128], eh[p][:, :], ident[:, :]).then_inc(e_("hT_ps"), 1)

                def down(k, i, p):
                    which = pe.value_load(tile_row[0:1, 1, bass.ds(k, 1)], min_val=0, max_val=NE - 1)
                    pe.wait_ge(e_("ehT"), k + 1)
                    at_least(pe, e_("y"), k - 1)
                    mm(PS[6 + p][:, 0:E], ehT[p][:, :], wd[:, bass.ds(which, 1), :].squeeze(1), start=True, stop=True).then_inc(e_("y_ps"), 1)

                skewed(pe, [(turn, 0), (gate_up, 1), (turn_h, 2), (down, 3)], TILES)
                pe.wait_ge(e_("y"), TILES)

                def shared_in(u, i, p, c):
                    at_least(pe, h_("h"), 2 * (u - 1) + c + 1 if not isinstance(u, int) or u > 0 else 0)
                    for k in range(2):
                        last = mm(PS[2 * c + k][:, :], shT[:, 2 * k + c, :], x3T[:, bass.ds(512 * u, 512)], start=True, stop=True)
                    last.then_inc(h_("gu_ps"), 1)

                def shared_out(u, i, p):
                    pe.wait_ge(h_("h"), 2 * u + 2)
                    at_least(pe, h_("x"), u - 1)
                    for j in range(4):
                        for c in range(2):
                            last = mm(PS[4 + p][:, j * E:(j + 1) * E], shs[:, c, j * 128:(j + 1) * 128], shT[:, 4 + c, :], start=(c == 0), stop=(c == 1))
                    last.then_inc(h_("y_ps"), 1)

                def shared(u, i, p):
                    shared_in(u, i, p, 0)
                    shared_in(u, i, p, 1)
                    shared_out(u, i, p)

                loop2(pe, shared, B // 2)


W_LOADS = 7 + 8 + 1 + 6 + 2 + 2 + 6 + 1


def value_cells(eng, dst, bank, sem):
    for a in range(2):
        src = bank[64 * a:64 * a + 64, :].rearrange("p (ng jj a d) -> p ng jj a d", jj=2, a=2, d=D)[:, :, :, a, :]
        full = dst[64 * a:64 * a + 64].rearrange("p n (g jj) c -> p (n g) (jj c)", jj=2)
        for jj in range(2):
            cell = jj * 48 + a * D
            last = eng.copy(full[:, :, cell:cell + D], src[:, :, jj, :])
        last.then_inc(sem, 1)


_INS = ["x", "ctx_768", "L0_attn_Wq", "L0_attn_bq", "L0_attn_Wk", "L0_attn_bk", "L0_attn_Wv", "L0_attn_bv",
        "L0_attn_Wo", "L0_attn_bo", "L0_xattn_Wq", "L0_xattn_bq", "L0_xattn_Wk", "L0_xattn_bk", "L0_xattn_Wv",
        "L0_xattn_bv", "L0_xattn_W1", "L0_xattn_b1", "L0_xattn_W2", "L0_xattn_b2", "L0_ffn_router_w",
        "L0_ffn_gate_up_w", "L0_ffn_down_w", "L0_ffn_shared_gate_w", "L0_ffn_shared_up_w", "L0_ffn_shared_down_w"]


def kernel(**inputs):
    import numpy as _np
    import concourse.bacc as _bacc
    from concourse.bass_utils import run_bass_kernel_spmd as _run

    nc = _bacc.Bacc("TRN2", target_bir_lowering=False, num_devices=1)
    arrays, args = {}, {}
    given = {name: _np.ascontiguousarray(inputs[name]) for name in _INS}
    for name, a in {**given, **shape_constants()}.items():
        arrays[f"in_{name}"] = a
        args[name] = nc.dram_tensor(f"in_{name}", a.shape, mybir.dt.from_np(a.dtype), kind="ExternalInput").ap()
    out = nc.dram_tensor("out_0", (B, S, E), F32, kind="ExternalOutput").ap()
    decoder(nc, args, out)
    r = _run(nc, [arrays], core_ids=[0])
    return r.results[0]["out_0"]
```

```python
import numpy as np
import concourse.bass as bass
from concourse import mybir
from contextlib import ExitStack

F32 = mybir.dt.float32
BF16 = mybir.dt.bfloat16
I32 = mybir.dt.int32
U32 = mybir.dt.uint32
ACT = mybir.ActivationFunctionType
ALU = mybir.AluOpType
AX = mybir.AxisListType

B, S, E = 16, 256, 128
M, EC = 64, 96
H, D = 16, 8
BLOCK, NGLOB = 64, 8
NB = S // BLOCK
PAIRS = H // 2
NT = B * S // 128
NE, TOPK, ED, SD = 16, 2, 128, 256
CAP = B * S + 128
TILES = B * S * TOPK // 128 + NE
EPS = 1e-5
SCALE = 1.0 / float(np.sqrt(D))
GLOBALS = [int(g) for g in np.linspace(0, S - 1, NGLOB)]
RUNS = [(GLOBALS[0], 1, 1, 0), (GLOBALS[1], GLOBALS[3] - GLOBALS[1], 4, 1), (GLOBALS[2], GLOBALS[4] - GLOBALS[2], 3, 5)]
G_ORDER = [a + s * i for a, s, c, _ in RUNS for i in range(c)]
assert sorted(G_ORDER) == GLOBALS
Q_PART = (0, 0, 0, 1, 1, 2)
K_PART = (0, 1, 2, 0, 1, 0)
NP = len(Q_PART)
KROWS = 2 * NP * D
SHIFT = KROWS


def constant_columns():
    p = np.arange(128)
    c = {}
    c["ident"] = np.eye(128)
    c["same_head"] = p[:, None] // D == p[None, :] // D
    c["head_of_row"] = (2 * (p % PAIRS) + p // 64)[:, None] == np.arange(H)[None, :]
    c["outside"] = np.array(G_ORDER)[p % NGLOB][:, None] // BLOCK != np.arange(NB)[None, :]
    c["shift_pair"] = (p % H)[:, None] == np.arange(H)[None, :]
    c["shift_glob"] = (p % H)[:, None] == p[None, :] // D
    o = np.zeros((128, 2, 2, 2, D))
    for jj in range(2):
        for a in range(2):
            o[a * 64:(a + 1) * 64, jj, jj, a] = 1.0
    c["key_ones"] = o.reshape(128, 64)
    e = np.arange(NE)
    c["experts"] = np.concatenate([np.tile(e, (128, 1)), np.tile(e * CAP, (128, 1)), p[:, None]], axis=1)
    c["ahead"] = np.concatenate([(p[:, None] < p[None, :]), np.ones((128, 128))], axis=1)
    return c


def shape_constants():
    return {"constants": np.concatenate(list(constant_columns().values()), axis=1).astype(np.float32)}


def at_least(eng, sem, value):
    if not isinstance(value, int) or value > 0:
        eng.wait_ge(sem, value)


def decoder(nc, t, out, phases="ABC"):
    ctx = ExitStack()
    with ctx:
        def sb(name, shape, dt=F32):
            return ctx.enter_context(nc.sbuf_tensor(name, shape, dt))

        class Sems:
            def __init__(self, prefix):
                self.prefix, self.made = prefix, {}

            def __call__(self, name):
                if name not in self.made:
                    self.made[name] = ctx.enter_context(nc.semaphore(self.prefix + name))
                return self.made[name]

        w_ = Sems("w_")
        s_ = Sems("self_")
        c_ = Sems("cross_")
        r_ = Sems("route_")
        e_ = Sems("expert_")
        h_ = Sems("shared_")
        g_ = Sems("gather_")

        X = sb("x_rows", [128, NT, E])
        constants = sb("constants", list(t["constants"].shape))
        held, at = {}, 0
        for name, a in constant_columns().items():
            held[name] = constants[:, at:at + a.shape[1]]
            at += a.shape[1]
        ident, same_head, outside, head_of_row = (held[n] for n in ("ident", "same_head", "outside", "head_of_row"))
        experts, ahead = held["experts"], held["ahead"]
        key_ones = held["key_ones"].rearrange("p (j c) -> p j c", j=2)
        identb = sb("identb", [128, 128], BF16)
        shift_glob = sb("shift_glob", [128, 128], BF16)
        minus_half = sb("minus_half", [128, 2])
        wq, wk, wv, wo = (sb(n, [E, E]) for n in ("wq", "wk", "wv", "wo"))
        cwq = sb("cwq", [E, E])
        cwk, cwv = sb("cwk", [EC, E]), sb("cwv", [EC, E])
        cw1, cw2 = sb("cw1", [E, 2 * E]), sb("cw2", [128, 2, E])
        cols = sb("cols", [128, 8])
        w_raw = sb("w_raw", [128, 4, E])
        rows = sb("rows", [128, 2, E])
        cb1_ = sb("cb1_", [128, 2])
        bo_ = sb("bo_", [128, E])
        ctx_rows = sb("ctx_rows", [128, B * M // 128, EC])
        ctxT = sb("ctxT", [EC, B * M])
        x3T = sb("x3T", [128, B * S])
        wgu = sb("wgu", [E, NE, 2 * ED])
        ck32 = x3T[:, 0:2 * B * M].rearrange("p (b a k) -> p b a k", a=2, k=M)
        ckres = x3T[:, 2 * B * M:4 * B * M].rearrange("p (b a k) -> p b a k", a=2, k=M)
        ckpart = wgu[:, 0:12, :].rearrange("p e h -> p (e h)").bitcast(BF16).rearrange("p (i b a k) -> p i b a k", i=3, a=2, k=M)
        cvbd_all = sb("cvbd_all", [128, B, PAIRS, 32])

        st = sb("st", [128, 2, 6])
        mv = sb("mv", [128, 2, 2])
        veps = sb("veps", [128, 2])
        rstd = sb("rstd", [128, 2])
        xn = sb("xn", [128, 2, E])
        xnT = sb("xnT", [128, S])
        xg = sb("xg", [128, H, NGLOB])
        qkz = [sb(f"qkz{i}", [128, 3 * S]) for i in range(2)]
        k32 = [sb(f"k32_{i}", [128, S]) for i in range(2)]
        res = sb("res", [128, 3 * S])
        part = sb("part", [128, 3, 3 * S], BF16)
        qs = [sb(f"qs{i}", [128, PAIRS, S], BF16) for i in range(2)]
        kbd = [sb(f"kbd{i}", [128, PAIRS, NB, 2, BLOCK], BF16) for i in range(2)]
        vbd = [sb(f"vbd{i}", [128, NB, PAIRS, 32]) for i in range(2)]
        vtok = [sb(f"vtok{i}", [128, 2, E]) for i in range(2)]
        vg = [sb(f"vg{i}", [128, E]) for i in range(2)]
        kg = [sb(f"kg{i}", [128, H, NGLOB]) for i in range(2)]
        qg = [sb(f"qg{i}", [128, H, NGLOB]) for i in range(2)]
        nmax = sb("nmax", [128, 2, H])
        nmaxg = sb("nmaxg", [128, 2, H])
        mparts = sb("mparts", [128, 2, 2, H], BF16)
        probs = sb("probs", [128, PAIRS, S])
        probs_g = sb("probs_g", [128, S])
        pgq = sb("pgq", [128, S])
        pgqT = sb("pgqT", [128, 2, 128])
        gstat = sb("gstat", [128, 4])
        gtmp = sb("gtmp", [128, H, NGLOB])
        rden = sb("rden", [128, S])
        attT = sb("attT", [128, S])
        ckbd = [sb(f"ckbd{i}", [128, PAIRS, 2, M], BF16) for i in range(2)]
        cvbd = [sb(f"cvbd{i}", [128, PAIRS, 32]) for i in range(2)]
        hT = sb("hT", [128, 2, S])

        aheadb = sb("aheadb", [128, 256], BF16)
        rw_rows = sb("rw_rows", [NE, E])
        rwT = sb("rwT", [E, NE])
        sh_rows = sb("sh_rows", [128, 6, 128])
        shT = sb("shT", [128, 6, 128])
        wd = kbd[0][:, :, :, :, :].rearrange("p j n a k -> p (j n a k)").bitcast(F32).rearrange("p (e c) -> p e c", c=E)
        zero_rows = sb("zero_rows", [128, E])
        st3, mv3 = sb("st3", [128, 2, 6]), sb("mv3", [128, 2, 2])
        veps3, rstd3 = sb("veps3", [128, 2]), sb("rstd3", [128, 2])
        xn3 = [sb(f"xn3_{i}", [128, 2, E]) for i in range(2)]
        x3s = sb("x3s", [128, S])
        logits = sb("logits", [128, 2, NE])
        top8 = sb("top8", [128, 2, 8])
        topi = sb("topi", [128, 2, 8], U32)
        topf = sb("topf", [128, 2, TOPK])
        onehot = sb("onehot", [128, NT, TOPK, NE])
        topv = sb("topv", [128, NT, TOPK])
        both = sb("both", [128, 2, NE], BF16)
        rowpos = sb("rowpos", [128, 2, NE])
        picked = sb("picked", [128, 2, TOPK, NE])
        slotf = sb("slotf", [128, NT, TOPK])
        sloti = [sb(f"sloti{i}", [128, 2 * TOPK], I32) for i in range(2)]
        used = [sb(f"used{i}", [128, NE]) for i in range(2)]
        plan = sb("plan", [128, 8, NE])
        plani = sb("plani", [128, 2, NE], I32)
        tile_of = sb("tile_of", [128, 4])
        tails = sb("tails", [1, NE], I32)
        tile_row = sb("tile_row", [1, 2, 128], I32)
        back = sb("back", [128, NT * TOPK])
        backi = sb("backi", [128, NT * TOPK], I32)
        picked_all = sb("picked_all", [128, NT * TOPK, NE])
        gate = sb("gate", [128, NT * TOPK])
        xt = [sb(f"xt{i}", [128, E]) for i in range(2)]
        xtT = [sb(f"xtT{i}", [E, 128]) for i in range(2)]
        sg = [sb(f"sg{i}", [128, ED]) for i in range(2)]
        eh = [sb(f"eh{i}", [128, ED]) for i in range(2)]
        ehT = [sb(f"ehT{i}", [ED, 128]) for i in range(2)]
        ey = [sb(f"ey{i}", [128, E]) for i in range(2)]
        sgs = probs[:, 0:4, :].rearrange("p (c i) n -> p c (i n)", c=2)
        shs = probs[:, 4:8, :].rearrange("p (c i) n -> p c (i n)", c=2)
        idx = [sb(f"idx{i}", [128, 4], I32) for i in range(2)]
        yrow = [sb(f"yrow{i}", [128, 4, E]) for i in range(2)]

        CV_BANKS = (2, 3, 6, 7)
        PS = [ctx.enter_context(nc.psum_tensor(f"ps{i}", [128, 512], F32)) for i in range(8)]
        A0, A1, MISC = PS[0], PS[1], PS[7]
        P1, P2, OD = PS[2:4], PS[4:6], PS[6]

        ck_scr = nc.dram_tensor("ck_scr", (NP, 2 * D, PAIRS, 2 * B * M), BF16, kind="Internal").ap()

        xs = nc.dram_tensor("expert_in", (NE * CAP + 128, E), F32, kind="Internal").ap()
        ys = nc.dram_tensor("expert_out", (TILES * 128, E), F32, kind="Internal").ap()

        def loop2(eng, body, n):
            for k in (0, 1):
                body(k, 0, k)
            with eng.Fori(1, n // 2 - 1) as i:
                for k in (0, 1):
                    body(2 * i + k, i, k)
            for k in (0, 1):
                body(n - 2 + k, n // 2 - 1, k)

        def skewed(eng, stages, n):
            most = max(lag for _, lag in stages)
            lead = 2 * ((most + 3) // 2)

            def at(k, i, q, from_, to):
                for f, lag in stages:
                    if from_ is None or from_ <= k - lag < to:
                        f(k - lag, i - (lag + 1 - q) // 2 if lag else i, (q - lag) % 2)

            for k in range(lead):
                at(k, k // 2, k % 2, 0, n)
            with eng.Fori(lead // 2, n // 2) as i:
                for q in (0, 1):
                    at(2 * i + q, i, q, None, None)
            for k in range(n, n + most):
                at(k, k // 2, k % 2, 0, n)

        def loop(eng, body):
            body(0, 0, True, True)
            body(1, 1, True, True)
            with eng.Fori(1, B // 2 - 1) as i:
                body(2 * i, 0, True, True)
                body(2 * i + 1, 1, True, True)
            body(B - 2, 0, True, False)
            body(B - 1, 1, False, False)

        def routed(b):
            return "C" in phases and (not isinstance(b, int) or 0 <= b < B)

        def wait_apart(eng, *waits):
            held = [(sem, v if isinstance(v, int) else eng.to_reg(v)) for sem, v in waits]
            eng.wait_ge(w_("began"), 1)
            for sem, v in held:
                at_least(eng, sem, v)

        GOT = {True: 16 * 2 * NP, False: 16 * (NP + 2)}

        block = ctx.enter_context(nc.Block())

        @block.sync
        def _(sp):
            def load(dst, src, sem="weights", **how):
                sp.dma_start(dst, src, **how).then_inc(w_(sem), 16)

            xv = t["x"].rearrange("b (u p) c -> p (b u) c", p=128)
            load(X[:, 0:2, :], xv[:, 0:2, :], "x_first")
            vec = lambda name: t[name].rearrange("(p o) -> p o", o=1)
            of_rows = lambda name: t[name].rearrange("(j r) -> r j", j=PAIRS)

            load(constants[:, :], t["constants"])
            load(w_raw[:, 0, :], t["L0_attn_Wq"])
            load(w_raw[:, 1, :], t["L0_attn_Wk"])
            load(cols[:, 0:1], of_rows("L0_attn_bq"), allow_slow_non_contiguous=True)
            load(cols[:, 1:2], of_rows("L0_attn_bk"), allow_slow_non_contiguous=True)
            load(wv[:, :], t["L0_attn_Wv"])
            load(ctx_rows[:, :, :], t["ctx_768"].rearrange("b m c -> (b m) c").rearrange("(u p) c -> p u c", p=128), "later")
            load(w_raw[0:EC, 3, :], t["L0_xattn_Wk"], "later")
            load(w_raw[:, 2, :], t["L0_xattn_Wq"], "later")
            load(cols[:, 3:4], of_rows("L0_xattn_bq"), "later", allow_slow_non_contiguous=True)
            load(cols[:, 4:5], of_rows("L0_xattn_bk"), "later", allow_slow_non_contiguous=True)
            for dst, name in ((wo, "L0_attn_Wo"), (cwv, "L0_xattn_Wv"), (cw1, "L0_xattn_W1")):
                load(dst[:, :], t[name], "later")
            load(cols[:, 2:3], vec("L0_attn_bv"), "later")
            load(cols[:, 5:6], vec("L0_xattn_bv"), "later")
            load(cols[:, 6:8], t["L0_xattn_b1"].rearrange("(i p) -> p i", p=128), "later", allow_slow_non_contiguous=True)
            load(rows[:, 0, :], t["L0_attn_bo"].rearrange("(o n) -> o n", o=1).to_broadcast([128, E]), "later")
            load(X[:, 2:NT, :], xv[:, 2:NT, :], "x_rest")
            load(rows[:, 1, :], t["L0_xattn_b2"].rearrange("(o n) -> o n", o=1).to_broadcast([128, E]), "later")
            load(cw2[:, :, :], t["L0_xattn_W2"].rearrange("(c p) n -> p c n", p=128), "later")
            load(rw_rows[:, :], t["L0_ffn_router_w"], "later")
            for i, name in enumerate(("gate", "up")):
                load(sh_rows[:, 2 * i:2 * i + 2, :], t[f"L0_ffn_shared_{name}_w"].rearrange("(k p) c -> p k c", p=128), "later")
            load(sh_rows[:, 4:6, :], t["L0_ffn_shared_down_w"].rearrange("p (k s) -> p k s", k=2), "later")

            sp.wait_ge(w_("ckpart"), 3)
            for i, k in enumerate(K_PART):
                sp.dma_start(ck_scr[i].rearrange("r j n -> (r j) n"), ckpart[:, k].rearrange("p b a k -> p (b a k)")).then_inc(w_("ck_put"), 16)

            def regroup(s, b, p, keys):
                at = 0 if keys else S * p
                at_least(sp, s("pair"), 4 * (b - 1))
                for k in range(3):
                    sp.wait_ge(s("part"), 3 * b + k + 1)
                    for i in range(NP):
                        if Q_PART[i] == k:
                            sp.dma_start(qs[p][16 * i:16 * i + 16, :, :], part[:, k, at:at + S]).then_inc(s("got"), 16)
                        if keys and K_PART[i] == k:
                            sp.dma_start(kbd[p][16 * i:16 * i + 16].rearrange("r j n a k -> r j (n a k)"),
                                         part[:, k, S:3 * S]).then_inc(s("got"), 16)
                    if k == 0 and not keys:
                        sp.dma_start(ckbd[p][0:KROWS, :, :, :].rearrange("r j a k -> r j (a k)"),
                                     ck_scr[:, :, :, bass.ds(2 * M * b, 2 * M)].rearrange("i r j n -> (i r) j n")).then_inc(s("got"), 16)
                        at_least(sp, s("od"), b - 1)
                        sp.dma_start(cvbd[p][:, :, :], cvbd_all[:, bass.ds(b, 1), :, :].squeeze(1)).then_inc(s("got"), 16)
                wait_apart(sp, (s("got"), GOT[keys] * b + GOT[keys]))

            regroup(s_, 0, 0, True)
            sp.wait_ge(w_("ck_put"), 16 * NP)
            load(wgu[:, :, :], t["L0_ffn_gate_up_w"].rearrange("e c h -> c e h"), "experts")
            loop(sp, lambda b, p, one, two: one and regroup(s_, b + 1, 1 - p, True))
            if "B" in phases:
                sp.wait_ge(w_("cv"), 8)
                regroup(c_, 0, 0, False)
                sp.wait_ge(s_("pair"), 4 * B)
                load(wd, t["L0_ffn_down_w"].rearrange("e c h -> c e h"), "experts")
                loop(sp, lambda b, p, one, two: one and regroup(c_, b + 1, 1 - p, False))
            ov = out.rearrange("b (u p) c -> p (b u) c", p=128)
            if "C" not in phases:
                sp.wait_ge((c_ if "B" in phases else s_)("x_new"), B)
                sp.dma_start(ov, X[:, :, :]).then_inc(w_("stored"), 16)
                sp.wait_ge(w_("stored"), 16)
                return

            sp.wait_ge(r_("tails"), 1)
            sp.wait_ge(r_("sent"), 64 * B)
            sp.dma_start(xs[NE * CAP:NE * CAP + 128, :], zero_rows[:, :]).then_inc(e_("zeros"), 16)
            with sp.Fori(0, NE) as i:
                end = sp.value_load(tails[0:1, bass.ds(i, 1)], min_val=0, max_val=NE * CAP - 128)
                sp.dma_start(xs[bass.ds(end, 128), :], zero_rows[:, :]).then_inc(e_("zeros"), 16)
            sp.wait_ge(e_("zeros"), 16 * (NE + 1))
            sp.wait_ge(e_("tile_row"), 1)

            def tile_in(k, i, p):
                at_least(sp, e_("xT_ps"), k - 1)
                first = sp.value_load(tile_row[0:1, 0, bass.ds(k, 1)], min_val=0, max_val=NE * CAP)
                sp.dma_start(xt[p][:, :], xs[bass.ds(first, 128), :]).then_inc(e_(f"in{p}"), 16)

            loop2(sp, tile_in, TILES)

            def store(b, i, p):
                sp.wait_ge(g_("x_out"), b + 1)
                sp.dma_start(ov[:, bass.ds(2 * b, 2), :], X[:, bass.ds(2 * b, 2), :]).then_inc(w_("stored"), 16)

            loop2(sp, store, B)
            sp.wait_ge(w_("stored"), 16 * B)

        @block.gpsimd
        def _(pool):
            g = nc.gpsimd

            def rstd_of(s, b, mv=mv, veps=veps, rstd=rstd):
                wait_apart(pool, (s("aggr"), 2 * b + 2), (s("norm"), 2 * b))
                g.tensor_scalar(veps[:, :], mv[:, :, 1], EPS, None, ALU.add).then_inc(s("veps"), 1)
                pool.wait_ge(s("veps"), b + 1)
                g.tensor_tensor(rstd[:, :], veps[:, :], minus_half[:, :], ALU.pow).then_inc(s("rstd"), 1)

            g.memset(minus_half[:, :], -0.5).then_inc(w_("began"), 1)
            for p in range(2):
                g.memset(vbd[p][:, :, :, :], 0.0)
            g.memset(cvbd_all[:, :, :, :], 0.0).then_inc(w_("zeroed"), 1)
            for p in range(2):
                g.memset(qkz[p][:, S:3 * S], 0.0)
            g.memset(ck32, 0.0).then_inc(w_("zeroed"), 1)
            pool.wait_ge(w_("zeroed"), 2)
            pool.wait_ge(w_("weights"), 16 * W_LOADS)
            def order(i, w):
                n = w.shape[0]
                g.tensor_copy(w[:, :].rearrange("c (r j) -> c r j", j=PAIRS),
                              w_raw[0:n, i, :].rearrange("c (j r) -> c r j", j=PAIRS)).then_inc(w_("ordered"), 1)

            order(0, wq)
            order(1, wk)
            g.tensor_copy(identb[:, :], ident).then_inc(w_("ordered"), 1)
            rstd_of(s_, 0)
            def add_bias(s, b, bias):
                pool.wait_ge(s("norm"), 2 * b + 2)
                g.tensor_tensor(X[:, bass.ds(2 * b, 2), :], X[:, bass.ds(2 * b, 2), :],
                                bias.unsqueeze(1).to_broadcast([128, 2, E]), ALU.add).then_inc(s("x_biased"), 1)

            def self_start(b, p):
                wait_apart(pool, (s_("xnT"), b + 1), (s_("vtok_ps"), b))
                for first, step, n, to in RUNS:
                    last = g.tensor_copy(xg[:, :, to:to + n],
                                         xnT[:, first:first + step * (n - 1) + 1:step].unsqueeze(1).to_broadcast([128, H, n]))
                last.then_inc(s_("xg"), 1)
                pool.wait_ge(s_("qk32"), 4 * b + 4)
                for dst, of in ((kg, k32), (qg, qkz)):
                    for first, step, n, to in RUNS:
                        src = of[p][:, first:first + step * (n - 1) + 1:step]
                        last = g.tensor_tensor(dst[p][:, :, to:to + n], src.unsqueeze(1).to_broadcast([128, H, n]),
                                               head_of_row[:, :].unsqueeze(2).to_broadcast([128, H, n]), ALU.mult)
                    last.then_inc(s_("kgqg"), 1)

            def self_body(b, p, one, two):
                if one:
                    self_start(b + 1, 1 - p)
                    add_bias(s_, b + 1, bo_[:, :])
                if two:
                    rstd_of(s_, b + 2)
                pool.wait_ge(s_("gexp"), b + 1)
                v = probs_g[:, :].rearrange("p (n q) -> p n q", n=NB)
                g.tensor_tensor(v, v, outside[:, :].unsqueeze(2).to_broadcast([128, NB, BLOCK]), ALU.mult).then_inc(s_("gmasked"), 1)
                wait_apart(pool, (s_("gq_rcp"), b + 1))
                g.tensor_scalar(pgq[:, :], pgq[:, :], gstat[:, 3:4], None, ALU.mult).then_inc(s_("gq_norm"), 1)

            self_start(0, 0)
            pool.wait_ge(w_("later"), 16 * W_LATER)
            order(2, cwq)
            order(3, cwk)
            rstd_of(s_, 1)
            pool.wait_ge(s_("rstd"), 2)
            sel = held["shift_pair"][SHIFT:128].rearrange("p (j a) -> p j a", a=2).unsqueeze(3)
            for p in range(2):
                for n in range(NB):
                    g.tensor_copy(kbd[p][SHIFT:128, :, n, :, :], sel.to_broadcast([32, PAIRS, 2, BLOCK]))
                g.tensor_copy(ckbd[p][SHIFT:128, :, :, :], sel.to_broadcast([32, PAIRS, 2, M]))
            g.tensor_copy(shift_glob[SHIFT:128, :], held["shift_glob"][SHIFT:128]).then_inc(w_("set"), 1)
            pool.wait_ge(w_("set"), 1)

            g.tensor_copy(aheadb[:, :], ahead[:, :]).then_inc(w_("set"), 1)
            g.memset(zero_rows[:, :], 0.0).then_inc(w_("set"), 1)
            g.tensor_copy(used[0][:, :], experts[:, NE:2 * NE]).then_inc(w_("set"), 1)
            pool.wait_ge(w_("bo_"), 1)
            add_bias(s_, 0, bo_[:, :])
            loop(pool, self_body)

            if "B" in phases:
                def scatter(b, p):
                    wait_apart(pool, (r_("slot"), b + 1), (r_("sent"), 64 * b))
                    for u in range(2):
                        for k in range(TOPK):
                            pool.indirect_dma_start(xs, bass.IndirectOffsetOnAxis(sloti[p][:, 2 * u + k:2 * u + k + 1], 0),
                                                    xn3[p][:, u, :], None).then_inc(r_("sent"), 16)

                def route(b, p):
                    if routed(b - 1):
                        rstd_of(r_, b - 1, mv3, veps3, rstd3)
                    if routed(b - 2):
                        scatter(b - 2, p)

                def cross_body(b, p, one, two):
                    add_bias(c_, b, rows[:, 1, :])
                    if two:
                        rstd_of(c_, b + 2)
                    route(b, p)

                rstd_of(c_, 0)
                rstd_of(c_, 1)
                loop(pool, cross_body)
                route(B, 0)
                route(B + 1, 1)

            if "C" in phases:
                pool.wait_ge(g_("backi"), 1)
                for q in range(2):
                    pool.wait_ge(e_(f"out{q}"), 16 * (TILES // 2))

                def gather(b, i, p):
                    wait_apart(pool, (g_("x_out"), b - 1))
                    g.tensor_copy(idx[p][:, :], backi[:, bass.ds(4 * b, 4)]).then_inc(g_("idx"), 1)
                    wait_apart(pool, (g_("idx"), b + 1))
                    for k in range(4):
                        pool.indirect_dma_start(yrow[p][:, k, :], None, ys,
                                                bass.IndirectOffsetOnAxis(idx[p][:, k:k + 1], 0)).then_inc(g_(f"got{p}"), 16)

                loop2(pool, gather, B)

        @block.vector
        def _(dve):
            v = nc.vector
            def context_parts():
                dve.wait_ge(w_("bias_ps"), 1)
                v.tensor_tensor(bo_[:, :], MISC[:, 0:E], rows[:, 0, :], ALU.add).then_inc(w_("bo_"), 1)
                v.tensor_tensor(cb1_[:, :], MISC[:, E:E + 2], cols[:, 6:8], ALU.add).then_inc(w_("bo_"), 1)
                dve.wait_ge(w_("ck32"), 4)
                v.tensor_copy(ckpart[:, 0], ck32).then_inc(w_("ckpart"), 1)
                dve.wait_ge(w_("ckpart"), 1)
                v.tensor_tensor(ckres, ck32, ckpart[:, 0], ALU.subtract).then_inc(w_("ckres"), 1)
                dve.wait_ge(w_("ckres"), 1)
                v.tensor_copy(ckpart[:, 1], ckres).then_inc(w_("ckpart"), 1)
                dve.wait_ge(w_("ckpart"), 2)
                v.tensor_tensor(ckpart[:, 2], ckres, ckpart[:, 1], ALU.subtract).then_inc(w_("ckpart"), 1)

            def stats(s, b, arrived, st=st, mv=mv):
                arrived(b)
                for u in range(2):
                    v.bn_stats(st[:, u, :], X[:, bass.ds(2 * b + u, 1), :].squeeze(1)).then_inc(s("stats"), 1)
                for u in range(2):
                    wait_apart(dve, (s("stats"), 2 * b + u + 1), (s("veps"), b))
                    v.bn_aggr(mv[:, u, :], st[:, u, :]).then_inc(s("aggr"), 1)

            def normalise(s, b):
                dve.wait_ge(s("rstd"), b + 1)
                at_least(dve, s("xT_ps"), b)
                for u in range(2):
                    v.tensor_scalar(xn[:, u, :], X[:, bass.ds(2 * b + u, 1), :].squeeze(1), mv[:, u, 0:1], rstd[:, u:u + 1],
                                    ALU.subtract, ALU.mult).then_inc(s("norm"), 1)

            def split(s, b, p, n, per, got, at=0):
                dve.wait_ge(s("qk32"), per * b + per)
                at_least(dve, s("got"), got)
                src, r = qkz[p][:, 0:n], res[:, 0:n]
                into = part[:, :, at:at + n]
                v.tensor_copy(into[:, 0, :], src).then_inc(s("part"), 1)
                dve.wait_ge(s("part"), 3 * b + 1)
                v.tensor_tensor(r, src, into[:, 0, :], ALU.subtract).then_inc(s("res"), 1)
                dve.wait_ge(s("res"), b + 1)
                v.tensor_copy(into[:, 1, :], r).then_inc(s("part"), 1)
                dve.wait_ge(s("part"), 3 * b + 2)
                v.tensor_tensor(into[:, 2, :], r, into[:, 1, :], ALU.subtract).then_inc(s("part"), 1)

            def row_max(s, b, u, half):
                use = 4 * b + 2 * u + half
                dve.wait_ge(s("scores"), use + 1)
                bank = P1[half]
                v.tensor_reduce(nmax[:, u, 8 * half:8 * half + 8], bank[:, :].rearrange("p (h k) -> p h k", k=64),
                                AX.X, ALU.max, negate=True).then_inc(s("nmax"), 1)

            def shift_rows(s, b, p):
                at_least(dve, s("mT_ps"), b)
                v.tensor_copy(mparts[:, :, 0, :], nmax[:, :, :]).then_inc(s("mpart"), 1)
                dve.wait_ge(s("mpart"), 2 * b + 1)
                v.tensor_tensor(mparts[:, :, 1, :], nmax[:, :, :], mparts[:, :, 0, :], ALU.subtract).then_inc(s("mpart"), 1)

            def shift_spread(s, b, p):
                dve.wait_ge(s("mT_ps"), b + 1)
                v.tensor_copy(qs[p][SHIFT:128, 0, :], P1[1][:, :].bitcast(BF16)[SHIFT:128, 0:S]).then_inc(s("mT"), 1)
                dve.wait_ge(s("mT"), 3 * b + 1)
                for j, to in ((1, 4), (4, PAIRS)):
                    v.tensor_copy(qs[p][SHIFT:128, j:to, :], qs[p][SHIFT:128, 0:1, :].to_broadcast([32, to - j, S])).then_inc(s("mT"), 1)

            def attended(s, b):
                dve.wait_ge(s("od"), b + 1)
                v.reciprocal(rden[:, :], OD[:, S:2 * S]).then_inc(s("rden"), 1)
                dve.wait_ge(s("rden"), b + 1)
                v.tensor_tensor(attT[:, :], OD[:, 0:S], rden[:, :], ALU.mult).then_inc(s("attT"), 1)

            def self_arrived(b):
                if isinstance(b, int) and b == 0:
                    dve.wait_ge(w_("x_first"), 16)
                elif isinstance(b, int) and b == 1:
                    dve.wait_ge(w_("x_rest"), 16)

            def self_split(b, p):
                split(s_, b, p, 3 * S, 4, GOT[True] * b)

            def self_vg(b, p):
                dve.wait_ge(s_("vtok_ps"), b + 1)
                v.tensor_tensor(vg[p][:, :], A1[:, 2 * E:3 * E], same_head[:, :], ALU.mult).then_inc(s_("vg"), 1)

            def self_end(b):
                dve.wait_ge(s_("wo_ps"), b + 1)
                dve.wait_ge(s_("x_biased"), b + 1)
                xb = X[:, bass.ds(2 * b, 2), :]
                v.tensor_tensor(xb, OD[:, 0:2 * E].rearrange("p (u c) -> p u c", u=2), xb, ALU.add).then_inc(s_("x_new"), 1)

            def self_body(b, p, one, two):
                row_max(s_, b, 0, 0)
                row_max(s_, b, 0, 1)
                row_max(s_, b, 1, 0)
                row_max(s_, b, 1, 1)
                dve.wait_ge(s_("scores_g"), b + 1)
                v.tensor_reduce(nmaxg[:, :, :], P2[1][:, 0:2 * 128].rearrange("p (h k) -> p h k", k=NGLOB),
                                AX.X, ALU.max, negate=True).then_inc(s_("nmaxg"), 1)
                dve.wait_ge(s_("nmaxg"), b + 1)
                dve.wait_ge(s_("nmax"), 4 * b + 4)
                v.tensor_tensor(nmax[:, :, :], nmax[:, :, :], nmaxg[:, :, :], ALU.min).then_inc(s_("nmaxall"), 1)
                dve.wait_ge(s_("nmaxall"), b + 1)
                shift_rows(s_, b, p)
                dve.wait_ge(s_("gq_ps"), b + 1)
                v.tensor_reduce(gstat[:, 0:1], MISC[:, 0:S], AX.X, ALU.max, negate=True).then_inc(s_("gq_max"), 1)
                dve.wait_ge(s_("gq_max"), b + 1)
                v.tensor_scalar(gstat[:, 1:2], gstat[:, 0:1], SCALE, None, ALU.mult).then_inc(s_("gq_bias"), 1)
                shift_spread(s_, b, p)
                if not isinstance(b, int) or b > 0:
                    self_end(b - 1)
                if one:
                    self_split(b + 1, 1 - p)
                if two:
                    stats(s_, b + 2, self_arrived)
                dve.wait_ge(s_("gq_exp"), b + 1)
                v.reciprocal(gstat[:, 3:4], gstat[:, 2:3]).then_inc(s_("gq_rcp"), 1)
                if one:
                    self_vg(b + 1, 1 - p)
                if two:
                    normalise(s_, b + 2)
                attended(s_, b)
                dve.wait_ge(s_("gq_o"), b + 1)
                v.tensor_tensor(gtmp[:, :, :], MISC[:, 0:128].rearrange("p (h g) -> p h g", g=NGLOB),
                                same_head[:, ::D].unsqueeze(2).to_broadcast([128, H, NGLOB]), ALU.mult).then_inc(s_("gtmp"), 1)
                dve.wait_ge(s_("gtmp"), b + 1)
                dve.wait_ge(s_("attT"), b + 1)
                for first, step, n, to in RUNS:
                    last = v.tensor_reduce(attT[:, first:first + step * (n - 1) + 1:step],
                                           gtmp[:, :, to:to + n].rearrange("p h g -> p g h"), AX.X, ALU.add)
                last.then_inc(s_("att_all"), 1)

            stats(s_, 0, self_arrived)
            normalise(s_, 0)
            self_split(0, 0)
            self_vg(0, 0)
            stats(s_, 1, self_arrived)
            normalise(s_, 1)
            context_parts()
            loop(dve, self_body)
            self_end(B - 1)

            if "B" in phases:
                def cross_arrived(b):
                    dve.wait_ge(s_("x_new"), b + 1)

                def cross_end(b):
                    dve.wait_ge(c_("y_ps"), b + 1)
                    dve.wait_ge(c_("x_biased"), b + 1)
                    xb = X[:, bass.ds(2 * b, 2), :]
                    v.tensor_tensor(xb, OD[:, 0:2 * E].rearrange("p (u c) -> p u c", u=2), xb, ALU.add).then_inc(c_("x_new"), 1)

                number = experts[:, 0:NE]

                def route_normalise(b, p):
                    dve.wait_ge(r_("rstd"), b + 1)
                    at_least(dve, r_("sent"), 64 * (b - 1))
                    for u in range(2):
                        v.tensor_scalar(xn3[p][:, u, :], X[:, bass.ds(2 * b + u, 1), :].squeeze(1), mv3[:, u, 0:1],
                                        rstd3[:, u:u + 1], ALU.subtract, ALU.mult).then_inc(r_("norm"), 1)

                def route_pick(b):
                    wait_apart(dve, (r_("logits"), b + 1))
                    for u in range(2):
                        v.max(top8[:, u, :], logits[:, u, :]).then_inc(r_("top"), 1)
                    for u in range(2):
                        wait_apart(dve, (r_("top"), 2 * b + u + 1))
                        v.max_index(topi[:, u, :], top8[:, u, :], logits[:, u, :]).then_inc(r_("topi"), 1)
                    v.tensor_copy(topv[:, bass.ds(2 * b, 2), :], top8[:, :, 0:TOPK]).then_inc(r_("topv"), 1)
                    dve.wait_ge(r_("topi"), 2 * b + 2)
                    v.tensor_copy(topf[:, :, :], topi[:, :, 0:TOPK]).then_inc(r_("topf"), 1)
                    dve.wait_ge(r_("topf"), b + 1)
                    for u in range(2):
                        v.tensor_tensor(onehot[:, bass.ds(2 * b + u, 1), :, :].squeeze(1), number.unsqueeze(1).to_broadcast([128, TOPK, NE]),
                                        topf[:, u, :].unsqueeze(2).to_broadcast([128, TOPK, NE]), ALU.is_equal).then_inc(r_("onehot"), 1)
                    dve.wait_ge(r_("onehot"), 2 * b + 2)
                    oh = onehot[:, bass.ds(2 * b, 2), :, :]
                    v.tensor_tensor(both[:, :, :], oh[:, :, 0, :], oh[:, :, 1, :], ALU.add).then_inc(r_("both"), 1)

                def route_slots(b, p):
                    dve.wait_ge(r_("count_ps"), b + 1)
                    v.tensor_tensor(rowpos[:, :, :], MISC[:, 0:2 * NE].rearrange("p (u e) -> p u e", e=NE),
                                    used[p][:, :].unsqueeze(1).to_broadcast([128, 2, NE]), ALU.add).then_inc(r_("rowpos"), 1)
                    v.tensor_tensor(used[1 - p][:, :], MISC[:, 2 * NE:3 * NE], used[p][:, :], ALU.add).then_inc(r_("used"), 1)
                    dve.wait_ge(r_("rowpos"), b + 1)
                    for u in range(2):
                        v.tensor_tensor(picked[:, u, :, :], onehot[:, bass.ds(2 * b + u, 1), :, :].squeeze(1),
                                        rowpos[:, u, :].unsqueeze(1).to_broadcast([128, TOPK, NE]), ALU.mult).then_inc(r_("picked"), 1)
                    dve.wait_ge(r_("picked"), 2 * b + 2)
                    sl = slotf[:, bass.ds(2 * b, 2), :]
                    v.tensor_reduce(sl, picked[:, :, :, :], AX.X, ALU.add).then_inc(r_("slotf"), 1)
                    wait_apart(dve, (r_("slotf"), b + 1))
                    v.tensor_copy(sloti[p][:, :].rearrange("p (u k) -> p u k", k=TOPK), sl).then_inc(r_("slot"), 1)
                    dve.wait_ge(r_("used"), b + 1)

                def route(b, p, stage):
                    if stage == 0 and routed(b - 2):
                        route_pick(b - 2)
                    if stage == 0 and routed(b - 1):
                        stats(r_, b - 1, lambda b: wait_apart(dve, (c_("x_new"), b + 1)), st3, mv3)
                    if stage == 1 and routed(b - 1):
                        route_normalise(b - 1, 1 - p)
                    if stage == 2 and routed(b - 2):
                        route_slots(b - 2, p)

                def cross_body(b, p, one, two):
                    row_max(c_, b, 0, 0)
                    row_max(c_, b, 0, 1)
                    row_max(c_, b, 1, 0)
                    row_max(c_, b, 1, 1)
                    dve.wait_ge(c_("nmax"), 4 * b + 4)
                    shift_rows(c_, b, p)
                    shift_spread(c_, b, p)
                    if not isinstance(b, int) or b > 0:
                        cross_end(b - 1)
                    if one:
                        split(c_, b + 1, 1 - p, S, 1, GOT[False] * b, (1 - p) * S)
                    route(b, p, 0)
                    if two:
                        stats(c_, b + 2, cross_arrived)
                    if two:
                        normalise(c_, b + 2)
                    route(b, p, 1)
                    attended(c_, b)
                    route(b, p, 2)

                stats(c_, 0, cross_arrived)
                normalise(c_, 0)
                split(c_, 0, 0, S, 1, 0)
                stats(c_, 1, cross_arrived)
                normalise(c_, 1)
                loop(dve, cross_body)
                cross_end(B - 1)
                for stage in range(3):
                    route(B, 0, stage)
                for stage in (0, 2):
                    route(B + 1, 1, stage)

            if "C" in phases:
                COUNT, TL, CUM, MET, NUM, AHEAD, ADJ, ONE = range(8)
                step = [0]

                def then(ins):
                    step[0] += 1
                    ins.then_inc(r_("plan"), 1)
                    dve.wait_ge(r_("plan"), step[0])

                end = used[0]
                v.tensor_copy(tails[0:1, :], end[0:1, :]).then_inc(r_("tails"), 1)
                then(v.tensor_tensor(plan[:, COUNT, :], end[:, :], experts[:, NE:2 * NE], ALU.subtract))
                then(v.tensor_scalar(plani[:, 0, :], plan[:, COUNT, :], 127.0, None, ALU.add))
                then(v.tensor_scalar(plani[:, 1, :], plani[:, 0, :], 7, None, ALU.arith_shift_right))
                then(v.tensor_copy(plan[:, TL, :], plani[:, 1, :]))
                then(v.memset(plan[:, ONE, :], 1.0))
                then(v.tensor_tensor_scan(plan[:, CUM, :], plan[:, ONE, :], plan[:, TL, :], 0.0, ALU.mult, ALU.add))
                then(v.tensor_scalar(plan[:, MET, :], plan[:, CUM, :], experts[:, 2 * NE:2 * NE + 1], None, ALU.is_le))
                then(v.tensor_tensor(plan[:, AHEAD, :], plan[:, MET, :], plan[:, TL, :], ALU.mult))
                then(v.tensor_reduce(tile_of[:, 0:1], plan[:, MET, :], AX.X, ALU.add))
                then(v.tensor_reduce(tile_of[:, 1:2], plan[:, AHEAD, :], AX.X, ALU.add))
                then(v.tensor_tensor(tile_of[:, 2:3], experts[:, 2 * NE:2 * NE + 1], tile_of[:, 1:2], ALU.subtract))
                then(v.tensor_scalar(tile_of[:, 2:3], tile_of[:, 2:3], 128.0, None, ALU.mult))
                then(v.scalar_tensor_tensor(tile_of[:, 2:3], tile_of[:, 0:1], float(CAP), tile_of[:, 2:3], ALU.mult, ALU.add))
                then(v.tensor_scalar(tile_of[:, 2:3], tile_of[:, 2:3], float(NE * CAP), None, ALU.min))
                v.tensor_scalar(tile_of[:, 3:4], tile_of[:, 0:1], float(NE - 1), None, ALU.min).then_inc(e_("tile_of"), 1)
                then(v.tensor_tensor(plan[:, ADJ, :], plan[:, CUM, :], plan[:, TL, :], ALU.subtract))
                then(v.tensor_scalar(plan[:, ADJ, :], plan[:, ADJ, :], 128.0, None, ALU.mult))
                then(v.tensor_tensor(plan[:, ADJ, :], plan[:, ADJ, :], experts[:, NE:2 * NE], ALU.subtract))
                then(v.tensor_tensor(picked_all[:, :, :], onehot[:, :, :, :].rearrange("p t k e -> p (t k) e"),
                                     plan[:, ADJ, :].unsqueeze(1).to_broadcast([128, NT * TOPK, NE]), ALU.mult))
                then(v.tensor_reduce(back[:, :], picked_all[:, :, :], AX.X, ALU.add))
                then(v.tensor_tensor(back[:, :], back[:, :], slotf[:, :, :].rearrange("p t k -> p (t k)"), ALU.add))
                v.tensor_copy(backi[:, :], back[:, :]).then_inc(g_("backi"), 1)
                dve.wait_ge(g_("gate_exp"), 1)
                then(v.tensor_scalar(gate[:, :], gate[:, :], 1.0, None, ALU.add))
                then(v.reciprocal(gate[:, :], gate[:, :]))
                dve.wait_ge(e_("map_ps"), 1)
                v.tensor_copy(tile_row[0:1, :, :], MISC[0:1, 0:256].rearrange("p (i k) -> p i k", i=2)).then_inc(e_("tile_row"), 1)

                def tile(k, i, p):
                    dve.wait_ge(e_("silu"), k + 1)
                    at_least(dve, e_("hT_ps"), k - 1)
                    v.tensor_tensor(eh[p][:, :], PS[2 + p][:, ED:2 * ED], sg[p][:, :], ALU.mult).then_inc(e_("h"), 1)

                def tile_end(k, i, p):
                    dve.wait_ge(e_("y_ps"), k + 1)
                    at_least(dve, e_(f"out{p}"), 16 * i)
                    v.tensor_copy(ey[p][:, :], PS[6 + p][:, 0:E]).then_inc(e_("y"), 1)

                skewed(dve, [(tile, 0), (tile_end, 2)], TILES)

                def shared(u, i, p):
                    for c in range(2):
                        dve.wait_ge(h_("silu"), 2 * u + c + 1)
                        at_least(dve, h_("y_ps"), u)
                        v.tensor_tensor(shs[:, c, :], PS[2 * c + 1][:, :], sgs[:, c, :], ALU.mult).then_inc(h_("h"), 1)
                    dve.wait_ge(h_("y_ps"), u + 1)
                    xu = X[:, bass.ds(4 * u, 4), :]
                    v.tensor_tensor(xu, PS[4 + p][:, :].rearrange("p (t c) -> p t c", t=4), xu, ALU.add).then_inc(h_("x"), 1)

                loop2(dve, shared, B // 2)

                def combine(b, i, p):
                    dve.wait_ge(h_("x"), B // 2)
                    dve.wait_ge(g_(f"got{p}"), 64 * (i + 1))
                    for u in range(2):
                        xu = X[:, bass.ds(2 * b + u, 1), :].squeeze(1)
                        for k in range(TOPK):
                            if k:
                                dve.wait_ge(g_("first"), 2 * b + u + 1)
                            last = v.scalar_tensor_tensor(xu, yrow[p][:, 2 * u + k, :], gate[:, bass.ds(4 * b + 2 * u + k, 1)], xu,
                                                          ALU.mult, ALU.add)
                            if k == 0:
                                last.then_inc(g_("first"), 1)
                    last.then_inc(g_("x_out"), 1)

                loop2(dve, combine, B)

        @block.scalar
        def _(act):
            a_ = nc.scalar
            def context():
                act.wait_ge(w_("ctxT_ps"), 1)
                for i in range(2):
                    a_.copy(ctxT[:, 512 * i:512 * i + 512], PS[2 + i][0:EC, :]).then_inc(w_("ctxT"), 1)
                act.wait_ge(w_("zeroed"), 2)
                for i in range(2):
                    act.wait_ge(w_("ck_ps"), i + 1)
                    for a in range(2):
                        h = slice(64 * a, 64 * a + 64)
                        a_.activation(ck32[h, 8 * i:8 * i + 8, a, :], PS[4 + i][h, :].rearrange("p (b k) -> p b k", k=M), ACT.Identity,
                                      bias=cols[h, 4:5]).then_inc(w_("ck32"), 1)
                for i in range(4):
                    act.wait_ge(w_("cv_ps"), i + 1)
                    value_cells(a_, cvbd_all[:, 4 * i:4 * i + 4, :, :], PS[CV_BANKS[i]], w_("cv"))
                act.wait_ge(w_("turned_ps"), 1)
                a_.copy(rwT[:, :], PS[4][:, 0:NE]).then_inc(w_("turned"), 1)
                for i in range(2):
                    a_.copy(shT[:, 3 * i:3 * i + 3, :], PS[5 + i][:, 0:384].rearrange("p (i c) -> p i c", i=3)).then_inc(w_("turned"), 1)

            def self_start(b, p):
                act.wait_ge(s_("xT_ps"), b + 1)
                at_least(act, s_("vtok_ps"), b)
                a_.copy(xnT[:, :], A0[:, 0:S]).then_inc(s_("xnT"), 1)

            def self_start2(b, p):
                act.wait_ge(s_("qk_ps"), 2 * b + 2)
                a_.activation(qkz[p][:, 0:S], A0[:, 0:S], ACT.Identity, bias=cols[:, 0:1]).then_inc(s_("qk32"), 1)
                kz = qkz[p][:, S:3 * S].rearrange("p (n a k) -> p n a k", a=2, k=BLOCK)
                for a in range(2):
                    h = slice(64 * a, 64 * a + 64)
                    a_.activation(kz[h, :, a, :], A0[h, S:2 * S].rearrange("p (n k) -> p n k", k=BLOCK), ACT.Identity,
                                  bias=cols[h, 1:2]).then_inc(s_("qk32"), 1)
                a_.activation(k32[p][:, :], A0[:, S:2 * S], ACT.Identity, bias=cols[:, 1:2]).then_inc(s_("qk32"), 1)

            def self_start_values(b, p):
                act.wait_ge(s_("vdup_ps"), b + 1)
                value_cells(a_, vbd[p][:, :, :, :], A1, s_("vbd"))

            def self_start3(b, p):
                act.wait_ge(s_("vtok_ps"), b + 1)
                dve_done = s_("vg")
                act.wait_ge(dve_done, b + 1)
                a_.copy(vtok[p][:, :, :], A1[:, 0:2 * E].rearrange("p (u c) -> p u c", u=2)).then_inc(s_("vtok"), 1)

            def exps(s, b):
                for i in range(4):
                    act.wait_ge(s("pair"), 4 * b + i + 1)
                    if i == 0:
                        at_least(act, s("od"), b)
                    a_.activation(probs[:, 2 * i:2 * i + 2, :], P2[i % 2][:, :].rearrange("p (j q) -> p j q", j=2),
                                  ACT.Exp, scale=SCALE).then_inc(s("probs"), 1)

            def self_body(b, p, one, two):
                if one:
                    self_start(b + 1, 1 - p)
                if one:
                    self_start2(b + 1, 1 - p)
                act.wait_ge(s_("gq_bias"), b + 1)
                at_least(act, s_("gq_T"), b)
                a_.activation(pgq[:, :], MISC[:, 0:S], ACT.Exp, bias=gstat[:, 1:2], scale=SCALE,
                              accum_out=gstat[:, 2:3]).then_inc(s_("gq_exp"), 1)
                if one:
                    self_start_values(b + 1, 1 - p)
                exps(s_, b)
                act.wait_ge(s_("gk_ps"), b + 1)
                a_.activation(probs_g[:, :], P2[0][:, 0:S], ACT.Exp, scale=SCALE).then_inc(s_("gexp"), 1)
                if one:
                    self_start3(b + 1, 1 - p)
                act.wait_ge(s_("gq_T"), b + 1)
                a_.copy(pgqT[:, :, :], MISC[:, 0:256].rearrange("p (u c) -> p u c", u=2)).then_inc(s_("pgqT"), 1)

            self_start(0, 0)
            self_start2(0, 0)
            self_start_values(0, 0)
            self_start3(0, 0)
            context()
            loop(act, self_body)

            if "B" in phases:
                def cross_start(b, p):
                    act.wait_ge(c_("xT_ps"), b + 1)
                    a_.copy(xnT[:, :], A0[:, 0:S]).then_inc(c_("xnT"), 1)

                def cross_start2(b, p):
                    act.wait_ge(c_("q_ps"), b + 1)
                    a_.activation(qkz[p][:, 0:S], A0[:, 0:S], ACT.Identity, bias=cols[:, 3:4]).then_inc(c_("qk32"), 1)

                def cross_hidden(b):
                    act.wait_ge(c_("h_ps"), b + 1)
                    for i in range(2):
                        a_.activation(hT[:, i, :], MISC[:, i * S:(i + 1) * S], ACT.Relu, bias=cb1_[:, i:i + 1]).then_inc(c_("h"), 1)

                def route_turn(b):
                    act.wait_ge(r_("xT_ps"), b + 1)
                    at_least(act, r_("logit_ps"), b)
                    a_.copy(x3s[:, :], A1[:, 0:S]).then_inc(r_("xnT"), 1)
                    a_.copy(x3T[:, bass.ds(S * b, S)], A1[:, 0:S]).then_inc(r_("xnT"), 1)

                def route_logits(b):
                    act.wait_ge(r_("logit_ps"), b + 1)
                    at_least(act, r_("topi"), 2 * b)
                    a_.copy(logits[:, :, :], MISC[:, 0:2 * NE].rearrange("p (u e) -> p u e", e=NE)).then_inc(r_("logits"), 1)

                def cross_body(b, p, one, two):
                    if one:
                        cross_start(b + 1, 1 - p)
                    if routed(b - 2):
                        route_turn(b - 2)
                    if not isinstance(b, int) or b > 0:
                        cross_hidden(b - 1)
                    if one:
                        cross_start2(b + 1, 1 - p)
                    if routed(b - 2):
                        route_logits(b - 2)
                    exps(c_, b)

                act.wait_ge(w_("bo_"), 2)
                cross_start(0, 0)
                cross_start2(0, 0)
                loop(act, cross_body)
                cross_hidden(B - 1)
                for b in (B - 2, B - 1):
                    if routed(b):
                        route_turn(b)
                        route_logits(b)

            if "C" in phases:
                act.wait_ge(r_("topv"), B)
                a_.activation(gate[:, :], topv[:, :, :].rearrange("p t k -> p (t k)"), ACT.Exp, scale=-1.0).then_inc(g_("gate_exp"), 1)

                def turn(k, i, p):
                    act.wait_ge(e_("xT_ps"), k + 1)
                    at_least(act, e_("gu_ps"), k - 1)
                    a_.copy(xtT[p][:, :], PS[p][:, 0:128]).then_inc(e_("xtT"), 1)

                def silu(k, i, p):
                    act.wait_ge(e_("gu_ps"), k + 1)
                    at_least(act, e_("h"), k - 1)
                    a_.activation(sg[p][:, :], PS[2 + p][:, 0:ED], ACT.Silu).then_inc(e_("silu"), 1)

                def turn_h(k, i, p):
                    act.wait_ge(e_("hT_ps"), k + 1)
                    at_least(act, e_("y_ps"), k - 1)
                    a_.copy(ehT[p][:, :], PS[4 + p][:, 0:128]).then_inc(e_("ehT"), 1)

                def out_rows(k, i, p):
                    act.wait_ge(e_("y"), k + 1)
                    act.dma_start(ys[bass.ds(128 * k, 128), :], ey[p][:, :]).then_inc(e_(f"out{p}"), 16)

                skewed(act, [(turn, 0), (silu, 1), (turn_h, 2), (out_rows, 4)], TILES)

                def shared(u, i, p):
                    for c in range(2):
                        act.wait_ge(h_("gu_ps"), 2 * u + c + 1)
                        at_least(act, h_("h"), 2 * u)
                        a_.activation(sgs[:, c, :], PS[2 * c][:, :], ACT.Silu).then_inc(h_("silu"), 1)

                loop2(act, shared, B // 2)

        @block.tensor
        def _(pe):
            mm, tr = nc.tensor.matmul, nc.tensor.transpose

            pe.wait_ge(w_("weights"), 16 * W_LOADS)

            def context():
                pe.wait_ge(w_("later"), 16 * W_LATER)
                for i in range(B * M // 128):
                    last = tr(PS[2 + i // 4][0:EC, (i % 4) * 128:(i % 4) * 128 + 128], ctx_rows[:, i, :], ident[:, :])
                last.then_inc(w_("ctxT_ps"), 1)
                mm(MISC[:, 0:E], cols[:, 2:3].to_broadcast([128, 128]), wo[:, :], start=True, stop=True)
                for i in range(2):
                    last = mm(MISC[:, E + i:E + i + 1], cw1[:, i * 128:(i + 1) * 128], cols[:, 5:6], start=True, stop=True)
                last.then_inc(w_("bias_ps"), 1)
                pe.wait_ge(w_("ordered"), 5)
                pe.wait_ge(w_("ctxT"), 2)
                for i in range(2):
                    mm(PS[4 + i][:, :], cwk[:, :], ctxT[:, 512 * i:512 * i + 512], start=True, stop=True).then_inc(w_("ck_ps"), 1)
                for i in range(4):
                    if CV_BANKS[i] == 7:
                        pe.wait_ge(w_("bo_"), 2)
                    for j in range(4):
                        bb = 4 * i + j
                        for a in range(2):
                            last = mm(PS[CV_BANKS[i]][64 * a:64 * a + 64, j * 128:(j + 1) * 128], ctxT[:, bb * M:(bb + 1) * M], cwv[:, :],
                                      start=True, stop=True)
                    last.then_inc(w_("cv_ps"), 1)
                pe.wait_ge(w_("ck32"), 4)
                pe.wait_ge(w_("cv"), 6)
                tr(PS[4][:, 0:NE], rw_rows[:, :], ident[0:NE, 0:NE])
                for i in range(6):
                    last = tr(PS[5 + i // 3][:, (i % 3) * 128:(i % 3) * 128 + 128], sh_rows[:, i, :], ident[:, :])
                last.then_inc(w_("turned_ps"), 1)
                pe.wait_ge(w_("turned"), 3)
                pe.wait_ge(w_("cv"), 8)
                pe.wait_ge(w_("set"), 4)
                pe.wait_ge(w_("bo_"), 2)

            def columns(s, b, free):
                pe.wait_ge(s("norm"), 2 * b + 2)
                at_least(pe, s("qk32"), free * b)
                for u in range(2):
                    last = tr(A0[:, u * 128:(u + 1) * 128], xn[:, u, :], ident[:, :])
                last.then_inc(s("xT_ps"), 1)

            def self_project(b, p):
                pe.wait_ge(s_("xnT"), b + 1)
                for i, w in enumerate((wq, wk)):
                    mm(A0[:, i * S:(i + 1) * S], w[:, :], xnT[:, :], start=True, stop=True).then_inc(s_("qk_ps"), 1)

            def self_values(b):
                at_least(pe, s_("vtok"), b)
                at_least(pe, s_("vg"), b)
                for n in range(NB):
                    for a in range(2):
                        last = mm(A1[64 * a:64 * a + 64, n * E:(n + 1) * E], xnT[:, n * BLOCK:(n + 1) * BLOCK], wv[:, :], start=True, stop=True)
                last.then_inc(s_("vdup_ps"), 1)

            def self_project2(b, p):
                pe.wait_ge(s_("vbd"), 2 * b + 2)
                pe.wait_ge(s_("xg"), b + 1)
                for u in range(2):
                    mm(A1[:, u * E:(u + 1) * E], xnT[:, u * 128:(u + 1) * 128], wv[:, :], start=True, stop=True)
                mm(A1[:, 2 * E:3 * E], xg[:, :, :].rearrange("p h g -> p (h g)"), wv[:, :],
                   start=True, stop=True).then_inc(s_("vtok_ps"), 1)

            def turn_shift(s, b):
                pe.wait_ge(s("mpart"), 2 * b + 2)
                for u in range(2):
                    last = tr(P1[1][:, :].bitcast(BF16)[SHIFT:128, u * 128:(u + 1) * 128],
                              mparts[:, u, :, :].rearrange("p i h -> p (i h)"), identb[:, :])
                last.then_inc(s("mT_ps"), 1)

            def weigh(s, b, p, i, values, blocks):
                pe.wait_ge(s("probs"), 4 * b + i + 1)
                for jj in range(2):
                    j = 2 * i + jj
                    for n in range(blocks):
                        w = S // blocks
                        mm(OD[32 * i:32 * i + 32, n * w:(n + 1) * w], values(n, j), probs[:, j, n * w:(n + 1) * w],
                           start=(jj == 0 and n == 0), stop=False, skip_group_check=True)
                    last = mm(OD[32 * i:32 * i + 32, S:2 * S], key_ones[:, jj, :], probs[:, j, :],
                              start=False, stop=False, skip_group_check=True)
                return last

            def self_out(b):
                pe.wait_ge(s_("att_all"), b + 1)
                for u in range(2):
                    last = mm(OD[:, u * E:(u + 1) * E], attT[:, u * 128:(u + 1) * 128], wo[:, :], start=True, stop=True)
                last.then_inc(s_("wo_ps"), 1)

            def self_body(b, p, one, two):
                if one:
                    columns(s_, b + 1, 4)
                pe.wait_ge(s_("got"), GOT[True] * b + GOT[True])
                for u in range(2):
                    for half in range(2):
                        if u == 0:
                            at_least(pe, s_("mT") if half else s_("nmax"), (3 * b if half else 4 * b))
                        else:
                            pe.wait_ge(s_("nmax"), 4 * b + half + 1)
                        for j in range(4):
                            for i in range(2):
                                n = 2 * u + i
                                last = mm(P1[half][64 * i:64 * i + 64, j * 128:(j + 1) * 128],
                                          qs[p][0:KROWS, 4 * half + j, n * BLOCK:(n + 1) * BLOCK],
                                          kbd[p][0:KROWS, 4 * half + j, n, :, :].rearrange("r a k -> r (a k)"), start=True, stop=True)
                        last.then_inc(s_("scores"), 1)
                pe.wait_ge(s_("kgqg"), 2 * b + 2)
                at_least(pe, s_("probs"), 4 * b)
                for u in range(2):
                    last = mm(P2[1][:, u * 128:(u + 1) * 128], qkz[p][:, u * 128:(u + 1) * 128],
                              kg[p][:, :, :].rearrange("p h g -> p (h g)"), start=True, stop=True)
                last.then_inc(s_("scores_g"), 1)
                at_least(pe, s_("gtmp"), b)
                mm(MISC[:, 0:S], qg[p][:, :, :].rearrange("p h g -> p (h g)"), k32[p][:, :], start=True, stop=True).then_inc(s_("gq_ps"), 1)
                if one:
                    self_project(b + 1, 1 - p)
                turn_shift(s_, b)
                if not isinstance(b, int) or b > 0:
                    self_out(b - 1)
                if one:
                    self_values(b + 1)

                def pair(i):
                    pe.wait_ge(s_("mT"), 3 * b + (2 if i < 2 else 3))
                    for jj in range(2):
                        j = 2 * i + jj
                        for n in range(NB):
                            last = mm(P2[i % 2][:, jj * S + n * BLOCK:jj * S + (n + 1) * BLOCK],
                                      kbd[p][:, j, n, :, :].rearrange("r a k -> r (a k)"), qs[p][:, j, n * BLOCK:(n + 1) * BLOCK],
                                      start=True, stop=True)
                    last.then_inc(s_("pair"), 1)

                values = lambda n, j: vbd[p][:, n, j, :]
                at_least(pe, s_("gexp"), b)
                pair(0)
                pair(1)
                pe.wait_ge(s_("probs"), 4 * b + 1)
                pair(2)
                at_least(pe, s_("x_new"), b)
                weigh(s_, b, p, 0, values, NB)
                pe.wait_ge(s_("probs"), 4 * b + 2)
                pair(3)
                weigh(s_, b, p, 1, values, NB)
                pe.wait_ge(s_("probs"), 4 * b + 3)
                mm(P2[0][:, 0:S], kg[p][:, :, :].rearrange("p h g -> p (h g)"), qkz[p][:, 0:S], start=True, stop=False)
                mm(P2[0][:, 0:S], shift_glob[SHIFT:128, :], qs[p][SHIFT:128, 0, :], start=False, stop=True).then_inc(s_("gk_ps"), 1)
                weigh(s_, b, p, 2, values, NB)
                weigh(s_, b, p, 3, values, NB)
                if one:
                    self_project2(b + 1, 1 - p)
                pe.wait_ge(s_("gmasked"), b + 1)
                mm(OD[:, 0:S], vg[p][:, :], probs_g[:, :], start=False, stop=True, skip_group_check=True)
                mm(OD[:, S:2 * S], same_head[:, :], probs_g[:, :], start=False, stop=True, skip_group_check=True).then_inc(s_("od"), 1)
                pe.wait_ge(s_("gq_norm"), b + 1)
                for u in range(2):
                    last = tr(MISC[:, u * 128:(u + 1) * 128], pgq[:, u * 128:(u + 1) * 128], ident[:, :])
                last.then_inc(s_("gq_T"), 1)
                pe.wait_ge(s_("pgqT"), b + 1)
                for u in range(2):
                    last = mm(MISC[:, 0:128], vtok[p][:, u, :], pgqT[:, u, :], start=(u == 0), stop=(u == 1))
                last.then_inc(s_("gq_o"), 1)

            columns(s_, 0, 4)
            pe.wait_ge(w_("ordered"), 3)
            self_project(0, 0)
            self_values(0)
            self_project2(0, 0)
            context()
            loop(pe, self_body)
            self_out(B - 1)

            if "B" in phases:
                def cross_project(b, p):
                    pe.wait_ge(c_("xnT"), b + 1)
                    mm(A0[:, 0:S], cwq[:, :], xnT[:, :], start=True, stop=True).then_inc(c_("q_ps"), 1)

                def cross_hidden(b):
                    pe.wait_ge(c_("attT"), b + 1)
                    for i in range(2):
                        last = mm(MISC[:, i * S:(i + 1) * S], cw1[:, i * 128:(i + 1) * 128], attT[:, :], start=True, stop=True)
                    last.then_inc(c_("h_ps"), 1)

                def cross_out(b):
                    pe.wait_ge(c_("h"), 2 * b + 2)
                    for u in range(2):
                        for i in range(2):
                            last = mm(OD[:, u * E:(u + 1) * E], hT[:, i, u * 128:(u + 1) * 128], cw2[:, i, :], start=(i == 0), stop=(i == 1))
                    last.then_inc(c_("y_ps"), 1)

                def route_turn(b, p):
                    pe.wait_ge(r_("norm"), 2 * b + 2)
                    at_least(pe, r_("xnT"), 2 * b)
                    for u in range(2):
                        last = tr(A1[:, u * 128:(u + 1) * 128], xn3[p][:, u, :], ident[:, :])
                    last.then_inc(r_("xT_ps"), 1)

                def route_logits(b):
                    pe.wait_ge(r_("xnT"), 2 * b + 2)
                    for u in range(2):
                        last = mm(MISC[:, u * NE:(u + 1) * NE], x3s[:, u * 128:(u + 1) * 128], rwT[:, :], start=True, stop=True)
                    last.then_inc(r_("logit_ps"), 1)

                def route_count(b):
                    pe.wait_ge(r_("both"), b + 1)
                    mm(MISC[:, 0:NE], aheadb[:, 0:128], both[:, 0, :], start=True, stop=True)
                    mm(MISC[:, NE:2 * NE], aheadb[:, 0:128], both[:, 1, :], start=True, stop=False)
                    mm(MISC[:, NE:2 * NE], aheadb[:, 128:256], both[:, 0, :], start=False, stop=True)
                    mm(MISC[:, 2 * NE:3 * NE], aheadb[:, 128:256], both[:, 0, :], start=True, stop=False)
                    mm(MISC[:, 2 * NE:3 * NE], aheadb[:, 128:256], both[:, 1, :], start=False, stop=True).then_inc(r_("count_ps"), 1)

                def cross_body(b, p, one, two):
                    if one:
                        columns(c_, b + 1, 1)
                    pe.wait_ge(c_("got"), GOT[False] * b + GOT[False])
                    for u in range(2):
                        for half in range(2):
                            if u == 0:
                                at_least(pe, c_("mT") if half else c_("nmax"), (3 * b if half else 4 * b))
                            else:
                                pe.wait_ge(c_("nmax"), 4 * b + half + 1)
                            for j in range(4):
                                last = mm(P1[half][:, j * 128:(j + 1) * 128], qs[p][0:KROWS, 4 * half + j, u * 128:(u + 1) * 128],
                                          ckbd[p][0:KROWS, 4 * half + j, :, :].rearrange("r a k -> r (a k)"), start=True, stop=True)
                            last.then_inc(c_("scores"), 1)
                        if u == 0 and (not isinstance(b, int) or b > 0):
                            if routed(b - 3):
                                pe.wait_ge(r_("used"), b - 2)
                            cross_hidden(b - 1)
                    if one:
                        cross_project(b + 1, 1 - p)
                    if not isinstance(b, int) or b > 0:
                        cross_out(b - 1)
                    turn_shift(c_, b)
                    if routed(b - 2):
                        route_logits(b - 2)

                    def pair(i):
                        pe.wait_ge(c_("mT"), 3 * b + (2 if i < 2 else 3))
                        for jj in range(2):
                            j = 2 * i + jj
                            last = mm(P2[i % 2][:, jj * S:(jj + 1) * S], ckbd[p][:, j, :, :].rearrange("p a k -> p (a k)"), qs[p][:, j, :],
                                      start=True, stop=True)
                        last.then_inc(c_("pair"), 1)

                    values = lambda n, j: cvbd[p][:, j, :]
                    at_least(pe, c_("probs"), 4 * b)
                    pair(0)
                    pair(1)
                    pe.wait_ge(c_("probs"), 4 * b + 1)
                    pair(2)
                    at_least(pe, c_("x_new"), b)
                    weigh(c_, b, p, 0, values, 1)
                    pe.wait_ge(c_("probs"), 4 * b + 2)
                    pair(3)
                    for i in range(1, 4):
                        last = weigh(c_, b, p, i, values, 1)
                    last.then_inc(c_("od"), 1)
                    if routed(b - 2):
                        route_count(b - 2)
                    if routed(b - 1):
                        route_turn(b - 1, 1 - p)

                columns(c_, 0, 1)
                cross_project(0, 0)
                pe.wait_ge(s_("x_new"), B)
                loop(pe, cross_body)
                if routed(B - 3):
                    pe.wait_ge(r_("used"), B - 2)
                cross_hidden(B - 1)
                cross_out(B - 1)
                for b in (B - 2, B - 1):
                    if routed(b):
                        if b == B - 1:
                            route_turn(b, 1)
                        at_least(pe, r_("used"), b)
                        route_logits(b)
                        route_count(b)

            if "C" in phases:
                pe.wait_ge(e_("tile_of"), 1)
                pe.wait_ge(c_("h"), 2 * B)
                for i in range(2):
                    last = tr(MISC[0:1, i * 128:(i + 1) * 128], tile_of[:, 2 + i:3 + i], ident[:, :])
                last.then_inc(e_("map_ps"), 1)
                pe.wait_ge(e_("tile_row"), 1)
                pe.wait_ge(w_("experts"), 32)
                pe.wait_ge(c_("y_ps"), B)
                pe.wait_ge(c_("x_new"), B)
                pe.wait_ge(c_("attT"), B)

                def turn(k, i, p):
                    pe.wait_ge(e_(f"in{p}"), 16 * (i + 1))
                    at_least(pe, e_("xtT"), k - 1)
                    tr(PS[p][:, 0:128], xt[p][:, :], ident[:, :]).then_inc(e_("xT_ps"), 1)

                def gate_up(k, i, p):
                    which = pe.value_load(tile_row[0:1, 1, bass.ds(k, 1)], min_val=0, max_val=NE - 1)
                    pe.wait_ge(e_("xtT"), k + 1)
                    at_least(pe, e_("h"), k - 1)
                    mm(PS[2 + p][:, 0:2 * ED], xtT[p][:, :], wgu[:, bass.ds(which, 1), :].squeeze(1), start=True, stop=True).then_inc(e_("gu_ps"), 1)

                def turn_h(k, i, p):
                    pe.wait_ge(e_("h"), k + 1)
                    at_least(pe, e_("ehT"), k - 1)
                    tr(PS[4 + p][:, 0:128], eh[p][:, :], ident[:, :]).then_inc(e_("hT_ps"), 1)

                def down(k, i, p):
                    which = pe.value_load(tile_row[0:1, 1, bass.ds(k, 1)], min_val=0, max_val=NE - 1)
                    pe.wait_ge(e_("ehT"), k + 1)
                    at_least(pe, e_("y"), k - 1)
                    mm(PS[6 + p][:, 0:E], ehT[p][:, :], wd[:, bass.ds(which, 1), :].squeeze(1), start=True, stop=True).then_inc(e_("y_ps"), 1)

                skewed(pe, [(turn, 0), (gate_up, 1), (turn_h, 2), (down, 3)], TILES)
                pe.wait_ge(e_("y"), TILES)

                def shared_in(u, i, p, c):
                    at_least(pe, h_("h"), 2 * (u - 1) + c + 1 if not isinstance(u, int) or u > 0 else 0)
                    for k in range(2):
                        last = mm(PS[2 * c + k][:, :], shT[:, 2 * k + c, :], x3T[:, bass.ds(512 * u, 512)], start=True, stop=True)
                    last.then_inc(h_("gu_ps"), 1)

                def shared_out(u, i, p):
                    pe.wait_ge(h_("h"), 2 * u + 2)
                    at_least(pe, h_("x"), u - 1)
                    for j in range(4):
                        for c in range(2):
                            last = mm(PS[4 + p][:, j * E:(j + 1) * E], shs[:, c, j * 128:(j + 1) * 128], shT[:, 4 + c, :], start=(c == 0), stop=(c == 1))
                    last.then_inc(h_("y_ps"), 1)

                def shared(u, i, p):
                    shared_in(u, i, p, 0)
                    shared_in(u, i, p, 1)
                    shared_out(u, i, p)

                loop2(pe, shared, B // 2)


W_LOADS, W_LATER = 6, 18


def value_cells(eng, dst, bank, sem):
    for a in range(2):
        src = bank[64 * a:64 * a + 64, :].rearrange("p (ng jj a d) -> p ng jj a d", jj=2, a=2, d=D)[:, :, :, a, :]
        full = dst[64 * a:64 * a + 64].rearrange("p n (g jj) c -> p (n g) (jj c)", jj=2)
        for jj in range(2):
            cell = jj * 48 + a * D
            last = eng.copy(full[:, :, cell:cell + D], src[:, :, jj, :])
        last.then_inc(sem, 1)


_INS = ["x", "ctx_768", "L0_attn_Wq", "L0_attn_bq", "L0_attn_Wk", "L0_attn_bk", "L0_attn_Wv", "L0_attn_bv",
        "L0_attn_Wo", "L0_attn_bo", "L0_xattn_Wq", "L0_xattn_bq", "L0_xattn_Wk", "L0_xattn_bk", "L0_xattn_Wv",
        "L0_xattn_bv", "L0_xattn_W1", "L0_xattn_b1", "L0_xattn_W2", "L0_xattn_b2", "L0_ffn_router_w",
        "L0_ffn_gate_up_w", "L0_ffn_down_w", "L0_ffn_shared_gate_w", "L0_ffn_shared_up_w", "L0_ffn_shared_down_w"]


def kernel(**inputs):
    import numpy as _np
    import concourse.bacc as _bacc
    from concourse.bass_utils import run_bass_kernel_spmd as _run

    nc = _bacc.Bacc("TRN2", target_bir_lowering=False, num_devices=1)
    arrays, args = {}, {}
    given = {name: _np.ascontiguousarray(inputs[name]) for name in _INS}
    for name, a in {**given, **shape_constants()}.items():
        arrays[f"in_{name}"] = a
        args[name] = nc.dram_tensor(f"in_{name}", a.shape, mybir.dt.from_np(a.dtype), kind="ExternalInput").ap()
    out = nc.dram_tensor("out_0", (B, S, E), F32, kind="ExternalOutput").ap()
    decoder(nc, args, out)
    r = _run(nc, [arrays], core_ids=[0])
    return r.results[0]["out_0"]
```

```python
import numpy as np
import concourse.bass as bass
from concourse import mybir
from contextlib import ExitStack

F32 = mybir.dt.float32
BF16 = mybir.dt.bfloat16
I32 = mybir.dt.int32
U32 = mybir.dt.uint32
ACT = mybir.ActivationFunctionType
ALU = mybir.AluOpType
AX = mybir.AxisListType

B, S, E = 16, 256, 128
M, EC = 64, 96
H, D = 16, 8
BLOCK, NGLOB = 64, 8
NB = S // BLOCK
PAIRS = H // 2
NT = B * S // 128
NE, TOPK, ED, SD = 16, 2, 128, 256
CAP = B * S + 128
TILES = B * S * TOPK // 128 + NE
EPS = 1e-5
SCALE = 1.0 / float(np.sqrt(D))
GLOBALS = [int(g) for g in np.linspace(0, S - 1, NGLOB)]
RUNS = [(GLOBALS[0], 1, 1, 0), (GLOBALS[1], GLOBALS[3] - GLOBALS[1], 4, 1), (GLOBALS[2], GLOBALS[4] - GLOBALS[2], 3, 5)]
G_ORDER = [a + s * i for a, s, c, _ in RUNS for i in range(c)]
assert sorted(G_ORDER) == GLOBALS
Q_PART = (0, 0, 0, 1, 1, 2)
K_PART = (0, 1, 2, 0, 1, 0)
NP = len(Q_PART)
KROWS = 2 * NP * D
SHIFT = KROWS


def constant_columns():
    p = np.arange(128)
    c = {}
    c["ident"] = np.eye(128)
    c["same_head"] = p[:, None] // D == p[None, :] // D
    c["head_of_row"] = (2 * (p % PAIRS) + p // 64)[:, None] == np.arange(H)[None, :]
    c["outside"] = np.array(G_ORDER)[p % NGLOB][:, None] // BLOCK != np.arange(NB)[None, :]
    c["shift_pair"] = (p % H)[:, None] == np.arange(H)[None, :]
    c["shift_glob"] = (p % H)[:, None] == p[None, :] // D
    o = np.zeros((128, 2, 2, 2, D))
    for jj in range(2):
        for a in range(2):
            o[a * 64:(a + 1) * 64, jj, jj, a] = 1.0
    c["key_ones"] = o.reshape(128, 64)
    e = np.arange(NE)
    c["experts"] = np.concatenate([np.tile(e, (128, 1)), np.tile(e * CAP, (128, 1)), p[:, None]], axis=1)
    c["ahead"] = np.concatenate([(p[:, None] < p[None, :]), np.ones((128, 128))], axis=1)
    return c


def shape_constants():
    return {"constants": np.concatenate(list(constant_columns().values()), axis=1).astype(np.float32)}


def at_least(eng, sem, value):
    if not isinstance(value, int) or value > 0:
        eng.wait_ge(sem, value)


def decoder(nc, t, out, phases="ABC"):
    ctx = ExitStack()
    with ctx:
        def sb(name, shape, dt=F32):
            return ctx.enter_context(nc.sbuf_tensor(name, shape, dt))

        class Sems:
            def __init__(self, prefix):
                self.prefix, self.made = prefix, {}

            def __call__(self, name):
                if name not in self.made:
                    self.made[name] = ctx.enter_context(nc.semaphore(self.prefix + name))
                return self.made[name]

        w_ = Sems("w_")
        s_ = Sems("self_")
        c_ = Sems("cross_")
        r_ = Sems("route_")
        e_ = Sems("expert_")
        h_ = Sems("shared_")
        g_ = Sems("gather_")

        X = sb("x_rows", [128, NT, E])
        constants = sb("constants", list(t["constants"].shape))
        held, at = {}, 0
        for name, a in constant_columns().items():
            held[name] = constants[:, at:at + a.shape[1]]
            at += a.shape[1]
        ident, same_head, outside, head_of_row = (held[n] for n in ("ident", "same_head", "outside", "head_of_row"))
        experts, ahead = held["experts"], held["ahead"]
        shift_pair = held["shift_pair"][SHIFT:128].rearrange("p (j a) -> p j a", a=2).unsqueeze(3)
        key_ones = held["key_ones"].rearrange("p (j c) -> p j c", j=2)
        identb = sb("identb", [128, 128], BF16)
        shift_glob = sb("shift_glob", [128, 128], BF16)
        minus_half = sb("minus_half", [128, 2])
        wq, wk, wv, wo = (sb(n, [E, E]) for n in ("wq", "wk", "wv", "wo"))
        cwq = sb("cwq", [E, E])
        cwk, cwv = sb("cwk", [EC, E]), sb("cwv", [EC, E])
        cw1, cw2 = sb("cw1", [E, 2 * E]), sb("cw2", [128, 2, E])
        cols = sb("cols", [128, 8])
        w_raw = sb("w_raw", [128, 4, E])
        rows = sb("rows", [128, 2, E])
        cb1_ = sb("cb1_", [128, 2])
        bo_ = sb("bo_", [128, E])
        ctx_rows = sb("ctx_rows", [128, B * M // 128, EC])
        ctxT = sb("ctxT", [EC, B * M])
        x3T = sb("x3T", [128, B * S])
        wgu = sb("wgu", [E, NE, 2 * ED])
        ck32 = x3T[:, 0:2 * B * M].rearrange("p (b a k) -> p b a k", a=2, k=M)
        ckres = x3T[:, 2 * B * M:4 * B * M].rearrange("p (b a k) -> p b a k", a=2, k=M)
        ckpart = wgu[:, 0:12, :].rearrange("p e h -> p (e h)").bitcast(BF16).rearrange("p (i b a k) -> p i b a k", i=3, a=2, k=M)
        cvbd_all = sb("cvbd_all", [128, B, PAIRS, 32])

        st = sb("st", [128, 2, 6])
        mv = sb("mv", [128, 2, 2])
        veps = sb("veps", [128, 2])
        rstd = sb("rstd", [128, 2])
        xn = sb("xn", [128, 2, E])
        xnT = sb("xnT", [128, S])
        xg = sb("xg", [128, H, NGLOB])
        qkz = [sb(f"qkz{i}", [128, 3 * S]) for i in range(2)]
        k32 = [sb(f"k32_{i}", [128, S]) for i in range(2)]
        res = sb("res", [128, 3 * S])
        part = sb("part", [128, 3, 3 * S], BF16)
        qs = [sb(f"qs{i}", [128, PAIRS, S], BF16) for i in range(2)]
        kbd = [sb(f"kbd{i}", [128, PAIRS, NB, 2, BLOCK], BF16) for i in range(2)]
        vbd = [sb(f"vbd{i}", [128, NB, PAIRS, 32]) for i in range(2)]
        vtok = [sb(f"vtok{i}", [128, 2, E]) for i in range(2)]
        vg = [sb(f"vg{i}", [128, E]) for i in range(2)]
        kg = [sb(f"kg{i}", [128, H, NGLOB]) for i in range(2)]
        qg = [sb(f"qg{i}", [128, H, NGLOB]) for i in range(2)]
        nmax = sb("nmax", [128, 2, H])
        nmaxg = sb("nmaxg", [128, 2, H])
        mparts = sb("mparts", [128, 2, 2, H], BF16)
        probs = sb("probs", [128, PAIRS, S])
        probs_g = sb("probs_g", [128, S])
        pgq = sb("pgq", [128, S])
        pgqT = sb("pgqT", [128, 2, 128])
        gstat = sb("gstat", [128, 4])
        gtmp = sb("gtmp", [128, H, NGLOB])
        rden = sb("rden", [128, S])
        attT = sb("attT", [128, S])
        ckbd = [sb(f"ckbd{i}", [128, PAIRS, 2, M], BF16) for i in range(2)]
        cvbd = [sb(f"cvbd{i}", [128, PAIRS, 32]) for i in range(2)]
        hT = sb("hT", [128, 2, S])

        aheadb = sb("aheadb", [128, 256], BF16)
        rw_rows = sb("rw_rows", [NE, E])
        rwT = sb("rwT", [E, NE])
        sh_rows = sb("sh_rows", [128, 6, 128])
        shT = sb("shT", [128, 6, 128])
        wd = kbd[0][:, :, :, :, :].rearrange("p j n a k -> p (j n a k)").bitcast(F32).rearrange("p (e c) -> p e c", c=E)
        zero_rows = sb("zero_rows", [128, E])
        st3, mv3 = sb("st3", [128, 2, 6]), sb("mv3", [128, 2, 2])
        veps3, rstd3 = sb("veps3", [128, 2]), sb("rstd3", [128, 2])
        xn3 = [sb(f"xn3_{i}", [128, 2, E]) for i in range(2)]
        x3s = sb("x3s", [128, S])
        logits = sb("logits", [128, 2, NE])
        top8 = sb("top8", [128, 2, 8])
        topi = sb("topi", [128, 2, 8], U32)
        topf = sb("topf", [128, 2, TOPK])
        onehot = sb("onehot", [128, NT, TOPK, NE])
        topv = sb("topv", [128, NT, TOPK])
        both = sb("both", [128, 2, NE], BF16)
        counts = sb("counts", [128, 3, NE])
        rowpos = sb("rowpos", [128, 2, NE])
        slots = sb("slots", [128, 2 * TOPK])
        picked = sb("picked", [128, 2, TOPK, NE])
        slotf = sb("slotf", [128, NT, TOPK])
        sloti = [sb(f"sloti{i}", [128, 2 * TOPK], I32) for i in range(2)]
        used = [sb(f"used{i}", [128, NE]) for i in range(2)]
        plan = sb("plan", [128, 8, NE])
        plani = sb("plani", [128, 2, NE], I32)
        tile_of = sb("tile_of", [128, 4])
        tails = sb("tails", [1, NE], I32)
        tile_row = sb("tile_row", [1, 2, 128], I32)
        back = sb("back", [128, NT * TOPK])
        backi = sb("backi", [128, NT * TOPK], I32)
        picked_all = sb("picked_all", [128, NT * TOPK, NE])
        gate = sb("gate", [128, NT * TOPK])
        xt = [sb(f"xt{i}", [128, E]) for i in range(4)]
        xtT = [sb(f"xtT{i}", [E, 128]) for i in range(2)]
        sg = [sb(f"sg{i}", [128, ED]) for i in range(2)]
        eh = [sb(f"eh{i}", [128, ED]) for i in range(2)]
        ehT = [sb(f"ehT{i}", [ED, 128]) for i in range(2)]
        ey = [sb(f"ey{i}", [128, E]) for i in range(4)]
        sgs = probs[:, 0:4, :].rearrange("p (c i) n -> p c (i n)", c=2)
        shs = probs[:, 4:8, :].rearrange("p (c i) n -> p c (i n)", c=2)
        idx = [sb(f"idx{i}", [128, 4], I32) for i in range(4)]
        yrow = [qs[i // 2][:, 4 * (i % 2):4 * (i % 2) + 4, :].rearrange("p j q -> p (j q)").bitcast(F32)
                .rearrange("p (k c) -> p k c", c=E) for i in range(4)]

        CV_BANKS = (2, 3, 6, 7)
        PS = [ctx.enter_context(nc.psum_tensor(f"ps{i}", [128, 512], F32)) for i in range(8)]
        A0, A1, MISC = PS[0], PS[1], PS[7]
        P1, P2, OD = PS[2:4], PS[4:6], PS[6]

        ck_scr = nc.dram_tensor("ck_scr", (NP, 2 * D, PAIRS, 2 * B * M), BF16, kind="Internal").ap()

        xs = nc.dram_tensor("expert_in", (NE * CAP + 128, E), F32, kind="Internal").ap()
        ys = nc.dram_tensor("expert_out", (TILES * 128, E), F32, kind="Internal").ap()

        def loop2(eng, body, n):
            for k in (0, 1):
                body(k, 0, k)
            with eng.Fori(1, n // 2 - 1) as i:
                for k in (0, 1):
                    body(2 * i + k, i, k)
            for k in (0, 1):
                body(n - 2 + k, n // 2 - 1, k)

        def skewed(eng, stages, n, before=None):
            most = max(lag for _, lag in stages)
            lead = 8 if most else 4

            def at(k, i, q):
                for f, lag in stages:
                    if not isinstance(k, int) or 0 <= k - lag < n:
                        f(k - lag, i - (lag + 3 - q) // 4, (q - lag) % 4)

            for k in range(lead):
                at(k, k // 4, k % 4)
            with eng.Fori(lead // 4, n // 4) as i:
                if before:
                    before(i)
                for q in range(4):
                    at(4 * i + q, i, q)
            for k in range(n, n + most):
                at(k, k // 4, k % 4)

        EARLY = 2

        def later_units(eng, shared, after=None):
            with eng.Fori(EARLY // 2, B // 4) as i:
                for q in (0, 1):
                    shared(2 * i + q, i, q)
                    if after:
                        after(i, q)

        def loop(eng, body, alone=2):
            for b in range(alone):
                body(b, b % 2, True, True)
            with eng.Fori(alone // 2, B // 2 - 1) as i:
                body(2 * i, 0, True, True)
                body(2 * i + 1, 1, True, True)
            body(B - 2, 0, True, False)
            body(B - 1, 1, False, False)

        def numbers(eng, where, most):
            return nc.values_load_multi_w_load_instructions(where, engines=[eng.engine], min_val=0, max_val=most,
                                                            skip_runtime_bounds_check_because="the plan keeps them in range")[1]

        CROSS = "B" in phases

        def routed(b):
            return "C" in phases and (not isinstance(b, int) or 0 <= b < B)

        def wait_apart(eng, *waits):
            held = [(sem, v if isinstance(v, int) else eng.to_reg(v)) for sem, v in waits]
            eng.wait_ge(w_("began"), 1)
            for sem, v in held:
                at_least(eng, sem, v)

        GOT = {True: 16 * 2 * NP, False: 16 * (NP + 2)}

        block = ctx.enter_context(nc.Block())

        @block.sync
        def _(sp):
            def load(dst, src, sem="weights", **how):
                sp.dma_start(dst, src, **how).then_inc(w_(sem), 16)

            xv = t["x"].rearrange("b (u p) c -> p (b u) c", p=128)
            load(X[:, 0:2, :], xv[:, 0:2, :], "x_first")
            vec = lambda name: t[name].rearrange("(p o) -> p o", o=1)
            of_rows = lambda name: t[name].rearrange("(j r) -> r j", j=PAIRS)

            load(constants[:, :], t["constants"])
            load(w_raw[:, 0, :], t["L0_attn_Wq"])
            load(w_raw[:, 1, :], t["L0_attn_Wk"])
            load(cols[:, 0:1], of_rows("L0_attn_bq"), allow_slow_non_contiguous=True)
            load(cols[:, 1:2], of_rows("L0_attn_bk"), allow_slow_non_contiguous=True)
            load(wv[:, :], t["L0_attn_Wv"])
            load(ctx_rows[:, :, :], t["ctx_768"].rearrange("b m c -> (b m) c").rearrange("(u p) c -> p u c", p=128), "later")
            load(w_raw[0:EC, 3, :], t["L0_xattn_Wk"], "later")
            load(w_raw[:, 2, :], t["L0_xattn_Wq"], "later")
            load(cols[:, 3:4], of_rows("L0_xattn_bq"), "later", allow_slow_non_contiguous=True)
            load(cols[:, 4:5], of_rows("L0_xattn_bk"), "later", allow_slow_non_contiguous=True)
            for dst, name in ((wo, "L0_attn_Wo"), (cwv, "L0_xattn_Wv"), (cw1, "L0_xattn_W1")):
                load(dst[:, :], t[name], "later")
            load(cols[:, 2:3], vec("L0_attn_bv"), "later")
            load(cols[:, 5:6], vec("L0_xattn_bv"), "later")
            load(cols[:, 6:8], t["L0_xattn_b1"].rearrange("(i p) -> p i", p=128), "later", allow_slow_non_contiguous=True)
            load(rows[:, 0, :], t["L0_attn_bo"].rearrange("(o n) -> o n", o=1).to_broadcast([128, E]), "later")
            load(rows[:, 1, :], t["L0_xattn_b2"].rearrange("(o n) -> o n", o=1).to_broadcast([128, E]), "later")
            load(cw2[:, :, :], t["L0_xattn_W2"].rearrange("(c p) n -> p c n", p=128), "later")
            load(rw_rows[:, :], t["L0_ffn_router_w"], "later")
            for i, name in enumerate(("gate", "up")):
                load(sh_rows[:, 2 * i:2 * i + 2, :], t[f"L0_ffn_shared_{name}_w"].rearrange("(k p) c -> p k c", p=128), "later")
            load(sh_rows[:, 4:6, :], t["L0_ffn_shared_down_w"].rearrange("p (k s) -> p k s", k=2), "later")
            load(X[:, 2:NT, :], xv[:, 2:NT, :], "x_rest")

            def regroup(s, b, p, keys):
                at = 0 if keys else S * p
                at_least(sp, s("pair"), 4 * (b - 1))
                for k in range(3):
                    sp.wait_ge(s("part"), 3 * b + k + 1)
                    for i in range(NP):
                        if Q_PART[i] == k:
                            sp.dma_start(qs[p][16 * i:16 * i + 16, :, :], part[:, k, at:at + S]).then_inc(s("got"), 16)
                        if keys and K_PART[i] == k:
                            sp.dma_start(kbd[p][16 * i:16 * i + 16].rearrange("r j n a k -> r j (n a k)"),
                                         part[:, k, S:3 * S]).then_inc(s("got"), 16)
                    if k == 0 and not keys:
                        sp.dma_start(ckbd[p][0:KROWS, :, :, :].rearrange("r j a k -> r j (a k)"),
                                     ck_scr[:, :, :, bass.ds(2 * M * b, 2 * M)].rearrange("i r j n -> (i r) j n")).then_inc(s("got"), 16)
                        at_least(sp, s("od"), b - 1)
                        sp.dma_start(cvbd[p][:, :, :], cvbd_all[:, bass.ds(b, 1), :, :].squeeze(1)).then_inc(s("got"), 16)
                wait_apart(sp, (s("got"), GOT[keys] * b + GOT[keys]))

            regroup(s_, 0, 0, True)
            sp.wait_ge(w_("ckpart"), 3)
            for i, k in enumerate(K_PART):
                sp.dma_start(ck_scr[i].rearrange("r j n -> (r j) n"), ckpart[:, k].rearrange("p b a k -> p (b a k)")).then_inc(w_("ck_put"), 16)
            sp.wait_ge(w_("ck_put"), 16 * NP)
            load(wgu[:, :, :], t["L0_ffn_gate_up_w"].rearrange("e c h -> c e h"), "experts")
            loop(sp, lambda b, p, one, two: one and regroup(s_, b + 1, 1 - p, True))
            if "B" in phases:
                sp.wait_ge(w_("cv"), 8)
                regroup(c_, 0, 0, False)
                sp.wait_ge(s_("pair"), 4 * B)
                load(wd, t["L0_ffn_down_w"].rearrange("e c h -> c e h"), "experts")
                loop(sp, lambda b, p, one, two: one and regroup(c_, b + 1, 1 - p, False))
            ov = out.rearrange("b (u p) c -> p (b u) c", p=128)
            if "C" not in phases:
                sp.wait_ge((c_ if "B" in phases else s_)("x_new"), B)
                sp.dma_start(ov, X[:, :, :]).then_inc(w_("stored"), 16)
                sp.wait_ge(w_("stored"), 16)
                return

            sp.wait_ge(r_("tails"), 1)
            sp.dma_start(xs[NE * CAP:NE * CAP + 128, :], zero_rows[:, :]).then_inc(e_("zeros"), 16)
            with sp.Fori(0, NE // 4) as i:
                for end in numbers(sp, tails[0:1, bass.ds(4 * i, 4)], NE * CAP - 128):
                    sp.dma_start(xs[bass.ds(end, 128), :], zero_rows[:, :]).then_inc(e_("zeros"), 16)
            sp.wait_ge(e_("zeros"), 16 * (NE + 1))
            sp.wait_ge(r_("sent"), 64 * B)
            sp.wait_ge(e_("tile_row"), 1)

            def tile_in(k, i, p):
                at_least(sp, e_("xT_ps"), k - 3)
                if isinstance(k, int):
                    first = sp.value_load(tile_row[0:1, 0, bass.ds(k, 1)], min_val=0, max_val=NE * CAP)
                else:
                    first = loaded_first[p]
                sp.dma_start(xt[p][:, :], xs[bass.ds(first, 128), :]).then_inc(e_(f"in{p}"), 16)

            loaded_first = []

            def load_first(i):
                loaded_first[:] = numbers(sp, tile_row[0:1, 0, bass.ds(4 * i, 4)], NE * CAP)

            skewed(sp, [(tile_in, 0)], TILES, load_first)

            def store(b, i, p):
                sp.wait_ge(g_("x_out"), b + 1)
                sp.dma_start(ov[:, bass.ds(2 * b, 2), :], X[:, bass.ds(2 * b, 2), :]).then_inc(w_("stored"), 16)

            loop2(sp, store, B)
            sp.wait_ge(w_("stored"), 16 * B)

        @block.gpsimd
        def _(pool):
            g = nc.gpsimd

            def rstd_of(s, b, mv=mv, veps=veps, rstd=rstd):
                wait_apart(pool, (s("aggr"), 2 * b + 2), (s("norm"), 2 * b))
                g.tensor_scalar(veps[:, :], mv[:, :, 1], EPS, None, ALU.add).then_inc(s("veps"), 1)
                pool.wait_ge(s("veps"), b + 1)
                g.tensor_tensor(rstd[:, :], veps[:, :], minus_half[:, :], ALU.pow).then_inc(s("rstd"), 1)

            g.memset(minus_half[:, :], -0.5).then_inc(w_("began"), 1)
            rstd_of(s_, 0)
            pool.wait_ge(w_("weights"), 16 * W_LOADS)
            def order(i, w):
                n = w.shape[0]
                g.tensor_copy(w[:, :].rearrange("c (r j) -> c r j", j=PAIRS),
                              w_raw[0:n, i, :].rearrange("c (j r) -> c r j", j=PAIRS)).then_inc(w_("ordered"), 1)

            order(0, wq)
            order(1, wk)
            g.tensor_copy(identb[:, :], ident).then_inc(w_("ordered"), 1)
            g.memset(cvbd_all[:, :, :, :], 0.0).then_inc(w_("zeroed"), 1)
            g.memset(ck32, 0.0).then_inc(w_("zeroed"), 1)
            def add_bias(s, b, bias):
                pool.wait_ge(s("norm"), 2 * b + 2)
                g.tensor_tensor(X[:, bass.ds(2 * b, 2), :], X[:, bass.ds(2 * b, 2), :],
                                bias.unsqueeze(1).to_broadcast([128, 2, E]), ALU.add).then_inc(s("x_biased"), 1)

            def self_start(b, p):
                wait_apart(pool, (s_("xnT"), b + 1), (s_("vtok_ps"), b))
                for first, step, n, to in RUNS:
                    last = g.tensor_copy(xg[:, :, to:to + n],
                                         xnT[:, first:first + step * (n - 1) + 1:step].unsqueeze(1).to_broadcast([128, H, n]))
                last.then_inc(s_("xg"), 1)
                pool.wait_ge(s_("qk32"), 4 * b + 4)
                for dst, of in ((kg, k32), (qg, qkz)):
                    for first, step, n, to in RUNS:
                        src = of[p][:, first:first + step * (n - 1) + 1:step]
                        last = g.tensor_tensor(dst[p][:, :, to:to + n], src.unsqueeze(1).to_broadcast([128, H, n]),
                                               head_of_row[:, :].unsqueeze(2).to_broadcast([128, H, n]), ALU.mult)
                    last.then_inc(s_("kgqg"), 1)

            def self_body(b, p, one, two):
                if one:
                    self_start(b + 1, 1 - p)
                    add_bias(s_, b + 1, bo_[:, :])
                if two:
                    rstd_of(s_, b + 2)
                elif CROSS:
                    rstd_of(c_, b + 2 - B)
                pool.wait_ge(s_("gexp"), b + 1)
                v = probs_g[:, :].rearrange("p (n q) -> p n q", n=NB)
                g.tensor_tensor(v, v, outside[:, :].unsqueeze(2).to_broadcast([128, NB, BLOCK]), ALU.mult).then_inc(s_("gmasked"), 1)
                wait_apart(pool, (s_("gq_rcp"), b + 1))
                g.tensor_scalar(pgq[:, :], pgq[:, :], gstat[:, 3:4], None, ALU.mult).then_inc(s_("gq_norm"), 1)

            self_start(0, 0)
            pool.wait_ge(w_("later"), 16 * W_LATER)
            order(2, cwq)
            order(3, cwk)
            rstd_of(s_, 1)
            pool.wait_ge(s_("rstd"), 2)
            for p in range(2):
                last = g.tensor_copy(ckbd[p][SHIFT:128, :, :, :], shift_pair.to_broadcast([32, PAIRS, 2, M]))
            last.then_inc(w_("set"), 1)
            pool.wait_ge(w_("set"), 1)

            g.tensor_copy(aheadb[:, :], ahead[:, :]).then_inc(w_("set"), 1)
            g.memset(zero_rows[:, :], 0.0).then_inc(w_("set"), 1)
            g.tensor_copy(used[0][:, :], experts[:, NE:2 * NE]).then_inc(w_("set"), 1)
            pool.wait_ge(w_("bo_"), 1)
            add_bias(s_, 0, bo_[:, :])
            loop(pool, self_body)

            if "B" in phases:
                def route_slots(b, p):
                    pool.wait_ge(r_("counts"), b + 1)
                    g.tensor_tensor(rowpos[:, :, :], counts[:, 0:2, :],
                                    used[p][:, :].unsqueeze(1).to_broadcast([128, 2, NE]), ALU.add).then_inc(r_("rowpos"), 1)
                    g.tensor_tensor(used[1 - p][:, :], counts[:, 2, :], used[p][:, :], ALU.add).then_inc(r_("rowpos"), 1)
                    wait_apart(pool, (r_("rowpos"), 2 * b + 2), (r_("onehot"), 2 * b + 2))
                    for u in range(2):
                        g.tensor_tensor(picked[:, u, :, :], onehot[:, bass.ds(2 * b + u, 1), :, :].squeeze(1),
                                        rowpos[:, u, :].unsqueeze(1).to_broadcast([128, TOPK, NE]), ALU.mult).then_inc(r_("picked"), 1)
                    pool.wait_ge(r_("picked"), 2 * b + 2)
                    cells = picked[:, :, :, :].rearrange("p u k e -> p (u k) e")
                    for i, n in enumerate((8, 4, 2, 1)):
                        to = cells[:, :, 0:n] if n > 1 else slots[:, :].unsqueeze(2)
                        g.tensor_tensor(to, cells[:, :, 0:n], cells[:, :, n:2 * n], ALU.add).then_inc(r_("slotf"), 1)
                        if n > 1:
                            pool.wait_ge(r_("slotf"), 4 * b + i + 1)
                    wait_apart(pool, (r_("slotf"), 4 * b + 4))
                    g.tensor_copy(slotf[:, bass.ds(2 * b, 2), :], slots[:, :].rearrange("p (u k) -> p u k", k=TOPK))
                    g.tensor_copy(sloti[p][:, :], slots[:, :]).then_inc(r_("slot"), 1)

                def scatter(b, p):
                    wait_apart(pool, (r_("slot"), b + 1), (r_("sent"), 64 * b))
                    for u in range(2):
                        for k in range(TOPK):
                            pool.indirect_dma_start(xs, bass.IndirectOffsetOnAxis(sloti[p][:, 2 * u + k:2 * u + k + 1], 0),
                                                    xn3[p][:, u, :], None).then_inc(r_("sent"), 16)

                def route(b, p):
                    if routed(b - 1):
                        rstd_of(r_, b - 1, mv3, veps3, rstd3)
                    if routed(b - 2):
                        route_slots(b - 2, p)
                        scatter(b - 2, p)

                def cross_body(b, p, one, two):
                    add_bias(c_, b, rows[:, 1, :])
                    if two:
                        rstd_of(c_, b + 2)
                    route(b, p)

                loop(pool, cross_body, 4)
                route(B, 0)
                route(B + 1, 1)

            if "C" in phases:
                pool.wait_ge(g_("backi"), 1)
                for q in range(4):
                    pool.wait_ge(e_(f"out{q}"), 16 * (TILES // 4))

                def gather(b, i, p):
                    wait_apart(pool, (g_("x_out"), b - 3))
                    g.tensor_copy(idx[p][:, :], backi[:, bass.ds(4 * b, 4)]).then_inc(g_("idx"), 1)
                    wait_apart(pool, (g_("idx"), b + 1))
                    for k in range(4):
                        pool.indirect_dma_start(yrow[p][:, k, :], None, ys,
                                                bass.IndirectOffsetOnAxis(idx[p][:, k:k + 1], 0)).then_inc(g_(f"got{p}"), 16)

                skewed(pool, [(gather, 0)], B)

        @block.vector
        def _(dve):
            v = nc.vector
            def context_biases():
                dve.wait_ge(w_("bias_ps"), 1)
                v.tensor_tensor(bo_[:, :], MISC[:, 0:E], rows[:, 0, :], ALU.add).then_inc(w_("bo_"), 1)
                v.tensor_tensor(cb1_[:, :], MISC[:, E:E + 2], cols[:, 6:8], ALU.add).then_inc(w_("bo_"), 1)

            def context_parts():
                dve.wait_ge(w_("ck32"), 4)
                v.tensor_copy(ckpart[:, 0], ck32).then_inc(w_("ckpart"), 1)
                dve.wait_ge(w_("ckpart"), 1)
                v.tensor_tensor(ckres, ck32, ckpart[:, 0], ALU.subtract).then_inc(w_("ckres"), 1)
                dve.wait_ge(w_("ckres"), 1)
                v.tensor_copy(ckpart[:, 1], ckres).then_inc(w_("ckpart"), 1)
                dve.wait_ge(w_("ckpart"), 2)
                v.tensor_tensor(ckpart[:, 2], ckres, ckpart[:, 1], ALU.subtract).then_inc(w_("ckpart"), 1)

            def stats(s, b, arrived, st=st, mv=mv):
                arrived(b)
                for u in range(2):
                    v.bn_stats(st[:, u, :], X[:, bass.ds(2 * b + u, 1), :].squeeze(1)).then_inc(s("stats"), 1)
                for u in range(2):
                    wait_apart(dve, (s("stats"), 2 * b + u + 1), (s("veps"), b))
                    v.bn_aggr(mv[:, u, :], st[:, u, :]).then_inc(s("aggr"), 1)

            def normalise(s, b):
                dve.wait_ge(s("rstd"), b + 1)
                at_least(dve, s("xT_ps"), b)
                for u in range(2):
                    v.tensor_scalar(xn[:, u, :], X[:, bass.ds(2 * b + u, 1), :].squeeze(1), mv[:, u, 0:1], rstd[:, u:u + 1],
                                    ALU.subtract, ALU.mult).then_inc(s("norm"), 1)

            def split_rest(s, b, p, n, at=0):
                r = res[:, 0:n]
                dve.wait_ge(s("part"), 3 * b + 1)
                v.tensor_tensor(r, qkz[p][:, 0:n], part[:, 0, at:at + n], ALU.subtract).then_inc(s("res"), 1)
                dve.wait_ge(s("res"), b + 1)
                v.tensor_copy(part[:, 1, at:at + n], r).then_inc(s("part"), 1)
                dve.wait_ge(s("part"), 3 * b + 2)
                v.tensor_tensor(part[:, 2, at:at + n], r, part[:, 1, at:at + n], ALU.subtract).then_inc(s("part"), 1)

            def row_max(s, b, u, half):
                use = 4 * b + 2 * u + half
                dve.wait_ge(s("scores"), use + 1)
                bank = P1[half]
                v.tensor_reduce(nmax[:, u, 8 * half:8 * half + 8], bank[:, :].rearrange("p (h k) -> p h k", k=64),
                                AX.X, ALU.max, negate=True).then_inc(s("nmax"), 1)

            def shift_rows(s, b, p):
                at_least(dve, s("mT_ps"), b)
                v.tensor_copy(mparts[:, :, 0, :], nmax[:, :, :]).then_inc(s("mpart"), 1)
                dve.wait_ge(s("mpart"), 2 * b + 1)
                v.tensor_tensor(mparts[:, :, 1, :], nmax[:, :, :], mparts[:, :, 0, :], ALU.subtract).then_inc(s("mpart"), 1)

            def shift_spread(s, b, p):
                dve.wait_ge(s("mT_ps"), b + 1)
                v.tensor_copy(qs[p][SHIFT:128, 0, :], P1[1][:, :].bitcast(BF16)[SHIFT:128, 0:S]).then_inc(s("mT"), 1)
                dve.wait_ge(s("mT"), 3 * b + 1)
                for j, to in ((1, 4), (4, PAIRS)):
                    v.tensor_copy(qs[p][SHIFT:128, j:to, :], qs[p][SHIFT:128, 0:1, :].to_broadcast([32, to - j, S])).then_inc(s("mT"), 1)

            def attended(s, b):
                dve.wait_ge(s("od"), b + 1)
                v.reciprocal(rden[:, :], OD[:, S:2 * S]).then_inc(s("rden"), 1)
                dve.wait_ge(s("rden"), b + 1)
                v.tensor_tensor(attT[:, :], OD[:, 0:S], rden[:, :], ALU.mult).then_inc(s("attT"), 1)

            def self_arrived(b):
                if isinstance(b, int) and b == 0:
                    dve.wait_ge(w_("x_first"), 16)
                elif isinstance(b, int) and b == 1:
                    dve.wait_ge(w_("x_rest"), 16)

            def self_vg(b, p):
                dve.wait_ge(s_("vtok_ps"), b + 1)
                v.tensor_tensor(vg[p][:, :], A1[:, 2 * E:3 * E], same_head[:, :], ALU.mult).then_inc(s_("vg"), 1)

            def self_end(b):
                dve.wait_ge(s_("wo_ps"), b + 1)
                dve.wait_ge(s_("x_biased"), b + 1)
                xb = X[:, bass.ds(2 * b, 2), :]
                v.tensor_tensor(xb, OD[:, 0:2 * E].rearrange("p (u c) -> p u c", u=2), xb, ALU.add).then_inc(s_("x_new"), 1)

            def cross_arrived(b):
                dve.wait_ge(s_("x_new"), b + 1)

            def self_body(b, p, one, two):
                row_max(s_, b, 0, 0)
                row_max(s_, b, 0, 1)
                row_max(s_, b, 1, 0)
                row_max(s_, b, 1, 1)
                dve.wait_ge(s_("scores_g"), b + 1)
                v.tensor_reduce(nmaxg[:, :, :], P2[1][:, 0:2 * 128].rearrange("p (h k) -> p h k", k=NGLOB),
                                AX.X, ALU.max, negate=True).then_inc(s_("nmaxg"), 1)
                dve.wait_ge(s_("nmaxg"), 2 * b + 1)
                dve.wait_ge(s_("nmax"), 4 * b + 4)
                v.tensor_tensor(nmax[:, :, :], nmax[:, :, :], nmaxg[:, :, :], ALU.min).then_inc(s_("nmaxg"), 1)
                dve.wait_ge(s_("nmaxg"), 2 * b + 2)
                shift_rows(s_, b, p)
                dve.wait_ge(s_("gq_ps"), b + 1)
                v.tensor_reduce(gstat[:, 0:1], MISC[:, 0:S], AX.X, ALU.max, negate=True).then_inc(s_("gq_max"), 1)
                dve.wait_ge(s_("gq_max"), b + 1)
                v.tensor_scalar(gstat[:, 1:2], gstat[:, 0:1], SCALE, None, ALU.mult).then_inc(s_("gq_bias"), 1)
                shift_spread(s_, b, p)
                if not isinstance(b, int) or b > 0:
                    self_end(b - 1)
                if one:
                    split_rest(s_, b + 1, 1 - p, 3 * S)
                elif CROSS:
                    split_rest(c_, 0, 0, S)
                if two:
                    stats(s_, b + 2, self_arrived)
                elif CROSS:
                    stats(c_, b + 2 - B, cross_arrived)
                dve.wait_ge(s_("gq_exp"), b + 1)
                v.reciprocal(gstat[:, 3:4], gstat[:, 2:3]).then_inc(s_("gq_rcp"), 1)
                if one:
                    self_vg(b + 1, 1 - p)
                if two:
                    normalise(s_, b + 2)
                elif CROSS:
                    dve.wait_ge(s_("xT_ps"), B)
                    normalise(c_, b + 2 - B)
                attended(s_, b)
                dve.wait_ge(s_("gq_o"), b + 1)
                v.tensor_tensor(gtmp[:, :, :], MISC[:, 0:128].rearrange("p (h g) -> p h g", g=NGLOB),
                                same_head[:, ::D].unsqueeze(2).to_broadcast([128, H, NGLOB]), ALU.mult).then_inc(s_("gtmp"), 1)
                dve.wait_ge(s_("gtmp"), b + 1)
                dve.wait_ge(s_("attT"), b + 1)
                for first, step, n, to in RUNS:
                    last = v.tensor_reduce(attT[:, first:first + step * (n - 1) + 1:step],
                                           gtmp[:, :, to:to + n].rearrange("p h g -> p g h"), AX.X, ALU.add)
                last.then_inc(s_("att_all"), 1)

            def shift_rows_of_keys(p):
                for n in range(NB):
                    v.tensor_copy(kbd[p][SHIFT:128, :, n, :, :],
                                  shift_pair.to_broadcast([32, PAIRS, 2, BLOCK])).then_inc(w_("laid_out"), 1)

            for p in range(2):
                v.memset(vbd[p][:, :, :, :], 0.0)
            for p in range(2):
                v.memset(qkz[p][:, S:3 * S], 0.0).then_inc(w_("laid_out"), 1)
            stats(s_, 0, self_arrived)
            normalise(s_, 0)
            dve.wait_ge(w_("weights"), 16 * W_LOADS)
            v.tensor_copy(shift_glob[SHIFT:128, :], held["shift_glob"][SHIFT:128])
            shift_rows_of_keys(0)
            shift_rows_of_keys(1)
            split_rest(s_, 0, 0, 3 * S)
            self_vg(0, 0)
            context_biases()
            stats(s_, 1, self_arrived)
            normalise(s_, 1)
            context_parts()
            loop(dve, self_body)
            self_end(B - 1)

            if "B" in phases:
                def cross_end(b):
                    dve.wait_ge(c_("y_ps"), b + 1)
                    dve.wait_ge(c_("x_biased"), b + 1)
                    xb = X[:, bass.ds(2 * b, 2), :]
                    v.tensor_tensor(xb, OD[:, 0:2 * E].rearrange("p (u c) -> p u c", u=2), xb, ALU.add).then_inc(c_("x_new"), 1)

                number = experts[:, 0:NE]

                def route_normalise(b, p):
                    dve.wait_ge(r_("rstd"), b + 1)
                    at_least(dve, r_("sent"), 64 * (b - 1))
                    for u in range(2):
                        v.tensor_scalar(xn3[p][:, u, :], X[:, bass.ds(2 * b + u, 1), :].squeeze(1), mv3[:, u, 0:1],
                                        rstd3[:, u:u + 1], ALU.subtract, ALU.mult).then_inc(r_("norm"), 1)

                def route_pick(b):
                    wait_apart(dve, (r_("logits"), b + 1))
                    for u in range(2):
                        v.max(top8[:, u, :], logits[:, u, :]).then_inc(r_("top"), 1)
                    for u in range(2):
                        wait_apart(dve, (r_("top"), 2 * b + u + 1))
                        v.max_index(topi[:, u, :], top8[:, u, :], logits[:, u, :]).then_inc(r_("topi"), 1)
                    v.tensor_copy(topv[:, bass.ds(2 * b, 2), :], top8[:, :, 0:TOPK])
                    dve.wait_ge(r_("topi"), 2 * b + 2)
                    v.tensor_copy(topf[:, :, :], topi[:, :, 0:TOPK]).then_inc(r_("topf"), 1)
                    dve.wait_ge(r_("topf"), b + 1)
                    for u in range(2):
                        v.tensor_tensor(onehot[:, bass.ds(2 * b + u, 1), :, :].squeeze(1), number.unsqueeze(1).to_broadcast([128, TOPK, NE]),
                                        topf[:, u, :].unsqueeze(2).to_broadcast([128, TOPK, NE]), ALU.is_equal).then_inc(r_("onehot"), 1)
                    dve.wait_ge(r_("onehot"), 2 * b + 2)
                    oh = onehot[:, bass.ds(2 * b, 2), :, :]
                    v.tensor_tensor(both[:, :, :], oh[:, :, 0, :], oh[:, :, 1, :], ALU.add).then_inc(r_("both"), 1)

                def route(b, p, stage):
                    if stage == 0 and routed(b - 1):
                        stats(r_, b - 1, lambda b: wait_apart(dve, (c_("x_new"), b + 1)), st3, mv3)
                    if stage == 0 and routed(b - 2):
                        route_pick(b - 2)
                    if stage == 1 and routed(b - 1):
                        route_normalise(b - 1, 1 - p)

                def cross_body(b, p, one, two):
                    row_max(c_, b, 0, 0)
                    row_max(c_, b, 0, 1)
                    row_max(c_, b, 1, 0)
                    row_max(c_, b, 1, 1)
                    dve.wait_ge(c_("nmax"), 4 * b + 4)
                    shift_rows(c_, b, p)
                    if two:
                        stats(c_, b + 2, cross_arrived)
                    shift_spread(c_, b, p)
                    if not isinstance(b, int) or b > 0:
                        cross_end(b - 1)
                    if one:
                        split_rest(c_, b + 1, 1 - p, S, (1 - p) * S)
                    route(b, p, 0)
                    if two:
                        normalise(c_, b + 2)
                    route(b, p, 1)
                    attended(c_, b)

                loop(dve, cross_body, 4)
                cross_end(B - 1)
                for b in (B, B + 1):
                    for stage in range(2):
                        route(b, b % 2, stage)

            if "C" in phases:
                def shared(u, i, p):
                    for c in range(2):
                        dve.wait_ge(h_("silu"), 2 * u + c + 1)
                        at_least(dve, h_("y_ps"), u)
                        v.tensor_tensor(shs[:, c, :], PS[2 * c + 1][:, :], sgs[:, c, :], ALU.mult).then_inc(h_("h"), 1)
                    dve.wait_ge(h_("y_ps"), u + 1)
                    xu = X[:, bass.ds(4 * u, 4), :]
                    v.tensor_tensor(xu, PS[4 + p][:, :].rearrange("p (t c) -> p t c", t=4), xu, ALU.add).then_inc(h_("x"), 1)

                COUNT, TL, CUM, MET, NUM, AHEAD, ADJ, ONE = range(8)
                step = [0]

                def then(ins):
                    step[0] += 1
                    ins.then_inc(r_("plan"), 1)
                    dve.wait_ge(r_("plan"), step[0])

                end = used[0]
                dve.wait_ge(r_("slot"), B)
                v.tensor_copy(tails[0:1, :], end[0:1, :]).then_inc(r_("tails"), 1)
                then(v.tensor_tensor(plan[:, COUNT, :], end[:, :], experts[:, NE:2 * NE], ALU.subtract))
                then(v.tensor_scalar(plani[:, 0, :], plan[:, COUNT, :], 127.0, None, ALU.add))
                then(v.tensor_scalar(plani[:, 1, :], plani[:, 0, :], 7, None, ALU.arith_shift_right))
                then(v.tensor_copy(plan[:, TL, :], plani[:, 1, :]))
                then(v.memset(plan[:, ONE, :], 1.0))
                then(v.tensor_tensor_scan(plan[:, CUM, :], plan[:, ONE, :], plan[:, TL, :], 0.0, ALU.mult, ALU.add))
                then(v.tensor_scalar(plan[:, MET, :], plan[:, CUM, :], experts[:, 2 * NE:2 * NE + 1], None, ALU.is_le))
                then(v.tensor_tensor(plan[:, AHEAD, :], plan[:, MET, :], plan[:, TL, :], ALU.mult))
                then(v.tensor_reduce(tile_of[:, 0:1], plan[:, MET, :], AX.X, ALU.add))
                then(v.tensor_reduce(tile_of[:, 1:2], plan[:, AHEAD, :], AX.X, ALU.add))
                then(v.tensor_tensor(tile_of[:, 2:3], experts[:, 2 * NE:2 * NE + 1], tile_of[:, 1:2], ALU.subtract))
                then(v.tensor_scalar(tile_of[:, 2:3], tile_of[:, 2:3], 128.0, None, ALU.mult))
                then(v.scalar_tensor_tensor(tile_of[:, 2:3], tile_of[:, 0:1], float(CAP), tile_of[:, 2:3], ALU.mult, ALU.add))
                then(v.tensor_scalar(tile_of[:, 2:3], tile_of[:, 2:3], float(NE * CAP), None, ALU.min))
                v.tensor_scalar(tile_of[:, 3:4], tile_of[:, 0:1], float(NE - 1), None, ALU.min).then_inc(e_("tile_of"), 1)
                shared(0, 0, 0)
                dve.wait_ge(e_("map_ps"), 1)
                v.tensor_copy(tile_row[0:1, :, :], MISC[0:1, 0:256].rearrange("p (i k) -> p i k", i=2)).then_inc(e_("tile_row"), 1)

                shared(1, 0, 1)
                then(v.tensor_tensor(plan[:, ADJ, :], plan[:, CUM, :], plan[:, TL, :], ALU.subtract))
                then(v.tensor_scalar(plan[:, ADJ, :], plan[:, ADJ, :], 128.0, None, ALU.mult))
                then(v.tensor_tensor(plan[:, ADJ, :], plan[:, ADJ, :], experts[:, NE:2 * NE], ALU.subtract))
                then(v.tensor_tensor(picked_all[:, :, :], onehot[:, :, :, :].rearrange("p t k e -> p (t k) e"),
                                     plan[:, ADJ, :].unsqueeze(1).to_broadcast([128, NT * TOPK, NE]), ALU.mult))
                then(v.tensor_reduce(back[:, :], picked_all[:, :, :], AX.X, ALU.add))
                then(v.tensor_tensor(back[:, :], back[:, :], slotf[:, :, :].rearrange("p t k -> p (t k)"), ALU.add))
                v.tensor_copy(backi[:, :], back[:, :]).then_inc(g_("backi"), 1)
                dve.wait_ge(g_("gate_exp"), 1)
                then(v.tensor_scalar(gate[:, :], gate[:, :], 1.0, None, ALU.add))
                then(v.reciprocal(gate[:, :], gate[:, :]))

                def tile(k, i, p):
                    dve.wait_ge(e_("silu"), k + 1)
                    at_least(dve, e_("hT_ps"), k - 1)
                    p = p % 2
                    v.tensor_tensor(eh[p][:, :], PS[2 + p][:, ED:2 * ED], sg[p][:, :], ALU.mult).then_inc(e_("h"), 1)

                def tile_end(k, i, p):
                    dve.wait_ge(e_("y_ps"), k + 1)
                    at_least(dve, e_(f"out{p}"), 16 * i)
                    v.tensor_copy(ey[p][:, :], PS[6 + p % 2][:, 0:E]).then_inc(e_("y"), 1)

                skewed(dve, [(tile, 0), (tile_end, 2)], TILES)


                def combine(b, i, p):
                    dve.wait_ge(g_(f"got{p}"), 64 * (i + 1))
                    for u in range(2):
                        xu = X[:, bass.ds(2 * b + u, 1), :].squeeze(1)
                        for k in range(TOPK):
                            if k:
                                dve.wait_ge(g_("first"), 2 * b + u + 1)
                            last = v.scalar_tensor_tensor(xu, yrow[p][:, 2 * u + k, :], gate[:, bass.ds(4 * b + 2 * u + k, 1)], xu,
                                                          ALU.mult, ALU.add)
                            if k == 0:
                                last.then_inc(g_("first"), 1)
                    last.then_inc(g_("x_out"), 1)

                def two_combined(i, q):
                    u = 2 * i + q - EARLY
                    combine(2 * u, i - EARLY // 2, 2 * q)
                    combine(2 * u + 1, i - EARLY // 2, 2 * q + 1)

                dve.wait_ge(h_("x"), EARLY)
                later_units(dve, shared, two_combined)
                dve.wait_ge(h_("x"), B // 2)
                for b in range(B - 2 * EARLY, B):
                    combine(b, b // 4, b % 4)

        @block.scalar
        def _(act):
            a_ = nc.scalar
            def context():
                act.wait_ge(w_("ctxT_ps"), 1)
                for i in range(2):
                    a_.copy(ctxT[:, 512 * i:512 * i + 512], PS[2 + i][0:EC, :]).then_inc(w_("ctxT"), 1)
                act.wait_ge(w_("zeroed"), 2)
                for i in range(2):
                    act.wait_ge(w_("ck_ps"), i + 1)
                    for a in range(2):
                        h = slice(64 * a, 64 * a + 64)
                        a_.activation(ck32[h, 8 * i:8 * i + 8, a, :], PS[4 + i][h, :].rearrange("p (b k) -> p b k", k=M), ACT.Identity,
                                      bias=cols[h, 4:5]).then_inc(w_("ck32"), 1)
                for i in range(4):
                    act.wait_ge(w_("cv_ps"), i + 1)
                    value_cells(a_, cvbd_all[:, 4 * i:4 * i + 4, :, :], PS[CV_BANKS[i]], w_("cv"))
                act.wait_ge(w_("turned_ps"), 1)
                a_.copy(rwT[:, :], PS[4][:, 0:NE]).then_inc(w_("turned"), 1)
                for i in range(2):
                    a_.copy(shT[:, 3 * i:3 * i + 3, :], PS[5 + i][:, 0:384].rearrange("p (i c) -> p i c", i=3)).then_inc(w_("turned"), 1)

            def self_start(b, p):
                act.wait_ge(s_("xT_ps"), b + 1)
                at_least(act, s_("vtok_ps"), b)
                a_.copy(xnT[:, :], A0[:, 0:S]).then_inc(s_("xnT"), 1)

            def first_part(s, b, p, n, made, got, at=0):
                act.wait_ge(s("qk32"), made)
                at_least(act, s("got"), got)
                a_.copy(part[:, 0, at:at + n], qkz[p][:, 0:n]).then_inc(s("part"), 1)

            def self_start2(b, p):
                act.wait_ge(s_("qk_ps"), 2 * b + 2)
                a_.activation(qkz[p][:, 0:S], A0[:, 0:S], ACT.Identity, bias=cols[:, 0:1]).then_inc(s_("qk32"), 1)
                kz = qkz[p][:, S:3 * S].rearrange("p (n a k) -> p n a k", a=2, k=BLOCK)
                for a in range(2):
                    h = slice(64 * a, 64 * a + 64)
                    a_.activation(kz[h, :, a, :], A0[h, S:2 * S].rearrange("p (n k) -> p n k", k=BLOCK), ACT.Identity,
                                  bias=cols[h, 1:2]).then_inc(s_("qk32"), 1)
                first_part(s_, b, p, 3 * S, 4 * b + 3, GOT[True] * b)
                a_.activation(k32[p][:, :], A0[:, S:2 * S], ACT.Identity, bias=cols[:, 1:2]).then_inc(s_("qk32"), 1)

            def self_start_values(b, p):
                act.wait_ge(s_("vdup_ps"), b + 1)
                value_cells(a_, vbd[p][:, :, :, :], A1, s_("vbd"))

            def self_start3(b, p):
                act.wait_ge(s_("vtok_ps"), b + 1)
                act.wait_ge(s_("vg"), b + 1)
                a_.copy(vtok[p][:, :, :], A1[:, 0:2 * E].rearrange("p (u c) -> p u c", u=2)).then_inc(s_("vtok"), 1)

            def exps(s, b, which):
                for i in which:
                    act.wait_ge(s("pair"), 4 * b + i + 1)
                    if i == 0:
                        at_least(act, s("od"), b)
                    a_.activation(probs[:, 2 * i:2 * i + 2, :], P2[i % 2][:, :].rearrange("p (j q) -> p j q", j=2),
                                  ACT.Exp, scale=SCALE).then_inc(s("probs"), 1)

            def cross_start(b, p):
                act.wait_ge(c_("xT_ps"), b + 1)
                a_.copy(xnT[:, :], A0[:, 0:S]).then_inc(c_("xnT"), 1)

            def cross_start2(b, p):
                act.wait_ge(c_("q_ps"), b + 1)
                a_.activation(qkz[p][:, 0:S], A0[:, 0:S], ACT.Identity, bias=cols[:, 3:4]).then_inc(c_("qk32"), 1)
                if isinstance(b, int) and b == 0:
                    act.wait_ge(s_("got"), GOT[True] * B)
                first_part(c_, b, p, S, b + 1, GOT[False] * (b - 1), p * S)

            def cross_hidden(b):
                act.wait_ge(c_("h_ps"), b + 1)
                for i in range(2):
                    a_.activation(hT[:, i, :], MISC[:, i * S:(i + 1) * S], ACT.Relu, bias=cb1_[:, i:i + 1]).then_inc(c_("h"), 1)

            def self_body(b, p, one, two):
                if one:
                    self_start(b + 1, 1 - p)
                elif CROSS:
                    cross_start(0, 0)
                if one:
                    self_start2(b + 1, 1 - p)
                elif CROSS:
                    cross_start2(0, 0)
                act.wait_ge(s_("gq_bias"), b + 1)
                at_least(act, s_("gq_T"), b)
                a_.activation(pgq[:, :], MISC[:, 0:S], ACT.Exp, bias=gstat[:, 1:2], scale=SCALE,
                              accum_out=gstat[:, 2:3]).then_inc(s_("gq_exp"), 1)
                exps(s_, b, (0, 1))
                if one:
                    self_start_values(b + 1, 1 - p)
                exps(s_, b, (2, 3))
                act.wait_ge(s_("gk_ps"), b + 1)
                a_.activation(probs_g[:, :], P2[0][:, 0:S], ACT.Exp, scale=SCALE).then_inc(s_("gexp"), 1)
                if one:
                    self_start3(b + 1, 1 - p)
                act.wait_ge(s_("gq_T"), b + 1)
                a_.copy(pgqT[:, :, :], MISC[:, 0:256].rearrange("p (u c) -> p u c", u=2)).then_inc(s_("pgqT"), 1)

            self_start(0, 0)
            act.wait_ge(w_("laid_out"), 2)
            self_start2(0, 0)
            self_start_values(0, 0)
            self_start3(0, 0)
            context()
            loop(act, self_body)

            if "B" in phases:
                def route_turn(b):
                    act.wait_ge(r_("xT_ps"), b + 1)
                    at_least(act, r_("logit_ps"), b)
                    a_.copy(x3s[:, :], A1[:, 0:S]).then_inc(r_("xnT"), 1)
                    a_.copy(x3T[:, bass.ds(S * b, S)], A1[:, 0:S]).then_inc(r_("xnT"), 1)

                def route_logits(b):
                    act.wait_ge(r_("logit_ps"), b + 1)
                    at_least(act, r_("topi"), 2 * b)
                    a_.copy(logits[:, :, :], MISC[:, 0:2 * NE].rearrange("p (u e) -> p u e", e=NE)).then_inc(r_("logits"), 1)

                def route_counts(b):
                    act.wait_ge(r_("count_ps"), b + 1)
                    at_least(act, r_("rowpos"), 2 * b)
                    a_.copy(counts[:, :, :], MISC[:, 0:3 * NE].rearrange("p (i e) -> p i e", e=NE)).then_inc(r_("counts"), 1)

                def cross_body(b, p, one, two):
                    if one:
                        cross_start(b + 1, 1 - p)
                    if routed(b - 2):
                        route_turn(b - 2)
                    if not isinstance(b, int) or b > 0:
                        cross_hidden(b - 1)
                    if one:
                        cross_start2(b + 1, 1 - p)
                    if routed(b - 2):
                        route_logits(b - 2)
                    exps(c_, b, range(4))
                    if routed(b - 2):
                        route_counts(b - 2)

                act.wait_ge(w_("bo_"), 2)
                loop(act, cross_body, 4)
                cross_hidden(B - 1)
                for b in (B - 2, B - 1):
                    if routed(b):
                        route_turn(b)
                        route_logits(b)
                        route_counts(b)

            if "C" in phases:
                act.wait_ge(r_("both"), B)
                a_.activation(gate[:, :], topv[:, :, :].rearrange("p t k -> p (t k)"), ACT.Exp, scale=-1.0).then_inc(g_("gate_exp"), 1)

                def shared(u, i, p):
                    for c in range(2):
                        act.wait_ge(h_("gu_ps"), 2 * u + c + 1)
                        at_least(act, h_("h"), 2 * u)
                        a_.activation(sgs[:, c, :], PS[2 * c][:, :], ACT.Silu).then_inc(h_("silu"), 1)

                shared(0, 0, 0)
                shared(1, 0, 1)

                def turn(k, i, p):
                    act.wait_ge(e_("xT_ps"), k + 1)
                    at_least(act, e_("gu_ps"), k - 1)
                    p = p % 2
                    a_.copy(xtT[p][:, :], PS[p][:, 0:128]).then_inc(e_("xtT"), 1)

                def silu(k, i, p):
                    act.wait_ge(e_("gu_ps"), k + 1)
                    at_least(act, e_("h"), k - 1)
                    p = p % 2
                    a_.activation(sg[p][:, :], PS[2 + p][:, 0:ED], ACT.Silu).then_inc(e_("silu"), 1)

                def turn_h(k, i, p):
                    act.wait_ge(e_("hT_ps"), k + 1)
                    at_least(act, e_("y_ps"), k - 1)
                    p = p % 2
                    a_.copy(ehT[p][:, :], PS[4 + p][:, 0:128]).then_inc(e_("ehT"), 1)

                def out_rows(k, i, p):
                    act.wait_ge(e_("y"), k + 1)
                    act.dma_start(ys[bass.ds(128 * k, 128), :], ey[p][:, :]).then_inc(e_(f"out{p}"), 16)

                skewed(act, [(turn, 0), (silu, 1), (turn_h, 2), (out_rows, 4)], TILES)

                later_units(act, shared)

        @block.tensor
        def _(pe):
            mm, tr = nc.tensor.matmul, nc.tensor.transpose

            pe.wait_ge(w_("weights"), 16 * W_LOADS)

            def context():
                pe.wait_ge(w_("later"), 16 * W_LATER)
                for i in range(B * M // 128):
                    last = tr(PS[2 + i // 4][0:EC, (i % 4) * 128:(i % 4) * 128 + 128], ctx_rows[:, i, :], ident[:, :])
                last.then_inc(w_("ctxT_ps"), 1)
                mm(MISC[:, 0:E], cols[:, 2:3].to_broadcast([128, 128]), wo[:, :], start=True, stop=True)
                for i in range(2):
                    last = mm(MISC[:, E + i:E + i + 1], cw1[:, i * 128:(i + 1) * 128], cols[:, 5:6], start=True, stop=True)
                last.then_inc(w_("bias_ps"), 1)
                pe.wait_ge(w_("ordered"), 5)
                pe.wait_ge(w_("ctxT"), 2)
                for i in range(2):
                    mm(PS[4 + i][:, :], cwk[:, :], ctxT[:, 512 * i:512 * i + 512], start=True, stop=True).then_inc(w_("ck_ps"), 1)
                for i in range(4):
                    if CV_BANKS[i] == 7:
                        pe.wait_ge(w_("bo_"), 2)
                    for j in range(4):
                        bb = 4 * i + j
                        for a in range(2):
                            last = mm(PS[CV_BANKS[i]][64 * a:64 * a + 64, j * 128:(j + 1) * 128], ctxT[:, bb * M:(bb + 1) * M], cwv[:, :],
                                      start=True, stop=True)
                    last.then_inc(w_("cv_ps"), 1)
                pe.wait_ge(w_("ck32"), 4)
                pe.wait_ge(w_("cv"), 6)
                tr(PS[4][:, 0:NE], rw_rows[:, :], ident[0:NE, 0:NE])
                for i in range(6):
                    last = tr(PS[5 + i // 3][:, (i % 3) * 128:(i % 3) * 128 + 128], sh_rows[:, i, :], ident[:, :])
                last.then_inc(w_("turned_ps"), 1)
                pe.wait_ge(w_("turned"), 3)
                pe.wait_ge(w_("cv"), 8)
                pe.wait_ge(w_("laid_out"), 2 + 2 * NB)
                pe.wait_ge(w_("bo_"), 2)

            def columns(s, b, free):
                pe.wait_ge(s("norm"), 2 * b + 2)
                at_least(pe, s("qk32"), free * b)
                for u in range(2):
                    last = tr(A0[:, u * 128:(u + 1) * 128], xn[:, u, :], ident[:, :])
                last.then_inc(s("xT_ps"), 1)

            def self_project(b, p):
                pe.wait_ge(s_("xnT"), b + 1)
                for i, w in enumerate((wq, wk)):
                    mm(A0[:, i * S:(i + 1) * S], w[:, :], xnT[:, :], start=True, stop=True).then_inc(s_("qk_ps"), 1)

            def self_values(b):
                at_least(pe, s_("vtok"), b)
                at_least(pe, s_("vg"), b)
                for n in range(NB):
                    for a in range(2):
                        last = mm(A1[64 * a:64 * a + 64, n * E:(n + 1) * E], xnT[:, n * BLOCK:(n + 1) * BLOCK], wv[:, :], start=True, stop=True)
                last.then_inc(s_("vdup_ps"), 1)

            def self_project2(b, p):
                pe.wait_ge(s_("vbd"), 2 * b + 2)
                pe.wait_ge(s_("xg"), b + 1)
                for u in range(2):
                    mm(A1[:, u * E:(u + 1) * E], xnT[:, u * 128:(u + 1) * 128], wv[:, :], start=True, stop=True)
                mm(A1[:, 2 * E:3 * E], xg[:, :, :].rearrange("p h g -> p (h g)"), wv[:, :],
                   start=True, stop=True).then_inc(s_("vtok_ps"), 1)

            def turn_shift(s, b):
                pe.wait_ge(s("mpart"), 2 * b + 2)
                for u in range(2):
                    last = tr(P1[1][:, :].bitcast(BF16)[SHIFT:128, u * 128:(u + 1) * 128],
                              mparts[:, u, :, :].rearrange("p i h -> p (i h)"), identb[:, :])
                last.then_inc(s("mT_ps"), 1)

            def weigh(s, b, p, i, values, blocks):
                pe.wait_ge(s("probs"), 4 * b + i + 1)
                for jj in range(2):
                    j = 2 * i + jj
                    for n in range(blocks):
                        w = S // blocks
                        mm(OD[32 * i:32 * i + 32, n * w:(n + 1) * w], values(n, j), probs[:, j, n * w:(n + 1) * w],
                           start=(jj == 0 and n == 0), stop=False, skip_group_check=True)
                    last = mm(OD[32 * i:32 * i + 32, S:2 * S], key_ones[:, jj, :], probs[:, j, :],
                              start=False, stop=False, skip_group_check=True)
                return last

            def self_out(b):
                pe.wait_ge(s_("att_all"), b + 1)
                for u in range(2):
                    last = mm(OD[:, u * E:(u + 1) * E], attT[:, u * 128:(u + 1) * 128], wo[:, :], start=True, stop=True)
                last.then_inc(s_("wo_ps"), 1)

            def cross_project(b, p):
                pe.wait_ge(c_("xnT"), b + 1)
                mm(A0[:, 0:S], cwq[:, :], xnT[:, :], start=True, stop=True).then_inc(c_("q_ps"), 1)

            def self_body(b, p, one, two):
                if one:
                    columns(s_, b + 1, 4)
                elif CROSS:
                    pe.wait_ge(s_("qk32"), 4 * B)
                    columns(c_, 0, 1)
                pe.wait_ge(s_("got"), GOT[True] * b + GOT[True])
                for u in range(2):
                    for half in range(2):
                        if u == 0:
                            at_least(pe, s_("mT") if half else s_("nmax"), (3 * b if half else 4 * b))
                        else:
                            pe.wait_ge(s_("nmax"), 4 * b + half + 1)
                        for j in range(4):
                            for i in range(2):
                                n = 2 * u + i
                                last = mm(P1[half][64 * i:64 * i + 64, j * 128:(j + 1) * 128],
                                          qs[p][0:KROWS, 4 * half + j, n * BLOCK:(n + 1) * BLOCK],
                                          kbd[p][0:KROWS, 4 * half + j, n, :, :].rearrange("r a k -> r (a k)"), start=True, stop=True)
                        last.then_inc(s_("scores"), 1)
                    if u == 0 and one:
                        self_project(b + 1, 1 - p)
                    elif u == 0 and CROSS:
                        cross_project(0, 0)
                pe.wait_ge(s_("kgqg"), 2 * b + 2)
                at_least(pe, s_("probs"), 4 * b)
                for u in range(2):
                    last = mm(P2[1][:, u * 128:(u + 1) * 128], qkz[p][:, u * 128:(u + 1) * 128],
                              kg[p][:, :, :].rearrange("p h g -> p (h g)"), start=True, stop=True)
                last.then_inc(s_("scores_g"), 1)
                at_least(pe, s_("gtmp"), b)
                mm(MISC[:, 0:S], qg[p][:, :, :].rearrange("p h g -> p (h g)"), k32[p][:, :], start=True, stop=True).then_inc(s_("gq_ps"), 1)
                turn_shift(s_, b)
                if not isinstance(b, int) or b > 0:
                    self_out(b - 1)
                if one:
                    self_values(b + 1)

                def pair(i):
                    pe.wait_ge(s_("mT"), 3 * b + (2 if i < 2 else 3))
                    for jj in range(2):
                        j = 2 * i + jj
                        for n in range(NB):
                            last = mm(P2[i % 2][:, jj * S + n * BLOCK:jj * S + (n + 1) * BLOCK],
                                      kbd[p][:, j, n, :, :].rearrange("r a k -> r (a k)"), qs[p][:, j, n * BLOCK:(n + 1) * BLOCK],
                                      start=True, stop=True)
                    last.then_inc(s_("pair"), 1)

                values = lambda n, j: vbd[p][:, n, j, :]
                at_least(pe, s_("gexp"), b)
                pair(0)
                pair(1)
                pe.wait_ge(s_("probs"), 4 * b + 1)
                pair(2)
                at_least(pe, s_("x_new"), b)
                weigh(s_, b, p, 0, values, NB)
                pe.wait_ge(s_("probs"), 4 * b + 2)
                pair(3)
                weigh(s_, b, p, 1, values, NB)
                pe.wait_ge(s_("probs"), 4 * b + 3)
                mm(P2[0][:, 0:S], kg[p][:, :, :].rearrange("p h g -> p (h g)"), qkz[p][:, 0:S], start=True, stop=False)
                mm(P2[0][:, 0:S], shift_glob[SHIFT:128, :], qs[p][SHIFT:128, 0, :], start=False, stop=True).then_inc(s_("gk_ps"), 1)
                weigh(s_, b, p, 2, values, NB)
                weigh(s_, b, p, 3, values, NB)
                if one:
                    self_project2(b + 1, 1 - p)
                pe.wait_ge(s_("gmasked"), b + 1)
                mm(OD[:, 0:S], vg[p][:, :], probs_g[:, :], start=False, stop=True, skip_group_check=True)
                mm(OD[:, S:2 * S], same_head[:, :], probs_g[:, :], start=False, stop=True, skip_group_check=True).then_inc(s_("od"), 1)
                pe.wait_ge(s_("gq_norm"), b + 1)
                for u in range(2):
                    last = tr(MISC[:, u * 128:(u + 1) * 128], pgq[:, u * 128:(u + 1) * 128], ident[:, :])
                last.then_inc(s_("gq_T"), 1)
                pe.wait_ge(s_("pgqT"), b + 1)
                for u in range(2):
                    last = mm(MISC[:, 0:128], vtok[p][:, u, :], pgqT[:, u, :], start=(u == 0), stop=(u == 1))
                last.then_inc(s_("gq_o"), 1)

            columns(s_, 0, 4)
            pe.wait_ge(w_("ordered"), 3)
            self_project(0, 0)
            self_values(0)
            self_project2(0, 0)
            context()
            loop(pe, self_body)
            self_out(B - 1)

            if "B" in phases:
                def cross_hidden(b):
                    pe.wait_ge(c_("attT"), b + 1)
                    for i in range(2):
                        last = mm(MISC[:, i * S:(i + 1) * S], cw1[:, i * 128:(i + 1) * 128], attT[:, :], start=True, stop=True)
                    last.then_inc(c_("h_ps"), 1)

                def cross_out(b):
                    pe.wait_ge(c_("h"), 2 * b + 2)
                    for u in range(2):
                        for i in range(2):
                            last = mm(OD[:, u * E:(u + 1) * E], hT[:, i, u * 128:(u + 1) * 128], cw2[:, i, :], start=(i == 0), stop=(i == 1))
                    last.then_inc(c_("y_ps"), 1)

                def route_turn(b, p):
                    pe.wait_ge(r_("norm"), 2 * b + 2)
                    at_least(pe, r_("xnT"), 2 * b)
                    for u in range(2):
                        last = tr(A1[:, u * 128:(u + 1) * 128], xn3[p][:, u, :], ident[:, :])
                    last.then_inc(r_("xT_ps"), 1)

                def route_logits(b):
                    pe.wait_ge(r_("xnT"), 2 * b + 2)
                    for u in range(2):
                        last = mm(MISC[:, u * NE:(u + 1) * NE], x3s[:, u * 128:(u + 1) * 128], rwT[:, :], start=True, stop=True)
                    last.then_inc(r_("logit_ps"), 1)

                def route_count(b):
                    pe.wait_ge(r_("both"), b + 1)
                    mm(MISC[:, 0:NE], aheadb[:, 0:128], both[:, 0, :], start=True, stop=True)
                    mm(MISC[:, NE:2 * NE], aheadb[:, 0:128], both[:, 1, :], start=True, stop=False)
                    mm(MISC[:, NE:2 * NE], aheadb[:, 128:256], both[:, 0, :], start=False, stop=True)
                    mm(MISC[:, 2 * NE:3 * NE], aheadb[:, 128:256], both[:, 0, :], start=True, stop=False)
                    mm(MISC[:, 2 * NE:3 * NE], aheadb[:, 128:256], both[:, 1, :], start=False, stop=True).then_inc(r_("count_ps"), 1)

                def cross_body(b, p, one, two):
                    if one:
                        columns(c_, b + 1, 1)
                    pe.wait_ge(c_("got"), GOT[False] * b + GOT[False])
                    for u in range(2):
                        for half in range(2):
                            if u == 0:
                                at_least(pe, c_("mT") if half else c_("nmax"), (3 * b if half else 4 * b))
                            else:
                                pe.wait_ge(c_("nmax"), 4 * b + half + 1)
                            for j in range(4):
                                last = mm(P1[half][:, j * 128:(j + 1) * 128], qs[p][0:KROWS, 4 * half + j, u * 128:(u + 1) * 128],
                                          ckbd[p][0:KROWS, 4 * half + j, :, :].rearrange("r a k -> r (a k)"), start=True, stop=True)
                            last.then_inc(c_("scores"), 1)
                        if u == 0 and one:
                            cross_project(b + 1, 1 - p)
                        if u == 0 and (not isinstance(b, int) or b > 0):
                            if routed(b - 3):
                                pe.wait_ge(r_("counts"), b - 2)
                            cross_hidden(b - 1)
                    if not isinstance(b, int) or b > 0:
                        cross_out(b - 1)
                    turn_shift(c_, b)
                    if routed(b - 2):
                        route_logits(b - 2)

                    def pair(i):
                        pe.wait_ge(c_("mT"), 3 * b + (2 if i < 2 else 3))
                        for jj in range(2):
                            j = 2 * i + jj
                            last = mm(P2[i % 2][:, jj * S:(jj + 1) * S], ckbd[p][:, j, :, :].rearrange("p a k -> p (a k)"), qs[p][:, j, :],
                                      start=True, stop=True)
                        last.then_inc(c_("pair"), 1)

                    values = lambda n, j: cvbd[p][:, j, :]
                    at_least(pe, c_("probs"), 4 * b)
                    pair(0)
                    pair(1)
                    pe.wait_ge(c_("probs"), 4 * b + 1)
                    pair(2)
                    at_least(pe, c_("x_new"), b)
                    weigh(c_, b, p, 0, values, 1)
                    pe.wait_ge(c_("probs"), 4 * b + 2)
                    pair(3)
                    for i in range(1, 4):
                        last = weigh(c_, b, p, i, values, 1)
                    last.then_inc(c_("od"), 1)
                    if routed(b - 2):
                        route_count(b - 2)
                    if routed(b - 1):
                        route_turn(b - 1, 1 - p)

                pe.wait_ge(w_("set"), 4)
                pe.wait_ge(s_("x_new"), B)
                loop(pe, cross_body, 4)
                if routed(B - 3):
                    pe.wait_ge(r_("counts"), B - 2)
                cross_hidden(B - 1)
                cross_out(B - 1)
                for b in (B - 2, B - 1):
                    if routed(b):
                        if b == B - 1:
                            route_turn(b, 1)
                        at_least(pe, r_("counts"), b)
                        route_logits(b)
                        route_count(b)

            if "C" in phases:
                def shared_in(u, i, p, c):
                    at_least(pe, h_("h"), 2 * (u - 1) + c + 1 if not isinstance(u, int) or u > 0 else 0)
                    for k in range(2):
                        last = mm(PS[2 * c + k][:, :], shT[:, 2 * k + c, :], x3T[:, bass.ds(512 * u, 512)], start=True, stop=True)
                    last.then_inc(h_("gu_ps"), 1)

                def shared_out(u, i, p):
                    pe.wait_ge(h_("h"), 2 * u + 2)
                    at_least(pe, h_("x"), u - 1)
                    for j in range(4):
                        for c in range(2):
                            last = mm(PS[4 + p][:, j * E:(j + 1) * E], shs[:, c, j * 128:(j + 1) * 128], shT[:, 4 + c, :], start=(c == 0), stop=(c == 1))
                    last.then_inc(h_("y_ps"), 1)

                def shared(u, i, p):
                    shared_in(u, i, p, 0)
                    shared_in(u, i, p, 1)
                    shared_out(u, i, p)

                pe.wait_ge(r_("xnT"), 2 * B)
                pe.wait_ge(c_("x_new"), B)
                pe.wait_ge(r_("counts"), B)
                shared(0, 0, 0)
                pe.wait_ge(e_("tile_of"), 1)
                for i in range(2):
                    last = tr(MISC[0:1, i * 128:(i + 1) * 128], tile_of[:, 2 + i:3 + i], ident[:, :])
                last.then_inc(e_("map_ps"), 1)
                shared(1, 0, 1)
                pe.wait_ge(h_("x"), EARLY)
                pe.wait_ge(e_("tile_row"), 1)
                pe.wait_ge(w_("experts"), 32)

                loaded = []

                def load_experts(i):
                    loaded[:] = numbers(pe, tile_row[0:1, 1, bass.ds(4 * i - 3, 6)], NE - 1)

                def expert_of(k, place):
                    if isinstance(k, int):
                        return pe.value_load(tile_row[0:1, 1, bass.ds(k, 1)], min_val=0, max_val=NE - 1)
                    return loaded[place]

                def turn(k, i, p):
                    pe.wait_ge(e_(f"in{p}"), 16 * (i + 1))
                    at_least(pe, e_("xtT"), k - 1)
                    tr(PS[p % 2][:, 0:128], xt[p][:, :], ident[:, :]).then_inc(e_("xT_ps"), 1)

                def gate_up(k, i, p):
                    which = expert_of(k, (p + 1) % 4 + 2)
                    p = p % 2
                    pe.wait_ge(e_("xtT"), k + 1)
                    at_least(pe, e_("h"), k - 1)
                    mm(PS[2 + p][:, 0:2 * ED], xtT[p][:, :], wgu[:, bass.ds(which, 1), :].squeeze(1), start=True, stop=True).then_inc(e_("gu_ps"), 1)

                def turn_h(k, i, p):
                    p = p % 2
                    pe.wait_ge(e_("h"), k + 1)
                    at_least(pe, e_("ehT"), k - 1)
                    tr(PS[4 + p][:, 0:128], eh[p][:, :], ident[:, :]).then_inc(e_("hT_ps"), 1)

                def down(k, i, p):
                    which = expert_of(k, (p + 3) % 4)
                    p = p % 2
                    pe.wait_ge(e_("ehT"), k + 1)
                    at_least(pe, e_("y"), k - 1)
                    mm(PS[6 + p][:, 0:E], ehT[p][:, :], wd[:, bass.ds(which, 1), :].squeeze(1), start=True, stop=True).then_inc(e_("y_ps"), 1)

                skewed(pe, [(turn, 0), (gate_up, 1), (turn_h, 2), (down, 3)], TILES, load_experts)
                pe.wait_ge(e_("y"), TILES)

                later_units(pe, shared)


W_LOADS, W_LATER = 6, 18


def value_cells(eng, dst, bank, sem):
    for a in range(2):
        src = bank[64 * a:64 * a + 64, :].rearrange("p (ng jj a d) -> p ng jj a d", jj=2, a=2, d=D)[:, :, :, a, :]
        full = dst[64 * a:64 * a + 64].rearrange("p n (g jj) c -> p (n g) (jj c)", jj=2)
        for jj in range(2):
            cell = jj * 48 + a * D
            last = eng.copy(full[:, :, cell:cell + D], src[:, :, jj, :])
        last.then_inc(sem, 1)


_INS = ["x", "ctx_768", "L0_attn_Wq", "L0_attn_bq", "L0_attn_Wk", "L0_attn_bk", "L0_attn_Wv", "L0_attn_bv",
        "L0_attn_Wo", "L0_attn_bo", "L0_xattn_Wq", "L0_xattn_bq", "L0_xattn_Wk", "L0_xattn_bk", "L0_xattn_Wv",
        "L0_xattn_bv", "L0_xattn_W1", "L0_xattn_b1", "L0_xattn_W2", "L0_xattn_b2", "L0_ffn_router_w",
        "L0_ffn_gate_up_w", "L0_ffn_down_w", "L0_ffn_shared_gate_w", "L0_ffn_shared_up_w", "L0_ffn_shared_down_w"]


def kernel(**inputs):
    import numpy as _np
    import concourse.bacc as _bacc
    from concourse.bass_utils import run_bass_kernel_spmd as _run

    nc = _bacc.Bacc("TRN2", target_bir_lowering=False, num_devices=1)
    arrays, args = {}, {}
    given = {name: _np.ascontiguousarray(inputs[name]) for name in _INS}
    for name, a in {**given, **shape_constants()}.items():
        arrays[f"in_{name}"] = a
        args[name] = nc.dram_tensor(f"in_{name}", a.shape, mybir.dt.from_np(a.dtype), kind="ExternalInput").ap()
    out = nc.dram_tensor("out_0", (B, S, E), F32, kind="ExternalOutput").ap()
    decoder(nc, args, out)
    r = _run(nc, [arrays], core_ids=[0])
    return r.results[0]["out_0"]
```
